# Optimizing a Trainium2 kernel written in Bass

```python
import numpy as np
import jax
import jax.numpy as jnp

def _softmax(x, axis=-1):
    return jax.nn.softmax(x, axis=axis)

def _gelu(x):
    return jax.nn.gelu(x, approximate=True)

def _silu(x):
    return jax.nn.silu(x)

def _sigmoid(x):
    return jax.nn.sigmoid(x)

def _layernorm(x, axis=-1, eps=1e-05):
    m = jnp.mean(x, axis=axis, keepdims=True)
    v = jnp.var(x, axis=axis, keepdims=True)
    return (x - m) / jnp.sqrt(v + eps)

def _scatter_add(tgt, idx, src, axis=0):
    return tgt.at[idx].add(src)

def _segment_sum(src, seg, n):
    return jax.ops.segment_sum(src, seg, n)
kernel_name = 'mk_gnn_preln_d4_gnn_r8_720ca1'

def setup_inputs(seed: int=0):
    np.random.seed(seed)
    _w = jnp.asarray

    def _rec_inputs():
        import jax
        import jax.numpy as jnp
        _gk = jax.random.key(seed)
        x = -0.0003713 + 1 * jax.random.normal(jax.random.fold_in(_gk, 1), (12500, 128), jnp.float32)
        _s = jax.random.randint(jax.random.fold_in(_gk, 2), (100000,), 0, 12500, jnp.int32)
        _d = jax.random.randint(jax.random.fold_in(_gk, 3), (100000,), 0, 12500, jnp.int32)
        _loop = jnp.arange(12500, dtype=jnp.int32)
        src = jnp.concatenate([_s, _d, _loop])
        dst = jnp.concatenate([_d, _s, _loop])
        _o = jnp.argsort(dst, stable=True)
        src = src[_o]
        dst = dst[_o]
        edge_attr_4 = 0.000126197 + 0.999763 * jax.random.normal(jax.random.fold_in(_gk, 12), (212500, 4), jnp.float32)
        edge_attr_64 = 1.36993e-05 + 0.999972 * jax.random.normal(jax.random.fold_in(_gk, 13), (212500, 64), jnp.float32)
        edge_type_16 = jax.random.randint(jax.random.fold_in(_gk, 15), (212500,), 0, 16, jnp.int32)
        edge_weight = jax.random.uniform(jax.random.fold_in(_gk, 16), (212500,), jnp.float32, 0.0, 0.999998)
        node_type_8 = jax.random.randint(jax.random.fold_in(_gk, 17), (12500,), 0, 8, jnp.int32)
        return (x, src, dst, edge_attr_4, edge_attr_64, edge_type_16, edge_weight, node_type_8)
    x, src, dst, edge_attr_4, edge_attr_64, edge_type_16, edge_weight, node_type_8 = _rec_inputs()

    def _L0_gnn_setup():
        import jax, jax.numpy as jnp
        import numpy as np
        N_NODES = 12500
        N_EDGES = 200000
        D_MODEL = 128
        N_HEADS = 8
        D_HEAD = D_MODEL // N_HEADS

        def _batch_norm(x, w, b, eps=1e-05):
            m = x.mean(axis=0)
            v = x.var(axis=0)
            return (x - m) * jax.lax.rsqrt(v + eps) * w + b
        key = jax.random.key(seed)
        ks = jax.random.split(key, 12)
        s = 0.05
        inp = {'h': jax.random.normal(ks[0], (N_NODES, D_MODEL), dtype=jnp.float32), 'src': jax.random.randint(ks[1], (N_EDGES,), 0, N_NODES, dtype=jnp.int32), 'dst': jax.random.randint(ks[2], (N_EDGES,), 0, N_NODES, dtype=jnp.int32), 'Wq': jax.random.normal(ks[3], (D_MODEL, D_MODEL), dtype=jnp.float32) * s, 'Wk': jax.random.normal(ks[4], (D_MODEL, D_MODEL), dtype=jnp.float32) * s, 'Wv': jax.random.normal(ks[5], (D_MODEL, D_MODEL), dtype=jnp.float32) * s, 'Wo': jax.random.normal(ks[6], (D_MODEL, D_MODEL), dtype=jnp.float32) * s, 'bo': jnp.zeros((D_MODEL,), dtype=jnp.float32), 'W1': jax.random.normal(ks[7], (2 * D_MODEL, D_MODEL), dtype=jnp.float32) * s, 'b1': jnp.zeros((2 * D_MODEL,), dtype=jnp.float32), 'W2': jax.random.normal(ks[8], (D_MODEL, 2 * D_MODEL), dtype=jnp.float32) * s, 'b2': jnp.zeros((D_MODEL,), dtype=jnp.float32), 'bn1_w': jnp.ones((D_MODEL,), dtype=jnp.float32), 'bn1_b': jnp.zeros((D_MODEL,), dtype=jnp.float32), 'bn2_w': jnp.ones((D_MODEL,), dtype=jnp.float32), 'bn2_b': jnp.zeros((D_MODEL,), dtype=jnp.float32)}
        return inp
    _L0_gnn_all = _L0_gnn_setup()
    _L0_gnn_in = {k: v for k, v in _L0_gnn_all.items() if k in ('Wq', 'Wk', 'Wv', 'Wo', 'bo', 'W1', 'b1', 'W2', 'b2', 'bn1_w', 'bn1_b', 'bn2_w', 'bn2_b')}
    del _L0_gnn_all

    def _L1_gnn_setup():
        import jax, jax.numpy as jnp
        import numpy as np
        N_NODES = 6250
        N_EDGES = 80000
        D = 128
        N_RELS = 16
        N_NTYPES = 8
        key = jax.random.key(seed)
        ks = jax.random.split(key, 9)
        return {'feats': jax.random.normal(ks[0], (N_NODES, D), dtype=jnp.float32), 'W_edge': jax.random.normal(ks[1], (N_RELS, D, D), dtype=jnp.float32) / np.sqrt(D), 'b_edge': jax.random.normal(ks[2], (N_RELS, D), dtype=jnp.float32) * 0.02, 'W_node': jax.random.normal(ks[3], (N_NTYPES, D, D), dtype=jnp.float32) / np.sqrt(D), 'b_node': jax.random.normal(ks[4], (N_NTYPES, D), dtype=jnp.float32) * 0.02, 'src': jax.random.randint(ks[5], (N_EDGES,), 0, N_NODES, dtype=jnp.int32), 'dst': jax.random.randint(ks[6], (N_EDGES,), 0, N_NODES, dtype=jnp.int32), 'ntypes': jax.random.randint(ks[7], (N_NODES,), 0, N_NTYPES, dtype=jnp.int32), 'etypes': jax.random.randint(ks[8], (N_EDGES,), 0, N_RELS, dtype=jnp.int32)}
    _L1_gnn_all = _L1_gnn_setup()
    _L1_gnn_in = {k: v for k, v in _L1_gnn_all.items() if k in ('W_edge', 'b_edge', 'W_node', 'b_node')}
    del _L1_gnn_all

    def _L2_gnn_setup():
        import jax, jax.numpy as jnp
        import numpy as np
        N = 12500
        E = 75000
        D = 128
        key = jax.random.key(seed)
        k1, k2, k3, k4, k5 = jax.random.split(key, 5)
        x = jax.random.normal(k1, (N, D), dtype=jnp.float32)
        edge_index = jax.random.randint(k2, (2, E), 0, N, dtype=jnp.int64)
        dist_weight = jax.random.uniform(k3, (E,), dtype=jnp.float32)
        bound = float(np.sqrt(6.0 / (D + D)))
        W0 = jax.random.uniform(k4, (D, D), dtype=jnp.float32, minval=-bound, maxval=bound)
        W1 = jax.random.uniform(k5, (D, D), dtype=jnp.float32, minval=-bound, maxval=bound)
        return {'x': x, 'edge_index': edge_index, 'dist_weight': dist_weight, 'W0': W0, 'W1': W1}
    _L2_gnn_all = _L2_gnn_setup()
    _L2_gnn_in = {k: v for k, v in _L2_gnn_all.items() if k in ('W0', 'W1')}
    del _L2_gnn_all

    def _L3_gnn_setup():
        import jax, jax.numpy as jnp
        import numpy as np
        N, E = (1250, 40000)
        D = 128
        R, EF = (64, 4)
        NH = 16
        EPS = 1e-05

        def _ln(x, g, b):
            mu = x.mean(-1, keepdims=True)
            var = ((x - mu) ** 2).mean(-1, keepdims=True)
            return (x - mu) * jax.lax.rsqrt(var + EPS) * g + b

        def _mlp(x, w1, b1, g, beta, w2, b2):
            hdn = jax.nn.relu(_ln(x @ w1 + b1, g, beta))
            return hdn @ w2 + b2
        key = jax.random.key(seed)
        ks = jax.random.split(key, 12)

        def p(k, shape):
            return jax.random.normal(k, shape, jnp.float32) / np.sqrt(shape[0])
        kv_in = 2 * D + EF + R
        inp = {'h': jax.random.normal(ks[0], (N, D), jnp.float32), 'r_feat': jax.random.normal(ks[1], (E, R), jnp.float32), 'edge_feat': jax.random.normal(ks[2], (E, EF), jnp.float32), 'edge_index': jax.random.randint(ks[3], (2, E), 0, N), 'hk_w1': p(ks[4], (kv_in, D)), 'hk_b1': jnp.zeros(D), 'hk_g': jnp.ones(D), 'hk_beta': jnp.zeros(D), 'hk_w2': p(ks[5], (D, D)), 'hk_b2': jnp.zeros(D), 'hv_w1': p(ks[6], (kv_in, D)), 'hv_b1': jnp.zeros(D), 'hv_g': jnp.ones(D), 'hv_beta': jnp.zeros(D), 'hv_w2': p(ks[7], (D, D)), 'hv_b2': jnp.zeros(D), 'hq_w1': p(ks[8], (D, D)), 'hq_b1': jnp.zeros(D), 'hq_g': jnp.ones(D), 'hq_beta': jnp.zeros(D), 'hq_w2': p(ks[9], (D, D)), 'hq_b2': jnp.zeros(D), 'ew_w': p(ks[10], (R, 1)), 'ew_b': jnp.zeros(1), 'no_w1': p(ks[11], (2 * D, D)), 'no_b1': jnp.zeros(D), 'no_g': jnp.ones(D), 'no_beta': jnp.zeros(D), 'no_w2': p(jax.random.fold_in(key, 99), (D, D)), 'no_b2': jnp.zeros(D)}
        return inp
    _L3_gnn_all = _L3_gnn_setup()
    _L3_gnn_in = {k: v for k, v in _L3_gnn_all.items() if k in ('hk_w1', 'hk_b1', 'hk_g', 'hk_beta', 'hk_w2', 'hk_b2', 'hv_w1', 'hv_b1', 'hv_g', 'hv_beta', 'hv_w2', 'hv_b2', 'hq_w1', 'hq_b1', 'hq_g', 'hq_beta', 'hq_w2', 'hq_b2', 'ew_w', 'ew_b', 'no_w1', 'no_b1', 'no_g', 'no_beta', 'no_w2', 'no_b2')}
    del _L3_gnn_all
    return {'x': x, 'src': src, 'dst': dst, 'edge_attr_4': edge_attr_4, 'edge_attr_64': edge_attr_64, 'edge_type_16': edge_type_16, 'edge_weight': edge_weight, 'node_type_8': node_type_8, 'L0_gnn_Wq': _L0_gnn_in['Wq'], 'L0_gnn_Wk': _L0_gnn_in['Wk'], 'L0_gnn_Wv': _L0_gnn_in['Wv'], 'L0_gnn_Wo': _L0_gnn_in['Wo'], 'L0_gnn_bo': _L0_gnn_in['bo'], 'L0_gnn_W1': _L0_gnn_in['W1'], 'L0_gnn_b1': _L0_gnn_in['b1'], 'L0_gnn_W2': _L0_gnn_in['W2'], 'L0_gnn_b2': _L0_gnn_in['b2'], 'L0_gnn_bn1_w': _L0_gnn_in['bn1_w'], 'L0_gnn_bn1_b': _L0_gnn_in['bn1_b'], 'L0_gnn_bn2_w': _L0_gnn_in['bn2_w'], 'L0_gnn_bn2_b': _L0_gnn_in['bn2_b'], 'L1_gnn_W_edge': _L1_gnn_in['W_edge'], 'L1_gnn_b_edge': _L1_gnn_in['b_edge'], 'L1_gnn_W_node': _L1_gnn_in['W_node'], 'L1_gnn_b_node': _L1_gnn_in['b_node'], 'L2_gnn_W0': _L2_gnn_in['W0'], 'L2_gnn_W1': _L2_gnn_in['W1'], 'L3_gnn_hk_w1': _L3_gnn_in['hk_w1'], 'L3_gnn_hk_b1': _L3_gnn_in['hk_b1'], 'L3_gnn_hk_g': _L3_gnn_in['hk_g'], 'L3_gnn_hk_beta': _L3_gnn_in['hk_beta'], 'L3_gnn_hk_w2': _L3_gnn_in['hk_w2'], 'L3_gnn_hk_b2': _L3_gnn_in['hk_b2'], 'L3_gnn_hv_w1': _L3_gnn_in['hv_w1'], 'L3_gnn_hv_b1': _L3_gnn_in['hv_b1'], 'L3_gnn_hv_g': _L3_gnn_in['hv_g'], 'L3_gnn_hv_beta': _L3_gnn_in['hv_beta'], 'L3_gnn_hv_w2': _L3_gnn_in['hv_w2'], 'L3_gnn_hv_b2': _L3_gnn_in['hv_b2'], 'L3_gnn_hq_w1': _L3_gnn_in['hq_w1'], 'L3_gnn_hq_b1': _L3_gnn_in['hq_b1'], 'L3_gnn_hq_g': _L3_gnn_in['hq_g'], 'L3_gnn_hq_beta': _L3_gnn_in['hq_beta'], 'L3_gnn_hq_w2': _L3_gnn_in['hq_w2'], 'L3_gnn_hq_b2': _L3_gnn_in['hq_b2'], 'L3_gnn_ew_w': _L3_gnn_in['ew_w'], 'L3_gnn_ew_b': _L3_gnn_in['ew_b'], 'L3_gnn_no_w1': _L3_gnn_in['no_w1'], 'L3_gnn_no_b1': _L3_gnn_in['no_b1'], 'L3_gnn_no_g': _L3_gnn_in['no_g'], 'L3_gnn_no_beta': _L3_gnn_in['no_beta'], 'L3_gnn_no_w2': _L3_gnn_in['no_w2'], 'L3_gnn_no_b2': _L3_gnn_in['no_b2']}

def reference(x, src, dst, edge_attr_4, edge_attr_64, edge_type_16, edge_weight, node_type_8, L0_gnn_Wq, L0_gnn_Wk, L0_gnn_Wv, L0_gnn_Wo, L0_gnn_bo, L0_gnn_W1, L0_gnn_b1, L0_gnn_W2, L0_gnn_b2, L0_gnn_bn1_w, L0_gnn_bn1_b, L0_gnn_bn2_w, L0_gnn_bn2_b, L1_gnn_W_edge, L1_gnn_b_edge, L1_gnn_W_node, L1_gnn_b_node, L2_gnn_W0, L2_gnn_W1, L3_gnn_hk_w1, L3_gnn_hk_b1, L3_gnn_hk_g, L3_gnn_hk_beta, L3_gnn_hk_w2, L3_gnn_hk_b2, L3_gnn_hv_w1, L3_gnn_hv_b1, L3_gnn_hv_g, L3_gnn_hv_beta, L3_gnn_hv_w2, L3_gnn_hv_b2, L3_gnn_hq_w1, L3_gnn_hq_b1, L3_gnn_hq_g, L3_gnn_hq_beta, L3_gnn_hq_w2, L3_gnn_hq_b2, L3_gnn_ew_w, L3_gnn_ew_b, L3_gnn_no_w1, L3_gnn_no_b1, L3_gnn_no_g, L3_gnn_no_beta, L3_gnn_no_w2, L3_gnn_no_b2):
    import jax
    import jax.numpy as jnp

    def _L0_gnn_ref(h, src, dst, Wq, Wk, Wv, Wo, bo, W1, b1, W2, b2, bn1_w, bn1_b, bn2_w, bn2_b):
        import jax, jax.numpy as jnp
        import numpy as np
        N_NODES = 12500
        N_EDGES = 200000
        D_MODEL = 128
        N_HEADS = 8
        D_HEAD = D_MODEL // N_HEADS

        def _batch_norm(x, w, b, eps=1e-05):
            m = x.mean(axis=0)
            v = x.var(axis=0)
            return (x - m) * jax.lax.rsqrt(v + eps) * w + b
        N = h.shape[0]
        Q = (h @ Wq.T).reshape(N, N_HEADS, D_HEAD)
        K = (h @ Wk.T).reshape(N, N_HEADS, D_HEAD)
        V = (h @ Wv.T).reshape(N, N_HEADS, D_HEAD)
        score = jnp.einsum('ehd,ehd->eh', K[src], Q[dst]) / np.sqrt(D_HEAD).astype(np.float32)
        s = jnp.exp(jnp.clip(score, -5.0, 5.0))[:, :, None]
        wV = jax.ops.segment_sum(V[src] * s, dst, num_segments=N)
        z = jax.ops.segment_sum(s, dst, num_segments=N)
        h_attn = (wV / (z + 1e-06)).reshape(N, D_MODEL)
        x = h_attn @ Wo.T + bo
        x = h + x
        x = _batch_norm(x, bn1_w, bn1_b)
        y = jax.nn.relu(x @ W1.T + b1) @ W2.T + b2
        y = x + y
        y = _batch_norm(y, bn2_w, bn2_b)
        return y

    def _L1_gnn_ref(feats, W_edge, b_edge, W_node, b_node, src, dst, ntypes, etypes):
        import jax, jax.numpy as jnp
        import numpy as np
        N_NODES = 6250
        N_EDGES = 80000
        D = 128
        N_RELS = 16
        N_NTYPES = 8
        N, d = feats.shape
        T = W_edge.shape[0]
        hW = jnp.einsum('nd,tdf->tnf', feats, W_edge) + b_edge[:, None, :]
        msg = hW[etypes, src]
        seg = dst * T + etypes
        counts = jax.ops.segment_sum(jnp.ones(msg.shape[0], dtype=msg.dtype), seg, num_segments=N * T)
        msg = msg / counts[seg][:, None]
        agg = jax.ops.segment_sum(msg, dst, num_segments=N)
        hN = jnp.einsum('nd,tdf->tnf', feats, W_node) + b_node[:, None, :]
        out = hN[ntypes, jnp.arange(N)] + agg
        return jax.nn.relu(out)

    def _L2_gnn_ref(x, edge_index, dist_weight, W0, W1):
        import jax, jax.numpy as jnp
        import numpy as np
        N = 12500
        E = 75000
        D = 128
        row, col = (edge_index[0], edge_index[1])
        n = x.shape[0]
        deg = jax.ops.segment_sum(jnp.ones_like(dist_weight), col, num_segments=n)
        deg_inv_sqrt = jnp.where(deg > 0, jax.lax.rsqrt(deg), 0.0)
        norm = deg_inv_sqrt[row] * deg_inv_sqrt[col]
        w = dist_weight * norm
        side_embed = jax.ops.segment_sum(w[:, None] * x[col], row, num_segments=n)
        bi_embed = x * side_embed
        return side_embed @ W0.T + bi_embed @ W1.T

    def _L3_gnn_ref(h, r_feat, edge_feat, edge_index, hk_w1, hk_b1, hk_g, hk_beta, hk_w2, hk_b2, hv_w1, hv_b1, hv_g, hv_beta, hv_w2, hv_b2, hq_w1, hq_b1, hq_g, hq_beta, hq_w2, hq_b2, ew_w, ew_b, no_w1, no_b1, no_g, no_beta, no_w2, no_b2):
        import jax, jax.numpy as jnp
        import numpy as np
        N, E = (1250, 40000)
        D = 128
        R, EF = (64, 4)
        NH = 16
        EPS = 1e-05

        def _ln(x, g, b):
            mu = x.mean(-1, keepdims=True)
            var = ((x - mu) ** 2).mean(-1, keepdims=True)
            return (x - mu) * jax.lax.rsqrt(var + EPS) * g + b

        def _mlp(x, w1, b1, g, beta, w2, b2):
            hdn = jax.nn.relu(_ln(x @ w1 + b1, g, beta))
            return hdn @ w2 + b2
        n = h.shape[0]
        src, dst = (edge_index[0], edge_index[1])
        dh = D // NH
        kv_input = jnp.concatenate([edge_feat, r_feat, h[dst], h[src]], -1)
        k = _mlp(kv_input, hk_w1, hk_b1, hk_g, hk_beta, hk_w2, hk_b2).reshape(-1, NH, dh)
        v = _mlp(kv_input, hv_w1, hv_b1, hv_g, hv_beta, hv_w2, hv_b2)
        e_w = jax.nn.sigmoid(r_feat @ ew_w + ew_b)
        v = (v * e_w).reshape(-1, NH, dh)
        q = _mlp(h, hq_w1, hq_b1, hq_g, hq_beta, hq_w2, hq_b2).reshape(-1, NH, dh)
        logits = (q[dst] * k).sum(-1) / np.sqrt(dh)
        seg_max = jax.ops.segment_max(logits, dst, num_segments=n)
        ex = jnp.exp(logits - seg_max[dst])
        denom = jax.ops.segment_sum(ex, dst, num_segments=n)
        alpha = ex / denom[dst]
        m = alpha[..., None] * v
        out = jax.ops.segment_sum(m, dst, num_segments=n).reshape(n, D)
        out = _mlp(jnp.concatenate([out, h], -1), no_w1, no_b1, no_g, no_beta, no_w2, no_b2)
        return out + h
    edge_index = jnp.stack([src, dst])
    h = jnp.maximum(_layernorm(x, axis=-1), 0.0)
    x = x + _L0_gnn_ref(h, src, dst, L0_gnn_Wq, L0_gnn_Wk, L0_gnn_Wv, L0_gnn_Wo, L0_gnn_bo, L0_gnn_W1, L0_gnn_b1, L0_gnn_W2, L0_gnn_b2, L0_gnn_bn1_w, L0_gnn_bn1_b, L0_gnn_bn2_w, L0_gnn_bn2_b)
    h = jnp.maximum(_layernorm(x, axis=-1), 0.0)
    x = x + _L1_gnn_ref(h, L1_gnn_W_edge, L1_gnn_b_edge, L1_gnn_W_node, L1_gnn_b_node, src, dst, node_type_8, edge_type_16)
    h = jnp.maximum(_layernorm(x, axis=-1), 0.0)
    x = x + _L2_gnn_ref(h, edge_index, edge_weight, L2_gnn_W0, L2_gnn_W1)
    h = jnp.maximum(_layernorm(x, axis=-1), 0.0)
    x = x + _L3_gnn_ref(h, edge_attr_64, edge_attr_4, edge_index, L3_gnn_hk_w1, L3_gnn_hk_b1, L3_gnn_hk_g, L3_gnn_hk_beta, L3_gnn_hk_w2, L3_gnn_hk_b2, L3_gnn_hv_w1, L3_gnn_hv_b1, L3_gnn_hv_g, L3_gnn_hv_beta, L3_gnn_hv_w2, L3_gnn_hv_b2, L3_gnn_hq_w1, L3_gnn_hq_b1, L3_gnn_hq_g, L3_gnn_hq_beta, L3_gnn_hq_w2, L3_gnn_hq_b2, L3_gnn_ew_w, L3_gnn_ew_b, L3_gnn_no_w1, L3_gnn_no_b1, L3_gnn_no_g, L3_gnn_no_beta, L3_gnn_no_w2, L3_gnn_no_b2)
    return x

_drawn_inputs = setup_inputs


def setup_inputs(seed=0):
    import zlib

    import numpy as np

    out = dict(_drawn_inputs(seed))
    spreads = {'L0_gnn_bo': (0.0, 2.0),
     'L0_gnn_b1': (0.0, 0.44),
     'L0_gnn_b2': (0.0, 2.0),
     'L0_gnn_bn1_w': (1.0, 0.2),
     'L0_gnn_bn1_b': (0.0, 0.8),
     'L0_gnn_bn2_w': (1.0, 0.2),
     'L0_gnn_bn2_b': (0.0, 0.1),
     'L3_gnn_hk_b1': (0.0, 2.0),
     'L3_gnn_hk_g': (1.0, 0.6),
     'L3_gnn_hk_beta': (0.0, 0.8),
     'L3_gnn_hk_b2': (0.0, 2.0),
     'L3_gnn_hv_b1': (0.0, 0.8),
     'L3_gnn_hv_g': (1.0, 0.6),
     'L3_gnn_hv_beta': (0.0, 0.8),
     'L3_gnn_hv_b2': (0.0, 0.707),
     'L3_gnn_hq_b1': (0.0, 0.8),
     'L3_gnn_hq_g': (1.0, 0.6),
     'L3_gnn_hq_beta': (0.0, 0.8),
     'L3_gnn_hq_b2': (0.0, 0.8),
     'L3_gnn_no_b1': (0.0, 0.275),
     'L3_gnn_no_g': (1.0, 0.2),
     'L3_gnn_no_beta': (0.0, 0.425),
     'L3_gnn_no_b2': (0.0, 0.302)}
    factors = {'edge_attr_4': 8.0,
     'edge_attr_64': 3.68,
     'L0_gnn_Wq': 8.0,
     'L0_gnn_Wk': 8.0,
     'L1_gnn_b_edge': 3.285,
     'L1_gnn_b_node': 8.0,
     'L3_gnn_hk_w1': 8.0,
     'L3_gnn_hk_w2': 8.0,
     'L3_gnn_hq_w1': 8.0,
     'L3_gnn_hq_w2': 8.0,
     'L3_gnn_ew_w': 5.266}
    for name, (base, spread) in spreads.items():
        noise = np.random.default_rng([zlib.crc32(name.encode()), seed]).standard_normal(out[name].shape)
        drawn = base * np.exp(spread * noise) if base else spread * noise
        out[name] = jnp.asarray(drawn.astype(out[name].dtype))
    for name, factor in factors.items():
        out[name] = (out[name] * factor).astype(out[name].dtype)
    return out
```

```python
from contextlib import ExitStack

import concourse.bass as bass
from concourse import mybir

P = 128
D = 128
N = 12500
E = 212500
NW = -(-N // P)
NP = NW * P
NT = P * -(-E // (P * P))
EP = NT * P
TC = NT // P
GS = 4
NS = -(-(-(-E // P) + NW - 1) // (2 * GS)) * 2 * GS
NC = -(-NS // P)
NSP = NC * P
NH0, DH0 = 8, 16
RT, VT = 16, 8
NH3, DH3 = 16, 8
AF, RF = 4, 64
KA = AF + RF
AC0 = D + NH0 + RT
AC3 = D + NH3
BIG = 1.0e30
EPS = 1e-5

ALU = mybir.AluOpType
ACT = mybir.ActivationFunctionType
F32 = mybir.dt.float32
BF16 = mybir.dt.bfloat16
I32 = mybir.dt.int32
AX = mybir.AxisListType.X
ds = bass.ds


def hold(eng, sem, value):
    eng.wait_ge(sem, value)
    eng.nop(nofuse=True)


class Stage:

    def __init__(self, nc, ctx, prefix):
        self.nc, self.ctx, self.prefix = nc, ctx, prefix
        self.held, self.sems = ExitStack(), []
        ctx.callback(self.give_back)

    def sb(self, name, shape, dt=F32):
        return self.ctx.enter_context(self.nc.sbuf_tensor(f"{self.prefix}_{name}", shape, dt))

    def ps(self, name, shape):
        return self.ctx.enter_context(self.nc.psum_tensor(f"{self.prefix}_{name}", shape, F32))

    def gather_sem(self, name):
        return self.nc.alloc_semaphore(f"{self.prefix}_{name}")

    def sem(self, name):
        self.sems.append(self.held.enter_context(self.nc.semaphore(f"{self.prefix}_{name}")))
        return self.sems[-1]

    def give_back(self):
        if self.sems:
            with self.nc.Block() as block:
                @block.sync
                def _(sp):
                    for s in self.sems:
                        sp.sem_clear(s)
        self.held.close()


def constants(nc, keep):
    keep.iota_row = keep.sb("iota_row", [P, P])
    keep.iota_col = keep.sb("iota_col", [P, 1])
    keep.ident = keep.sb("ident", [P, P])
    keep.before = keep.sb("before", [P, P])
    keep.eps = keep.sb("eps", [P, 1])
    ones_ready, placed = keep.sem("ones_ready"), keep.sem("placed")
    with nc.Block() as block:
        @block.gpsimd
        def _(pool):
            nc.gpsimd.memset(keep.eps[:], EPS)
            nc.gpsimd.memset(keep.before[:], 1.0)
            nc.gpsimd.memset(keep.ident[:], 0.0).then_inc(ones_ready, 1)
            nc.gpsimd.iota(keep.iota_row[:], [[1, P]], base=0, channel_multiplier=0,
                           allow_small_or_imprecise_dtypes=True)
            nc.gpsimd.iota(keep.iota_col[:], [[1, 1]], base=0, channel_multiplier=1,
                           allow_small_or_imprecise_dtypes=True)
            pool.wait_ge(ones_ready, 1)
            nc.gpsimd.affine_select(out=keep.ident[:], in_=keep.ident[:], compare_op=ALU.not_equal, fill=1.0,
                                    base=0, pattern=[[-1, P]], channel_multiplier=1)
            nc.gpsimd.affine_select(out=keep.before[:], in_=keep.before[:], compare_op=ALU.is_ge, fill=0.0,
                                    base=-1, pattern=[[1, P]], channel_multiplier=-1).then_inc(placed, 1)
            pool.wait_ge(placed, 1)


def plan_slots(nc, keep, dram, src, dst, etype, eweight):
    ctx = ExitStack()
    st = Stage(nc, ctx, "plan")
    with ctx:
        drow = st.sb("drow", [P, TC * P], I32)
        ab = st.sb("ab", [P, 2, TC])
        abi = st.sb("abi", [P, 2, TC], I32)
        cnt = st.sb("cnt", [P, TC])
        incl = st.sb("incl", [P, TC])
        zero = st.sb("zero", [P, NT])
        offs = st.sb("offs", [P, 1])
        bv = st.sb("bv", [P, 2, TC])
        row = st.sb("row", [P, 2, NT])
        step = st.sb("step", [P, NT])
        mask = st.sb("mask", [P, NT])
        prod = st.sb("prod", [P, NT])
        sid = st.sb("sid", [P, NC])
        tsum = st.sb("tsum", [P, NC])
        ksum = st.sb("ksum", [P, NC])
        tk = st.sb("tk", [P, 2, NC])
        tki = st.sb("tki", [P, 2, NC], I32)
        raw = st.sb("raw", [P, 4, P], I32)
        flt = st.sb("flt", [P, 5, P])
        dlb = st.sb("dlb", [P, P], BF16)
        none = st.sb("none", [P, 1])
        ps_o = st.ps("ps_o", [P, 512])
        ps_t = st.ps("ps_t", [P, 4, P])
        loaded, iota_done, v, pe_done = st.sem("loaded"), st.sem("iota"), st.sem("v"), st.sem("offs_summed")
        stored, rows_back, tk_stored, tk_back = st.sem("stored"), st.sem("rows_back"), st.sem("tk_stored"), st.sem("tk_back")
        tk_ready, got, rows_ready, rows_out = st.sem("tk_ready"), st.gather_sem("got"), st.sem("rows_ready"), st.sem("rows_out")
        turned, kept, bv_ready, d_ready = st.sem("turned"), st.sem("kept"), st.sem("bv_ready"), st.sem("d_ready")
        cnt_ready = st.sem("cnt_ready")
        ni = [0]
        with nc.Block() as block:
            @block.sync
            def _(sp):
                sp.dma_start(drow[:], dst.rearrange("(p f) -> p f", p=P)).then_inc(loaded, 16)
                sp.wait_ge(bv_ready, 1)
                for j in range(2):
                    sp.dma_start(dram.plan[j].rearrange("(p c) -> p c", p=P), bv[:, j, :]).then_inc(stored, 16)
                sp.wait_ge(stored, 32)
                for j in range(2):
                    sp.dma_start(row[:, j, :], dram.plan[j].partition_broadcast(P)).then_inc(rows_back, 16)
                sp.wait_ge(tk_ready, 1)
                for j in range(2):
                    sp.dma_start(dram.tk[j].rearrange("(c p) -> p c", p=P), tki[:, j, :],
                                 allow_slow_non_contiguous=True).then_inc(tk_stored, 16)
                sp.wait_ge(tk_stored, 32)
                sp.dma_start(keep.window[0:1, :], dram.tk[1:2, :]).then_inc(tk_back, 16)
                sp.wait_ge(tk_back, 16)
                for c in range(NC):
                    sp.wait_ge(rows_ready, c + 1)
                    sp.dma_start(dram.dlrow[c * P:(c + 1) * P, :], dlb[:]).then_inc(rows_out, 16)
                    sp.dma_start(dram.srcrow[c * P:(c + 1) * P, :], flt[:, 1, :]).then_inc(rows_out, 16)
                    sp.dma_start(dram.dlflat[c * P:(c + 1) * P, :], flt[:, 0, :]).then_inc(rows_out, 16)
                    sp.dma_start(dram.dstflat[c * P * P + 1:(c + 1) * P * P + 1].rearrange("(s e) -> s e", e=P),
                                 flt[:, 4, :]).then_inc(rows_out, 16)
                    sp.wait_ge(rows_out, 64 * (c + 1))
                sp.dma_start(dram.dstflat[0:1].unsqueeze(0), none[0:1, :]).then_inc(rows_out, 16)
                sp.wait_ge(rows_out, 64 * NC + 16)

            @block.gpsimd
            def _(pool):
                nc.gpsimd.iota(sid[:], [[P, NC]], base=0, channel_multiplier=1,
                               allow_small_or_imprecise_dtypes=True).then_inc(iota_done, 1)
                pool.wait_ge(tk_ready, 1)
                for c in range(NC):
                    if c:
                        pool.wait_ge(rows_ready, c)
                    for j, table in enumerate((dst, src, etype, eweight)):
                        pool.indirect_dma_start(
                            out=raw[:, j, :].bitcast(table.dtype), out_offset=None,
                            in_=table.rearrange("(t e) -> t e", e=P),
                            in_offset=bass.IndirectOffsetOnAxis(ap=tki[:, 0, c:c + 1], axis=0)).then_inc(got, 16)

            @block.tensor
            def _(pe):
                pe.wait_ge(cnt_ready, 1)
                pe.matmul(ps_o[:, 0:1], keep.before[:], incl[:, TC - 1:TC], start=True, stop=True).then_inc(pe_done, 1)
                for c in range(NC):
                    pe.wait_ge(rows_ready, c + 1)
                    if c:
                        pe.wait_ge(kept, c)
                    for j in range(4):
                        t = pe.transpose(ps_t[:, j, :], flt[:, j, :], keep.ident[:])
                    t.then_inc(turned, 1)

            @block.vector
            def _(dve):
                n = [0]

                def link(ins):
                    n[0] += 1
                    ins.then_inc(v, 1)
                    dve.wait_ge(v, n[0])

                link(nc.vector.memset(none[:], -1.0))
                link(nc.vector.memset(zero[:], 0.0))
                dve.wait_ge(loaded, 16)
                dv = drow[:].rearrange("p (c e) -> p c e", e=P)
                link(nc.vector.tensor_scalar(abi[:, 0, :], dv[:, :, 0], 7, None, ALU.arith_shift_right))
                link(nc.vector.tensor_scalar(abi[:, 1, :], dv[:, :, P - 1], 7, None, ALU.arith_shift_right))
                link(nc.vector.tensor_copy(ab[:], abi[:]))
                link(nc.vector.scalar_tensor_tensor(out=cnt[:], in0=ab[:, 1, :], scalar=1.0, in1=ab[:, 0, :],
                                                    op0=ALU.add, op1=ALU.subtract))
                nc.vector.tensor_tensor_scan(incl[:], cnt[:], zero[:, 0:TC], 0.0, ALU.add, ALU.add).then_inc(cnt_ready, 1)
                dve.wait_ge(pe_done, 1)
                link(nc.vector.tensor_copy(offs[:], ps_o[:, 0:1]))
                link(nc.vector.scalar_tensor_tensor(out=bv[:, 0, :], in0=incl[:], scalar=offs[:, 0:1], in1=cnt[:],
                                                    op0=ALU.add, op1=ALU.subtract))
                nc.vector.tensor_tensor(bv[:, 1, :], ab[:, 0, :], bv[:, 0, :], ALU.subtract).then_inc(bv_ready, 1)
                dve.wait_ge(rows_back, 32)
                link(nc.vector.tensor_copy(step[:, 0:1], row[:, 1, 0:1]))
                link(nc.vector.tensor_tensor(step[:, 1:NT], row[:, 1, 1:NT], row[:, 1, 0:NT - 1], ALU.subtract))
                dve.wait_ge(iota_done, 1)
                for c in range(NC):
                    link(nc.vector.tensor_scalar(mask[:], row[:, 0, :], sid[:, c:c + 1], None, ALU.is_le))
                    link(nc.vector.tensor_reduce(tsum[:, c:c + 1], mask[:], AX, ALU.add))
                    link(nc.vector.tensor_tensor(prod[:], mask[:], step[:], ALU.mult))
                    link(nc.vector.tensor_reduce(ksum[:, c:c + 1], prod[:], AX, ALU.add))
                link(nc.vector.tensor_scalar(tk[:, 0, :], tsum[:], -1.0, None, ALU.add))
                link(nc.vector.tensor_tensor(tk[:, 1, :], ksum[:], sid[:], ALU.add))
                link(nc.vector.tensor_scalar(tk[:, 1, :], tk[:, 1, :], float(NW), None, ALU.min))
                nc.vector.tensor_copy(tki[:], tk[:]).then_inc(tk_ready, 1)
                link(nc.vector.tensor_scalar(ksum[:], tk[:, 1, :], float(-P), None, ALU.mult))
                for c in range(NC):
                    dve.wait_ge(got, 64 * (c + 1))
                    if c:
                        dve.wait_ge(rows_out, 64 * c)
                        dve.wait_ge(turned, c)
                    link(nc.vector.tensor_copy(flt[:, 4, :], raw[:, 0, :]))
                    link(nc.vector.tensor_copy(flt[:, 1:3, :], raw[:, 1:3, :]))
                    link(nc.vector.tensor_copy(flt[:, 3, :], raw[:, 3, :].bitcast(F32)))
                    link(nc.vector.tensor_scalar(flt[:, 0, :], flt[:, 4, :], ksum[:, c:c + 1], None, ALU.add))
                    nc.vector.tensor_copy(dlb[:], flt[:, 0, :]).then_inc(rows_ready, 1)
                    dve.wait_ge(turned, c + 1)
                    sl = slice(c * P, (c + 1) * P)
                    link(nc.vector.tensor_copy(keep.dl[:, sl], ps_t[:, 0, :]))
                    link(nc.vector.tensor_copy(keep.src[:, sl], ps_t[:, 1, :]))
                    link(nc.vector.tensor_copy(keep.srcf[:, sl], ps_t[:, 1, :]))
                    link(nc.vector.tensor_copy(keep.et[:, sl], ps_t[:, 2, :]))
                    link(nc.vector.tensor_copy(keep.ew[:, sl], ps_t[:, 3, :]))
                    link(nc.vector.tensor_scalar(mask[:, 0:P], ps_t[:, 1, :], float(RT), None, ALU.mult))
                    nc.vector.tensor_tensor(keep.srct[:, sl], mask[:, 0:P], ps_t[:, 2, :], ALU.add).then_inc(kept, 1)
                dve.wait_ge(kept, NC)


class Chain:

    def __init__(self, eng, sem, per):
        self.eng, self.sem, self.per, self.base, self.n = eng, sem, per, 0, 0

    def start(self, i):
        self.base, self.n = i * self.per, 0

    def end(self):
        assert self.n == self.per, (self.n, self.per)

    def link(self, ins, held=False):
        self.n += 1
        ins.then_inc(self.sem, 1)
        if held:
            hold(self.eng, self.sem, self.base + self.n)
        else:
            self.eng.wait_ge(self.sem, self.base + self.n)


def layer_norm_statistics(nc, chain, x, stats, mv, var_ready):
    for w in range(2):
        chain.link(nc.vector.bn_stats(stats[:, w, :], x[:, w, :]), held=True)
    nc.vector.bn_aggr(mv[:, 0, :], stats[:, 0, :])
    nc.vector.bn_aggr(mv[:, 1, :], stats[:, 1, :]).then_inc(var_ready, 1)


def layer_norm_apply(nc, chain, out, x, mv, std, rstd, relu=True):
    chain.link(nc.vector.reciprocal(rstd[:], std[:]))
    for w in range(2):
        chain.link(nc.vector.tensor_scalar(out[:, w, :], x[:, w, :], mv[:, w, 0:1], rstd[:, w:w + 1],
                                           ALU.subtract, ALU.mult))
    if relu:
        chain.link(nc.vector.tensor_scalar(out[:], out[:], 0.0, None, ALU.max))


def rows(table, i):
    return table[ds(i * 2 * P, 2 * P), :].rearrange("(w p) d -> p w d", p=P)


def project_qkv(nc, keep, dram, x, wqkv, q):
    ctx = ExitStack()
    st = Stage(nc, ctx, "qkv")
    with ctx:
        w = st.sb("w", [P, 3 * D])
        xt = st.sb("xt", [P, 2, D])
        h = st.sb("h", [P, 2, D])
        hT = st.sb("hT", [P, 2, P])
        kv = st.sb("kv", [P, 2, 2 * D])
        stats, mv = st.sb("stats", [P, 2, 6]), st.sb("mv", [P, 2, 2])
        std, rstd = st.sb("std", [P, 2]), st.sb("rstd", [P, 2])
        ps_t = st.ps("ps_t", [P, 2, P])
        ps_o = st.ps("ps_o", [P, 2, 512])
        w_in, x_in, x_used, v = st.sem("w_in"), st.sem("x_in"), st.sem("x_used"), st.sem("v")
        var_ready, std_ready, h_ready = st.sem("var_ready"), st.sem("std_ready"), st.sem("h_ready")
        h_turned, hT_ready, projected = st.sem("h_turned"), st.sem("hT_ready"), st.sem("projected")
        q_kept, kv_ready, stored = st.sem("q_kept"), st.sem("kv_ready"), st.sem("stored")
        with nc.Block() as block:
            @block.sync
            def _(sp):
                sp.dma_start(w[:], wqkv).then_inc(w_in, 16)
                sp.sem_inc(x_used, 1)
                with sp.Fori(0, NW // 2) as i:
                    sp.wait_ge(x_used, i + 1)
                    sp.dma_start(xt[:], rows(x, i)).then_inc(x_in, 16)

            @block.vector
            def _(dve):
                ch = Chain(dve, v, 6)
                nc.vector.memset(q[:, NW * D:], 0.0)
                with dve.Fori(0, NW // 2) as i:
                    ch.start(i)
                    hold(dve, x_in, 16 * (i + 1))
                    layer_norm_statistics(nc, ch, xt, stats, mv, var_ready)
                    hold(dve, std_ready, i + 1)
                    layer_norm_apply(nc, ch, h, xt, mv, std, rstd)
                    dve.sem_inc(h_ready, 1)
                    dve.sem_inc(x_used, 1)
                    hold(dve, projected, i + 1)
                    nc.vector.tensor_copy(q[:, ds(i * 2 * D, 2 * D)].rearrange("p (w d) -> p w d", w=2),
                                          ps_o[:, :, 0:D]).then_inc(q_kept, 1)

                    ch.end()
            @block.scalar
            def _(act):
                act.sem_inc(stored, 32)
                with act.Fori(0, NW // 2) as i:
                    act.wait_ge(var_ready, i + 1)
                    nc.scalar.activation(std[:], mv[:, :, 1], ACT.Sqrt, bias=keep.eps[:]).then_inc(std_ready, 1)
                    act.wait_ge(stored, 32 * (i + 1))
                    act.wait_ge(h_turned, i + 1)
                    nc.scalar.copy(hT[:], ps_t[:]).then_inc(hT_ready, 1)
                    act.wait_ge(hT_ready, i + 1)
                    act.dma_start(dram.hT[:, ds(i * 2 * P, 2 * P)].rearrange("f (w p) -> f w p", w=2),
                                  hT[:]).then_inc(stored, 16)
                    act.wait_ge(q_kept, i + 2)
                    nc.scalar.copy(kv[:], ps_o[:, :, D:3 * D]).then_inc(kv_ready, 1)
                    act.wait_ge(kv_ready, i + 1)
                    act.dma_start(rows(dram.kv, i), kv[:]).then_inc(stored, 16)
                act.wait_ge(stored, 32 * (NW // 2 + 1))

            @block.tensor
            def _(pe):
                pe.wait_ge(w_in, 16)
                pe.sem_inc(q_kept, 1)
                with pe.Fori(0, NW // 2) as i:
                    pe.wait_ge(h_ready, i + 1)
                    for u in range(2):
                        t = pe.transpose(ps_t[:, u, :], h[:, u, :], keep.ident[:])
                    t.then_inc(h_turned, 1)
                    pe.wait_ge(hT_ready, i + 1)
                    pe.wait_ge(q_kept, i + 1)
                    for u in range(2):
                        t = pe.matmul(ps_o[:, u, 0:3 * D], hT[:, u, :], w[:], start=True, stop=True)
                    t.then_inc(projected, 1)


def at_start(j):
    return isinstance(j, int) and j == 0


def passes(eng, half, group):
    for b, nxt in ((0, (0, 1)), (1, (1, 0))):
        group(0, b, nxt)
    with eng.Fori(1, half - 1) as i:
        for b, nxt in ((0, (i, 1)), (1, (i + 1, 0))):
            group(i, b, nxt)
    for b, nxt in ((0, (half - 1, 1)), (1, None)):
        group(half - 1, b, nxt)


class Numbers:

    def __init__(self, eng, table, top, prefix, slots=GS):
        self.eng, self.table, self.top, self.slots = eng, table, top, slots
        self.regs = [eng.alloc_register(f"{prefix}_{u}") for u in range(slots)]

    def load(self, g):
        self.eng.load(self.regs, self.table[0:1, ds(g * self.slots, self.slots)])
        return [self.eng.snap(r, min_val=0, max_val=self.top) for r in self.regs]


def edges_0(nc, keep, dram, q, acc):
    ctx = ExitStack()
    st = Stage(nc, ctx, "e0")
    with ctx:
        B = range(2)
        dlr = st.sb("dlr", [P, 2, GS * P], BF16)
        spread = st.sb("spread", [P, 2, GS * P])
        collect = st.sb("collect", [P, 2, GS, P])
        gidx = st.sb("gidx", [P, 2, GS], I32)
        kv = st.sb("kv", [P, 2, GS, 2 * D])
        prod = st.sb("prod", [P, GS, D])
        score = st.sb("score", [P, 2, GS * NH0])
        vals = st.sb("vals", [P, 2, GS, AC0])
        ps_q = st.ps("ps_q", [P, 2, GS, D])
        ps_a = st.ps("ps_a", [P, 2, GS, 256])
        dlr_in, kv_in = [st.sem(f"dlr_in{b}") for b in B], [st.gather_sem(f"kv_in{b}") for b in B]
        idx_ready = st.sem("idx_ready")
        spread_ready, collect_ready = [st.sem(f"spread_ready{b}") for b in B], [st.sem(f"collect_ready{b}") for b in B]
        q_spread, prod_ready = [st.sem(f"q_spread{b}") for b in B], [st.sem(f"prod_ready{b}") for b in B]
        dots, score_ready = [st.sem(f"dots{b}") for b in B], [st.sem(f"score_ready{b}") for b in B]
        weights_ready, vals_ready = [st.sem(f"weights_ready{b}") for b in B], [st.sem(f"vals_ready{b}") for b in B]
        summed, added = [st.sem(f"summed{b}") for b in B], st.sem("added")
        half = NS // GS // 2
        with nc.Block() as block:
            @block.sync
            def _(sp):
                def group(i, b, nxt):
                    if not at_start(i):
                        sp.wait_ge(spread_ready[b], i)
                    sp.dma_start(dlr[:, b, :], local_rows(dram, 2 * i + b)).then_inc(dlr_in[b], 16)
                passes(sp, half, group)

            @block.gpsimd
            def _(pool):
                def group(i, b, nxt):
                    if not at_start(i):
                        hold(pool, vals_ready[b], i)
                    nc.gpsimd.tensor_copy(gidx[:, b, :], keep.src[:, ds((2 * i + b) * GS, GS)]).then_inc(idx_ready, 1)
                    hold(pool, idx_ready, 2 * i + b + 1)
                    for u in range(GS):
                        pool.indirect_dma_start(
                            out=kv[:, b, u, :], out_offset=None, in_=dram.kv,
                            in_offset=bass.IndirectOffsetOnAxis(ap=gidx[:, b, u:u + 1], axis=0)).then_inc(kv_in[b], 16)
                passes(pool, half, group)

            @block.tensor
            def _(pe):
                windows = Numbers(pe, keep.window, NW, "e0_pe")

                def spread_q(i, b):
                    ks = windows.load(2 * i + b)
                    pe.wait_ge(spread_ready[b], i + 1)
                    if not at_start(i):
                        pe.wait_ge(prod_ready[b], i)
                    for u in range(GS):
                        t = pe.matmul(ps_q[:, b, u, :], spread[:, b, u * P:(u + 1) * P], q[:, ds(ks[u] * D, D)],
                                      start=True, stop=True)
                    t.then_inc(q_spread[b], 1)

                def group(i, b, nxt):
                    if nxt:
                        spread_q(*nxt)
                    pe.wait_ge(collect_ready[b], i + 1)
                    pe.wait_ge(vals_ready[b], i + 1)
                    if not at_start(i):
                        pe.wait_ge(added, (2 * i + b - 1) * GS + 1)
                    for u in range(GS):
                        t = pe.matmul(ps_a[:, b, u, 0:AC0], collect[:, b, u, :], vals[:, b, u, :], start=True, stop=True)
                    t.then_inc(summed[b], 1)

                spread_q(0, 0)
                passes(pe, half, group)

            @block.scalar
            def _(act):
                def group(i, b, nxt):
                    act.wait_ge(score_ready[b], i + 1)
                    nc.scalar.activation(vals[:, b, :, D:D + NH0],
                                         score[:, b, :].rearrange("p (u h) -> p u h", u=GS),
                                         ACT.Exp, scale=float(DH0) ** -0.5).then_inc(weights_ready[b], 1)
                passes(act, half, group)

            @block.vector
            def _(dve):
                windows = Numbers(dve, keep.window, NW, "e0_dve")

                def make_spread(i, b):
                    dve.wait_ge(dlr_in[b], 16 * (i + 1))
                    if not at_start(i):
                        dve.wait_ge(q_spread[b], i)
                    nc.vector.tensor_scalar(spread[:, b, :], dlr[:, b, :], keep.iota_col[:, 0:1], None,
                                            ALU.is_equal).then_inc(spread_ready[b], 1)

                def make_collect(i, b):
                    g = 2 * i + b
                    if not at_start(i):
                        dve.wait_ge(summed[b], i)
                    nc.vector.tensor_tensor(
                        collect[:, b], keep.iota_row[:].unsqueeze(1).broadcast_to([P, GS, P]),
                        keep.dl[:, ds(g * GS, GS)].unsqueeze(2).broadcast_to([P, GS, P]), ALU.is_equal)
                    nc.vector.tensor_tensor(
                        vals[:, b, :, D + NH0:AC0], keep.iota_row[:, 0:RT].unsqueeze(1).broadcast_to([P, GS, RT]),
                        keep.et[:, ds(g * GS, GS)].unsqueeze(2).broadcast_to([P, GS, RT]),
                        ALU.is_equal).then_inc(collect_ready[b], 1)

                def add_sums(i, b):
                    ks = windows.load(2 * i + b)
                    dve.wait_ge(summed[b], i + 1)
                    for u in range(GS):
                        a = acc[:, ds(ks[u] * AC0, AC0)]
                        dve.wait_ge(added, (2 * i + b) * GS + u + 1)
                        nc.vector.tensor_tensor(a, a, ps_a[:, b, u, 0:AC0], ALU.add).then_inc(added, 1)

                def group(i, b, nxt):
                    if nxt:
                        make_spread(*nxt)
                    dve.wait_ge(q_spread[b], i + 1)
                    dve.wait_ge(kv_in[b], 16 * GS * (i + 1))
                    if not (at_start(i) and b == 0):
                        dve.wait_ge(dots[1 - b], i + b)
                    nc.vector.tensor_tensor(prod[:], kv[:, b, :, 0:D], ps_q[:, b], ALU.mult).then_inc(prod_ready[b], 1)
                    dve.wait_ge(prod_ready[b], i + 1)
                    nc.vector.tensor_reduce(score[:, b, :], prod[:].rearrange("p u (h e) -> p (u h) e", e=DH0),
                                            AX, ALU.add).then_inc(dots[b], 1)
                    dve.wait_ge(dots[b], i + 1)
                    lim = 5.0 * float(DH0) ** 0.5
                    nc.vector.tensor_scalar(score[:, b, :], score[:, b, :], -lim, lim, ALU.max,
                                            ALU.min).then_inc(score_ready[b], 1)
                    if b == 1:
                        add_sums(i, 0)
                    elif not at_start(i):
                        add_sums(i - 1, 1)
                    if nxt:
                        make_collect(*nxt)
                    dve.wait_ge(weights_ready[b], i + 1)
                    nc.vector.tensor_tensor(
                        vals[:, b, :, 0:D].rearrange("p u (h e) -> p u h e", e=DH0),
                        kv[:, b, :, D:2 * D].rearrange("p u (h e) -> p u h e", e=DH0),
                        vals[:, b, :, D:D + NH0].unsqueeze(3).broadcast_to([P, GS, NH0, DH0]),
                        ALU.mult).then_inc(vals_ready[b], 1)

                nc.vector.memset(acc[:], 0.0).then_inc(added, 1)
                make_spread(0, 0)
                make_collect(0, 0)
                passes(dve, half, group)
                add_sums(half - 1, 1)


def local_rows(dram, g):
    return dram.dlrow.rearrange("s e -> (s e)")[ds(g * GS * P, GS * P)].partition_broadcast(P)


def norm_coefficients(nc, link, scale, shift, stats, mv, var_ready, std, std_ready, gain, offset, nodes, turn, dve):
    full = N // P // 4
    for c in range(full):
        link(nc.vector.bn_stats(stats[:, c, :], nodes[:, 4 * c:4 * c + 4, 0:D]), held=True)
    rest = [(w, min(P, N - w * P)) for w in range(4 * full, NW)]
    for j, (w, n) in enumerate(rest):
        link(nc.vector.bn_stats(stats[:, full + j, :], nodes[:, w, 0:n]), held=True)
    nc.vector.bn_aggr(mv[:], stats[:, 0:full + len(rest), :]).then_inc(var_ready, 1)
    dve.wait_ge(std_ready, turn)
    link(nc.vector.reciprocal(scale[:], std[:]))
    link(nc.vector.tensor_tensor(scale[:], scale[:], gain, ALU.mult))
    link(nc.vector.tensor_tensor(shift[:], mv[:, 0:1], scale[:], ALU.mult))
    link(nc.vector.tensor_tensor(shift[:], offset, shift[:], ALU.subtract))


def mix_0(nc, keep, dram, ins, nodes):
    ctx = ExitStack()
    st = Stage(nc, ctx, "m0")
    nd = nodes[:].rearrange("p (w c) -> p w c", c=AC0)
    HT = NW // 2
    with ctx:
        wo, w1 = st.sb("wo", [P, D]), st.sb("w1", [P, 2 * D])
        w2, cols = st.sb("w2", [P, 2, D]), st.sb("cols", [P, 8])
        wt, bt = st.sb("wt", [P, (RT + VT) * D]), st.sb("bt", [RT + VT, D])
        ntype, ntf = st.sb("ntype", [P, NW], I32), st.sb("ntf", [P, NW])
        den, rec = st.sb("den", [P, 2, NH0]), st.sb("rec", [P, 2, NH0])
        at, aT, hT = st.sb("at", [P, 2, D]), st.sb("aT", [P, 2, P]), st.sb("hT", [P, 2, P])
        xc, hid = st.sb("xc", [P, 2, P]), st.sb("hid", [P, 2, 2 * P])
        stats, mv = st.sb("stats", [P, 32, 6]), st.sb("mv", [P, 2])
        std, scale, shift = st.sb("std", [P, 1]), st.sb("scale", [P, 1]), st.sb("shift", [P, 1])
        deg, sqd, has = st.sb("deg", [P, NW + 1]), st.sb("sqd", [P, NW + 1]), st.sb("has", [P, NW + 1])
        xt, h = st.sb("xt", [P, 2, D]), st.sb("h", [P, 2, D])
        st2, mv2 = st.sb("st2", [P, 2, 6]), st.sb("mv2", [P, 2, 2])
        sd2, rs2 = st.sb("sd2", [P, 2]), st.sb("rs2", [P, 2])
        ind, indT = st.sb("ind", [P, 2, RT + VT]), st.sb("indT", [RT + VT, 2, P])
        hw = st.sb("hw", [P, 2, RT * D])
        ps_t = st.ps("ps_t", [P, 2, 2, P])
        ps_w = st.ps("ps_w", [P, RT + VT, D])
        ps_b = st.ps("ps_b", [P, 512])
        w_in, v, var_ready, std_ready = st.sem("w_in"), st.sem("v"), st.sem("var_ready"), st.sem("std_ready")
        hT_in, hT_used, at_ready, at_turned = st.sem("hT_in"), st.sem("hT_used"), st.sem("at_ready"), st.sem("at_turned")
        aT_ready, mixed, y_ready = st.sem("aT_ready"), st.sem("mixed"), st.sem("y_ready")
        xc_ready, up, hid_ready, down, y2_ready = (st.sem("xc_ready"), st.sem("up"), st.sem("hid_ready"),
                                                   st.sem("down"), st.sem("y2_ready"))
        x_in, z_ready, z_turned, x1_ready = st.sem("x_in"), st.sem("z_ready"), st.sem("z_turned"), st.sem("x1_ready")
        x1_out, var2_ready, std2_ready, h_ready = st.sem("x1_out"), st.sem("var2_ready"), st.sem("std2_ready"), st.sem("h_ready")
        h_turned, hT2_ready, typed, picked, hw_ready = (st.sem("h_turned"), st.sem("hT2_ready"), st.sem("typed"),
                                                        st.sem("picked"), st.sem("hw_ready"))
        hw_out, v1, v2, v3 = [st.sem(f"hw_out{u}") for u in range(2)], st.sem("v1"), st.sem("v2"), st.sem("v3")
        degs, roots = st.sem("degs"), st.sem("roots")
        WL = [(wo[:], ins["L0_gnn_Wo"]), (w1[:], ins["L0_gnn_W1"]),
              (w2[:], ins["L0_gnn_W2"].rearrange("(c p) d -> p c d", p=P)), (cols[:], ins["L0_cols"]),
              (wt[:], ins["L1_W"]), (bt[:], ins["L1_b"]), (ntype[:], ins["node_type_8"])]
        NWL = 16 * len(WL)
        with nc.Block() as block:
            @block.sync
            def _(sp):
                for to, frm in WL:
                    sp.dma_start(to, frm).then_inc(w_in, 16)
                sp.sem_inc(hT_used, 1)
                with sp.Fori(0, HT) as i:
                    sp.wait_ge(hT_used, i + 1)
                    sp.dma_start(hT[:], dram.hT[:, ds(i * 2 * P, 2 * P)].rearrange("f (w p) -> f w p", w=2)
                                 ).then_inc(hT_in, 16)
                with sp.Fori(0, HT) as i:
                    sp.wait_ge(x1_out, 16 * (i + 1))
                    sp.dma_start(xt[:], rows(ins["x"], i)).then_inc(x_in, 16)
                    for u in range(2):
                        sp.wait_ge(hw_ready, 2 * i + u + 2)
                        sp.dma_start(dram.hw.rearrange("(n t) d -> n (t d)", t=RT)[ds((2 * i + u) * P, P), :],
                                     hw[:, u, :]).then_inc(hw_out[u], 16)
                for u in range(2):
                    sp.wait_ge(hw_out[u], 16 * (HT + 1))

            @block.tensor
            def _(pe):
                pe.wait_ge(w_in, NWL)
                with pe.Fori(0, HT) as i:
                    pe.wait_ge(at_ready, i + 1)
                    for u in range(2):
                        t = pe.transpose(ps_t[:, 0, u, :], at[:, u, :], keep.ident[:])
                    t.then_inc(at_turned, 1)
                    pe.wait_ge(aT_ready, i + 1)
                    pe.matmul(ps_b[:, 0:2 * P], wo[:], aT[:].rearrange("p u e -> p (u e)"), start=True,
                              stop=True).then_inc(mixed, 1)
                with pe.Fori(0, HT) as i:
                    pe.wait_ge(xc_ready, i + 1)
                    for c in range(2):
                        t = pe.matmul(ps_w[:, 4 * c:4 * c + 2, :].rearrange("p a b -> p (a b)"),
                                      w1[:, c * D:(c + 1) * D], xc[:].rearrange("p u e -> p (u e)"),
                                      start=True, stop=True)
                    t.then_inc(up, 1)
                    pe.wait_ge(hid_ready, i + 1)
                    for c in range(2):
                        t = pe.matmul(ps_b[:, 0:2 * P], w2[:, c, :], hid[:, c, :], start=(c == 0), stop=(c == 1))
                    t.then_inc(down, 1)
                with pe.Fori(0, HT) as i:
                    pe.wait_ge(z_ready, i + 1)
                    for u in range(2):
                        t = pe.transpose(ps_t[:, 0, u, :], xc[:, u, :], keep.ident[:])
                    t.then_inc(z_turned, 1)
                    pe.wait_ge(h_ready, i + 1)
                    for u in range(2):
                        pe.transpose(ps_t[:, 1, u, :], h[:, u, :], keep.ident[:])
                        t = pe.transpose(ps_b[0:RT + VT, u * P:(u + 1) * P], ind[:, u, :], keep.ident[:])
                    t.then_inc(h_turned, 1)
                    pe.wait_ge(hT2_ready, i + 1)
                    for u in range(2):
                        pe.wait_ge(picked, 2 * i + u + 1)
                        pe.wait_ge(hw_ready, 2 * i + u + 1)
                        for c in range((RT + VT) // 4):
                            pe.matmul(ps_w[:, 4 * c:4 * c + 4, :].rearrange("p a b -> p (a b)"), hT[:, u, :],
                                      wt[:, c * 512:(c + 1) * 512], start=True, stop=True)
                        pe.matmul(ps_b[:, 256:256 + D], indT[:, u, :], bt[:], start=True, stop=True).then_inc(typed, 1)

            @block.scalar
            def _(act):
                act.wait_ge(w_in, NWL)
                with act.Fori(0, HT) as i:
                    act.wait_ge(at_turned, i + 1)
                    nc.scalar.copy(aT[:], ps_t[:, 0]).then_inc(aT_ready, 1)
                act.wait_ge(degs, 1)
                nc.scalar.activation(sqd[:], deg[:], ACT.Sqrt).then_inc(roots, 1)
                act.wait_ge(var_ready, 1)
                nc.scalar.activation(std[:], mv[:, 1:2], ACT.Sqrt, bias=keep.eps[:]).then_inc(std_ready, 1)
                with act.Fori(0, HT) as i:
                    act.wait_ge(up, i + 1)
                    for c in range(2):
                        a = nc.scalar.activation(hid[:, c, :], ps_w[:, 4 * c:4 * c + 2, :].rearrange("p a b -> p (a b)"),
                                                 ACT.Relu, bias=cols[:, 1 + c:2 + c])
                    a.then_inc(hid_ready, 1)
                act.wait_ge(var_ready, 2)
                nc.scalar.activation(std[:], mv[:, 1:2], ACT.Sqrt, bias=keep.eps[:]).then_inc(std_ready, 1)
                act.sem_inc(x1_out, 16)
                act.sem_inc(hw_ready, 1)
                act.sem_inc(hw_out[0], 16)
                act.sem_inc(hw_out[1], 16)
                with act.Fori(0, HT) as i:
                    act.wait_ge(x1_ready, i + 1)
                    act.dma_start(rows(dram.x1, i), xt[:]).then_inc(x1_out, 16)
                    act.wait_ge(var2_ready, i + 1)
                    nc.scalar.activation(sd2[:], mv2[:, :, 1], ACT.Sqrt, bias=keep.eps[:]).then_inc(std2_ready, 1)
                    act.wait_ge(h_turned, i + 1)
                    nc.scalar.copy(indT[:], ps_b[0:RT + VT, 0:2 * P].rearrange("p (u e) -> p u e", u=2))
                    nc.scalar.copy(hT[:], ps_t[:, 1]).then_inc(hT2_ready, 1)
                    for u in range(2):
                        act.wait_ge(typed, 2 * i + u + 1)
                        hold(act, hw_out[u], 16 * (i + 1))
                        nc.scalar.copy(hw[:, u, :], ps_w[:, 0:RT, :].rearrange("p a b -> p (a b)")).then_inc(hw_ready, 1)
                act.wait_ge(x1_out, 16 * (HT + 1))

            @block.vector
            def _(dve):
                ch = Chain(dve, v1, 3)
                dve.wait_ge(w_in, NWL)
                with dve.Fori(0, HT) as i:
                    ch.start(i)
                    w = nodes[:, ds(i * 2 * AC0, 2 * AC0)].rearrange("p (w c) -> p w c", w=2)
                    ch.link(nc.vector.tensor_scalar(den[:], w[:, :, D:D + NH0], 1e-6, None, ALU.add))
                    ch.link(nc.vector.reciprocal(rec[:], den[:]))
                    nc.vector.tensor_tensor(at[:].rearrange("p w (h e) -> p w h e", e=DH0),
                                            w[:, :, 0:D].rearrange("p w (h e) -> p w h e", e=DH0),
                                            rec[:].unsqueeze(3).broadcast_to([P, 2, NH0, DH0]),
                                            ALU.mult).then_inc(at_ready, 1)
                    dve.wait_ge(hT_in, 16 * (i + 1))
                    dve.wait_ge(mixed, i + 1)
                    ch.link(nc.vector.scalar_tensor_tensor(
                        out=w[:, :, 0:D], in0=ps_b[:, 0:2 * P].rearrange("p (w d) -> p w d", w=2),
                        scalar=cols[:, 0:1], in1=hT[:], op0=ALU.add, op1=ALU.add))
                    dve.sem_inc(hT_used, 1)
                    ch.end()
                n = [0]

                def link(ins_, held=False):
                    n[0] += 1
                    ins_.then_inc(v, 1)
                    (hold(dve, v, n[0]) if held else dve.wait_ge(v, n[0]))

                cnt = nd[:, :, D + NH0:AC0]
                link(nc.vector.tensor_reduce(deg[:], cnt, AX, ALU.add))
                link(nc.vector.tensor_scalar(has[:], deg[:], 1.0, None, ALU.min))
                nc.vector.tensor_scalar(deg[:], deg[:], 1.0, None, ALU.max).then_inc(degs, 1)
                dve.wait_ge(roots, 1)
                link(nc.vector.reciprocal(sqd[:], sqd[:]))
                link(nc.vector.tensor_tensor(keep.dis[:], sqd[:], has[:], ALU.mult))
                link(nc.vector.tensor_copy(ntf[:], ntype[:]))
                norm_coefficients(nc, link, scale, shift, stats, mv, var_ready, std, std_ready, cols[:, 3:4],
                                  cols[:, 4:5], nd, 1, dve)
                ch = Chain(dve, v2, 1)
                with dve.Fori(0, HT) as i:
                    ch.start(i)
                    w = nodes[:, ds(i * 2 * AC0, 2 * AC0)].rearrange("p (w c) -> p w c", w=2)
                    nc.vector.tensor_scalar(xc[:], w[:, :, 0:D], scale[:, 0:1], shift[:, 0:1], ALU.mult,
                                            ALU.add).then_inc(xc_ready, 1)
                    dve.wait_ge(down, i + 1)
                    ch.link(nc.vector.scalar_tensor_tensor(
                        out=w[:, :, 0:D], in0=ps_b[:, 0:2 * P].rearrange("p (w d) -> p w d", w=2),
                        scalar=cols[:, 5:6], in1=xc[:], op0=ALU.add, op1=ALU.add))
                    ch.end()
                norm_coefficients(nc, link, scale, shift, stats, mv, var_ready, std, std_ready, cols[:, 6:7],
                                  cols[:, 7:8], nd, 2, dve)
                dve.sem_inc(picked, 1)
                ch = Chain(dve, v3, 6 + 3 + 2 * (VT + 1))
                with dve.Fori(0, HT) as i:
                    ch.start(i)
                    w = nodes[:, ds(i * 2 * AC0, 2 * AC0)].rearrange("p (w c) -> p w c", w=2)
                    nc.vector.tensor_scalar(xc[:], w[:, :, 0:D], scale[:, 0:1], shift[:, 0:1], ALU.mult,
                                            ALU.add).then_inc(z_ready, 1)
                    dve.wait_ge(x_in, 16 * (i + 1))
                    dve.wait_ge(z_turned, i + 1)
                    ch.link(nc.vector.tensor_tensor(xt[:], xt[:], ps_t[:, 0], ALU.add), held=True)
                    dve.sem_inc(x1_ready, 1)
                    layer_norm_statistics(nc, ch, xt, st2, mv2, var2_ready)
                    ch.link(nc.vector.tensor_scalar(ind[:, :, 0:RT], w[:, :, D + NH0:AC0], 1.0, None, ALU.min))
                    ch.link(nc.vector.tensor_tensor(
                        ind[:, :, RT:RT + VT], keep.iota_row[:, 0:VT].unsqueeze(1).broadcast_to([P, 2, VT]),
                        ntf[:, ds(i * 2, 2)].unsqueeze(2).broadcast_to([P, 2, VT]), ALU.is_equal))
                    hold(dve, std2_ready, i + 1)
                    layer_norm_apply(nc, ch, h, xt, mv2, sd2, rs2)
                    dve.sem_inc(h_ready, 1)
                    for u in range(2):
                        dve.wait_ge(typed, 2 * i + u + 1)
                        hold(dve, hw_ready, 2 * i + u + 2)
                        ch.link(nc.vector.tensor_copy(w[:, u, 0:D], ps_b[:, 256:256 + D]), held=True)
                        for t in range(VT):
                            ch.link(nc.vector.scalar_tensor_tensor(
                                out=w[:, u, 0:D], in0=ps_w[:, RT + t, :], scalar=ind[:, u, RT + t:RT + t + 1],
                                in1=w[:, u, 0:D], op0=ALU.mult, op1=ALU.add))
                        dve.sem_inc(picked, 1)
                    ch.end()
                link(nc.vector.tensor_scalar(cnt, cnt, 1.0, None, ALU.max))
                link(nc.vector.reciprocal(cnt, cnt))


def edges_1(nc, keep, dram, nodes):
    ctx = ExitStack()
    st = Stage(nc, ctx, "e1")
    with ctx:
        B = range(2)
        dlr = st.sb("dlr", [P, 2, GS * P], BF16)
        spread = st.sb("spread", [P, 2, GS * P])
        collect = st.sb("collect", [P, 2, GS, P])
        gidx = st.sb("gidx", [P, 2, GS], I32)
        msg = st.sb("msg", [P, 2, GS, D])
        hot, share = st.sb("hot", [P, GS, RT]), st.sb("share", [P, GS])
        ps_r = st.ps("ps_r", [P, 2, 512])
        ps_a = st.ps("ps_a", [P, 2, GS, D])
        dlr_in, msg_in = [st.sem(f"dlr_in{b}") for b in B], [st.gather_sem(f"msg_in{b}") for b in B]
        idx_ready = st.sem("idx_ready")
        spread_ready, counts_spread = [st.sem(f"spread_ready{b}") for b in B], [st.sem(f"counts_spread{b}") for b in B]
        hot_ready, share_ready = st.sem("hot_ready"), st.sem("share_ready")
        counts_read, collect_ready = [st.sem(f"counts_read{b}") for b in B], [st.sem(f"collect_ready{b}") for b in B]
        summed, added = [st.sem(f"summed{b}") for b in B], st.sem("added")
        half = NS // GS // 2
        with nc.Block() as block:
            @block.sync
            def _(sp):
                def group(i, b, nxt):
                    if not at_start(i):
                        sp.wait_ge(spread_ready[b], i)
                    sp.dma_start(dlr[:, b, :], local_rows(dram, 2 * i + b)).then_inc(dlr_in[b], 16)
                passes(sp, half, group)

            @block.gpsimd
            def _(pool):
                def group(i, b, nxt):
                    if not at_start(i):
                        hold(pool, summed[b], i)
                    nc.gpsimd.tensor_copy(gidx[:, b, :], keep.srct[:, ds((2 * i + b) * GS, GS)]).then_inc(idx_ready, 1)
                    hold(pool, idx_ready, 2 * i + b + 1)
                    for u in range(GS):
                        pool.indirect_dma_start(
                            out=msg[:, b, u, :], out_offset=None, in_=dram.hw,
                            in_offset=bass.IndirectOffsetOnAxis(ap=gidx[:, b, u:u + 1], axis=0)).then_inc(msg_in[b], 16)
                passes(pool, half, group)

            @block.tensor
            def _(pe):
                windows = Numbers(pe, keep.window, NW, "e1_pe")

                def spread_counts(i, b):
                    ks = windows.load(2 * i + b)
                    pe.wait_ge(spread_ready[b], i + 1)
                    if not at_start(i):
                        pe.wait_ge(counts_read[b], i)
                    for u in range(GS):
                        t = pe.matmul(ps_r[:, b, u * RT:(u + 1) * RT], spread[:, b, u * P:(u + 1) * P],
                                      nodes[:, ds(ks[u] * AC0 + D + NH0, RT)], start=True, stop=True)
                    t.then_inc(counts_spread[b], 1)

                def group(i, b, nxt):
                    if nxt:
                        spread_counts(*nxt)
                    pe.wait_ge(collect_ready[b], i + 1)
                    pe.wait_ge(msg_in[b], 16 * GS * (i + 1))
                    if not at_start(i):
                        pe.wait_ge(added, (2 * i + b - 1) * GS)
                    for u in range(GS):
                        t = pe.matmul(ps_a[:, b, u, :], collect[:, b, u, :], msg[:, b, u, :], start=True, stop=True)
                    t.then_inc(summed[b], 1)

                spread_counts(0, 0)
                passes(pe, half, group)

            @block.vector
            def _(dve):
                windows = Numbers(dve, keep.window, NW, "e1_dve")

                def make_spread(i, b):
                    dve.wait_ge(dlr_in[b], 16 * (i + 1))
                    if not at_start(i):
                        dve.wait_ge(counts_spread[b], i)
                    nc.vector.tensor_scalar(spread[:, b, :], dlr[:, b, :], keep.iota_col[:, 0:1], None,
                                            ALU.is_equal).then_inc(spread_ready[b], 1)

                def add_sums(i, b):
                    ks = windows.load(2 * i + b)
                    dve.wait_ge(summed[b], i + 1)
                    for u in range(GS):
                        a = nodes[:, ds(ks[u] * AC0, D)]
                        s = (2 * i + b) * GS + u
                        if not (isinstance(s, int) and s == 0):
                            dve.wait_ge(added, s)
                        nc.vector.tensor_tensor(a, a, ps_a[:, b, u, :], ALU.add).then_inc(added, 1)

                def group(i, b, nxt):
                    g = 2 * i + b
                    if nxt:
                        make_spread(*nxt)
                    nc.vector.tensor_tensor(
                        hot[:], keep.iota_row[:, 0:RT].unsqueeze(1).broadcast_to([P, GS, RT]),
                        keep.et[:, ds(g * GS, GS)].unsqueeze(2).broadcast_to([P, GS, RT]),
                        ALU.is_equal).then_inc(hot_ready, 1)
                    dve.wait_ge(hot_ready, g + 1)
                    dve.wait_ge(counts_spread[b], i + 1)
                    nc.vector.tensor_tensor(hot[:], hot[:], ps_r[:, b, 0:GS * RT].rearrange("p (u t) -> p u t", u=GS),
                                            ALU.mult).then_inc(counts_read[b], 1)
                    dve.wait_ge(counts_read[b], i + 1)
                    nc.vector.tensor_reduce(share[:], hot[:], AX, ALU.add).then_inc(share_ready, 1)
                    dve.wait_ge(share_ready, g + 1)
                    if not at_start(i):
                        dve.wait_ge(summed[b], i)
                    for u in range(GS):
                        t = nc.vector.tensor_scalar(collect[:, b, u, :], keep.iota_row[:], keep.dl[:, ds(g * GS + u, 1)],
                                                    share[:, u:u + 1], ALU.is_equal, ALU.mult)
                    t.then_inc(collect_ready[b], 1)
                    if b == 1:
                        add_sums(i, 0)
                    elif not at_start(i):
                        add_sums(i - 1, 1)

                make_spread(0, 0)
                passes(dve, half, group)
                add_sums(half - 1, 1)


def clear_tables(nc, dram):
    ctx = ExitStack()
    st = Stage(nc, ctx, "clear")
    W = (NW + 1) * D // 9
    with ctx:
        zero = st.sb("zero", [P, W])
        made, out = st.sem("made"), st.sem("out")
        with nc.Block() as block:
            @block.gpsimd
            def _(pool):
                nc.gpsimd.memset(zero[:], 0.0).then_inc(made, 1)

            @block.sync
            def _(sp):
                sp.wait_ge(made, 1)
                for table in dram.side:
                    flat = table.rearrange("(p w) d -> p (w d)", p=P)
                    with sp.Fori(0, 9) as i:
                        sp.dma_start(flat[:, ds(i * W, W)], zero[:]).then_inc(out, 16)
                sp.wait_ge(out, 16 * 9 * GS)


def mix_1(nc, keep, dram, nodes, hp):
    ctx = ExitStack()
    st = Stage(nc, ctx, "m1")
    HT = NW // 2
    with ctx:
        xt, h = st.sb("xt", [P, 2, 2, D]), st.sb("h", [P, 2, D])
        stats, mv = st.sb("stats", [P, 2, 6]), st.sb("mv", [P, 2, 2])
        std, rstd = st.sb("std", [P, 2]), st.sb("rstd", [P, 2])
        x_in, x2_ready, x_out = st.sem("x_in"), st.sem("x2_ready"), st.sem("x_out")
        var_ready, std_ready, v, done = st.sem("var_ready"), st.sem("std_ready"), st.sem("v"), st.sem("done")
        h_ready = st.sem("h_ready")
        with nc.Block() as block:
            @block.sync
            def _(sp):
                with sp.Fori(0, HT) as i:
                    sp.wait_ge(done, i + 1)
                    sp.dma_start(xt[:, 0], rows(dram.x1, i)).then_inc(x_in, 16)

            @block.scalar
            def _(act):
                act.sem_inc(x_out, 32)
                with act.Fori(0, HT) as i:
                    act.wait_ge(x2_ready, i + 1)
                    act.dma_start(rows(dram.x2, i), xt[:, 1]).then_inc(x_out, 16)
                    act.wait_ge(var_ready, i + 1)
                    nc.scalar.activation(std[:], mv[:, :, 1], ACT.Sqrt, bias=keep.eps[:]).then_inc(std_ready, 1)
                    act.wait_ge(h_ready, i + 1)
                    act.dma_start(rows(dram.h2, i), h[:]).then_inc(x_out, 16)
                act.wait_ge(x_out, 32 * (HT + 1))

            @block.vector
            def _(dve):
                nc.vector.memset(hp[:, NW * D:], 0.0)
                ch = Chain(dve, v, 8)
                dve.sem_inc(done, 1)
                with dve.Fori(0, HT) as i:
                    ch.start(i)
                    w = nodes[:, ds(i * 2 * AC0, 2 * AC0)].rearrange("p (w c) -> p w c", w=2)
                    dve.wait_ge(x_in, 16 * (i + 1))
                    dve.wait_ge(x_out, 32 * (i + 1))
                    ch.link(nc.vector.scalar_tensor_tensor(out=xt[:, 1], in0=w[:, :, 0:D], scalar=0.0, in1=xt[:, 0],
                                                           op0=ALU.max, op1=ALU.add), held=True)
                    dve.sem_inc(x2_ready, 1)
                    dve.sem_inc(done, 1)
                    layer_norm_statistics(nc, ch, xt[:, 1], stats, mv, var_ready)
                    hold(dve, std_ready, i + 1)
                    layer_norm_apply(nc, ch, h, xt[:, 1], mv, std, rstd)
                    dve.sem_inc(h_ready, 1)
                    for u in range(2):
                        t = nc.vector.tensor_scalar(hp[:, ds((2 * i + u) * D, D)], h[:, u, :],
                                                    keep.dis[:, ds(2 * i + u, 1)], None, ALU.mult)
                    ch.link(t)


                    ch.end()
def edges_2(nc, keep, dram, hp):
    ctx = ExitStack()
    st = Stage(nc, ctx, "e2")
    with ctx:
        B = range(2)
        srow = st.sb("srow", [P, 2, GS, P])
        same, collect = st.sb("same", [P, 2, GS, P]), st.sb("collect", [P, 2, GS, P])
        lower, earlier = st.sb("lower", [P, P]), st.sb("earlier", [P, GS, P])
        cnt, spare, dest = st.sb("cnt", [P, GS]), st.sb("spare", [P, GS]), st.sb("dest", [P, GS])
        ncol = st.sb("ncol", [P, 1])
        index = st.sb("index", [P, 2, GS], I32)
        joint, sums = st.sb("joint", [P, 2, GS, P]), st.sb("sums", [P, 2, GS, D])
        ps_j, ps_s = st.ps("ps_j", [P, 2, GS, P]), st.ps("ps_s", [P, 2, GS, D])
        srow_in, same_ready = [st.sem(f"srow_in{b}") for b in B], [st.sem(f"same_ready{b}") for b in B]
        joined, joint_ready = [st.sem(f"joined{b}") for b in B], [st.sem(f"joint_ready{b}") for b in B]
        summed, sums_ready = [st.sem(f"summed{b}") for b in B], [st.sem(f"sums_ready{b}") for b in B]
        index_ready, v = [st.sem(f"index_ready{b}") for b in B], st.sem("v")
        added = [st.gather_sem(f"added{u}") for u in range(GS)]
        lower_made = st.sem("lower_made")
        half = NS // GS // 2
        with nc.Block() as block:
            @block.sync
            def _(sp):
                def group(i, b, nxt):
                    if not at_start(i):
                        sp.wait_ge(same_ready[b], i)
                    sp.dma_start(srow[:, b].rearrange("p u e -> p (u e)"),
                                 dram.srcrow.rearrange("s e -> (s e)")[ds((2 * i + b) * GS * P, GS * P)]
                                 .partition_broadcast(P)).then_inc(srow_in[b], 16)
                passes(sp, half, group)

            @block.gpsimd
            def _(pool):
                nc.gpsimd.memset(lower[:], 1.0).then_inc(lower_made, 1)
                pool.wait_ge(lower_made, 1)
                nc.gpsimd.affine_select(out=lower[:], in_=lower[:], compare_op=ALU.is_ge, fill=0.0, base=-1,
                                        pattern=[[-1, P]], channel_multiplier=1).then_inc(lower_made, 1)

                def group(i, b, nxt):
                    hold(pool, index_ready[b], i + 1)
                    hold(pool, sums_ready[b], i + 1)
                    for u in range(GS):
                        if not (at_start(i) and b == 0):
                            hold(pool, added[u], 16 * (2 * i + b))
                        pool.indirect_dma_start(
                            out=dram.side[u], out_offset=bass.IndirectOffsetOnAxis(ap=index[:, b, u:u + 1], axis=0),
                            in_=sums[:, b, u, :], in_offset=None, compute_op=ALU.add).then_inc(added[u], 16)
                passes(pool, half, group)
                for u in range(GS):
                    pool.wait_ge(added[u], 16 * (NS // GS))

            @block.tensor
            def _(pe):
                windows = Numbers(pe, keep.window, NW, "e2_pe")

                def join(i, b):
                    pe.wait_ge(same_ready[b], i + 1)
                    if not at_start(i):
                        pe.wait_ge(joint_ready[b], i)
                    for u in range(GS):
                        t = pe.matmul(ps_j[:, b, u, :], collect[:, b, u, :], same[:, b, u, :], start=True, stop=True)
                    t.then_inc(joined[b], 1)

                def group(i, b, nxt):
                    if nxt:
                        join(*nxt)
                    ks = windows.load(2 * i + b)
                    pe.wait_ge(joint_ready[b], i + 1)
                    if not at_start(i):
                        pe.wait_ge(sums_ready[b], i)
                    for u in range(GS):
                        t = pe.matmul(ps_s[:, b, u, :], joint[:, b, u, :], hp[:, ds(ks[u] * D, D)], start=True, stop=True)
                    t.then_inc(summed[b], 1)

                join(0, 0)
                passes(pe, half, group)

            @block.scalar
            def _(act):
                def copy_joint(i, b):
                    act.wait_ge(joined[b], i + 1)
                    if not at_start(i):
                        act.wait_ge(summed[b], i)
                    nc.scalar.copy(joint[:, b], ps_j[:, b]).then_inc(joint_ready[b], 1)

                def group(i, b, nxt):
                    if nxt:
                        copy_joint(*nxt)
                    if not at_start(i):
                        for u in range(GS):
                            act.wait_ge(added[u], 16 * (2 * i + b - 1))
                    act.wait_ge(summed[b], i + 1)
                    nc.scalar.copy(sums[:, b], ps_s[:, b]).then_inc(sums_ready[b], 1)

                copy_joint(0, 0)
                passes(act, half, group)

            @block.vector
            def _(dve):
                ch = Chain(dve, v, 6)

                def group(i, b, nxt):
                    g = 2 * i + b
                    ch.start(g)
                    cols = ds(g * GS, GS)
                    dve.wait_ge(srow_in[b], 16 * (i + 1))
                    if not at_start(i):
                        dve.wait_ge(joined[b], i)
                    for u in range(GS):
                        nc.vector.tensor_scalar(collect[:, b, u, :], keep.iota_row[:], keep.dl[:, ds(g * GS + u, 1)],
                                                keep.ew[:, ds(g * GS + u, 1)], ALU.is_equal, ALU.mult)
                    nc.vector.tensor_tensor(same[:, b], srow[:, b], keep.srcf[:, cols].unsqueeze(2)
                                            .broadcast_to([P, GS, P]), ALU.is_equal).then_inc(same_ready[b], 1)
                    dve.wait_ge(same_ready[b], i + 1)
                    ch.link(nc.vector.tensor_tensor(earlier[:], same[:, b], lower[:].unsqueeze(1)
                                                    .broadcast_to([P, GS, P]), ALU.mult))
                    ch.link(nc.vector.tensor_reduce(cnt[:], earlier[:], AX, ALU.add))
                    ch.link(nc.vector.scalar_tensor_tensor(out=spare[:], in0=keep.srcf[:, cols], scalar=-1.0,
                                                           in1=ncol[:, 0:1].broadcast_to([P, GS]), op0=ALU.mult,
                                                           op1=ALU.add))
                    ch.link(nc.vector.scalar_tensor_tensor(out=spare[:], in0=cnt[:], scalar=1.0, in1=spare[:],
                                                           op0=ALU.min, op1=ALU.mult))
                    ch.link(nc.vector.tensor_tensor(dest[:], spare[:], keep.srcf[:, cols], ALU.add))
                    if not at_start(i):
                        for u in range(GS):
                            hold(dve, added[u], 16 * (g - 1))
                    ch.link(nc.vector.tensor_copy(index[:, b, :], dest[:]))
                    dve.sem_inc(index_ready[b], 1)

                    ch.end()
                nc.vector.tensor_scalar(ncol[:], keep.iota_col[:], float(NP), None, ALU.add)
                dve.wait_ge(lower_made, 2)
                passes(dve, half, group)


KQ = 3 * D


def mix_2(nc, keep, dram, ins, kvq):
    ctx = ExitStack()
    st = Stage(nc, ctx, "m2")
    HT = NW // 2
    with ctx:
        w01, wp, wq2 = st.sb("w01", [P, 2, D]), st.sb("wp", [P, 5 * D]), st.sb("wq2", [P, D])
        bias, cols = st.sb("bias", [P, 4 * D]), st.sb("cols", [P, 2])
        tab, side = st.sb("tab", [P, GS, 2, D]), st.sb("side", [P, 2, 2, D])
        sT, hT = st.sb("sT", [P, 4, P]), st.sb("hT", [P, 2, P])
        xt, h, hx = st.sb("xt", [P, 2, D]), st.sb("h", [P, 2, D]), st.sb("hx", [P, 2, D])
        h2 = st.sb("h2", [P, 2, D])
        q1, qT = st.sb("q1", [P, 2, D]), st.sb("qT", [P, 2, P])
        bt = st.sb("bt", [P, 2, 2 * D])
        stats, mv = st.sb("stats", [P, 2, 6]), st.sb("mv", [P, 2, 2])
        std, rstd = st.sb("std", [P, 2]), st.sb("rstd", [P, 2])
        ps_t, ps_o = st.ps("ps_t", [P, 4, P]), st.ps("ps_o", [P, 512])
        ps_p = st.ps("ps_p", [P, 2, 1024])
        ps_q = st.ps("ps_q", [P, 512])
        w_in, x_in, used = st.sem("w_in"), st.sem("x_in"), st.sem("used")
        side_ready, side_turned, sT_ready, mixed = st.sem("side_ready"), st.sem("side_turned"), st.sem("sT_ready"), st.sem("mixed")
        var_ready, std_ready, h_ready, h_turned = st.sem("var_ready"), st.sem("std_ready"), st.sem("h_ready"), st.sem("h_turned")
        hT_ready, projected, q1_ready, q1_turned = st.sem("hT_ready"), st.sem("projected"), st.sem("q1_ready"), st.sem("q1_turned")
        qT_ready, q_done, bt_ready, stored, v = st.sem("qT_ready"), st.sem("q_done"), st.sem("bt_ready"), st.sem("stored"), st.sem("v")
        dve_left = st.sem("dve_left")
        WL = [(w01[:], ins["L2_W"].rearrange("(c p) d -> p c d", p=P)), (wp[:], ins["L3_Wp"]), (wq2[:], ins["L3_gnn_hq_w2"]),
              (bias[:], ins["L3_brow"].partition_broadcast(P)), (cols[:], ins["L3_qcols"])]
        with nc.Block() as block:
            @block.sync
            def _(sp):
                for to, frm in WL:
                    sp.dma_start(to, frm).then_inc(w_in, 16)
                with sp.Fori(0, HT) as i:
                    sp.wait_ge(used, i + 1)
                    for u in range(GS):
                        sp.dma_start(tab[:, u], rows(dram.side[u], i)).then_inc(x_in, 16)
                    sp.dma_start(xt[:], rows(dram.x2, i)).then_inc(x_in, 16)
                    sp.dma_start(h2[:], rows(dram.h2, i)).then_inc(x_in, 16)

            @block.tensor
            def _(pe):
                pe.wait_ge(w_in, 16 * len(WL))
                with pe.Fori(0, HT) as i:
                    pe.wait_ge(side_ready, i + 1)
                    for j in range(4):
                        t = pe.transpose(ps_t[:, j, :], side[:, j // 2, j % 2, :], keep.ident[:])
                    t.then_inc(side_turned, 1)
                    pe.wait_ge(sT_ready, i + 1)
                    for u in range(2):
                        pe.matmul(ps_o[:, u * D:(u + 1) * D], sT[:, u, :], w01[:, 0, :], start=True, stop=False)
                        t = pe.matmul(ps_o[:, u * D:(u + 1) * D], sT[:, 2 + u, :], w01[:, 1, :], start=False, stop=True)
                    t.then_inc(mixed, 1)
                    pe.wait_ge(h_ready, i + 1)
                    for u in range(2):
                        t = pe.transpose(ps_t[:, u, :], h[:, u, :], keep.ident[:])
                    t.then_inc(h_turned, 1)
                    pe.wait_ge(hT_ready, i + 1)
                    for u in range(2):
                        pe.matmul(ps_p[:, u, 0:512], hT[:, u, :], wp[:, 0:512], start=True, stop=True)
                        t = pe.matmul(ps_p[:, u, 512:640], hT[:, u, :], wp[:, 512:640], start=True, stop=True)
                    t.then_inc(projected, 1)
                    pe.wait_ge(q1_ready, i + 1)
                    for u in range(2):
                        t = pe.transpose(ps_t[:, u, :], q1[:, u, :], keep.ident[:])
                    t.then_inc(q1_turned, 1)
                    pe.wait_ge(qT_ready, i + 1)
                    for u in range(2):
                        t = pe.matmul(ps_q[:, u * D:(u + 1) * D], qT[:, u, :], wq2[:], start=True, stop=True)
                    t.then_inc(q_done, 1)

            @block.scalar
            def _(act):
                act.wait_ge(w_in, 16 * len(WL))
                act.sem_inc(stored, 48)
                with act.Fori(0, HT) as i:
                    act.wait_ge(side_turned, i + 1)
                    nc.scalar.copy(sT[:], ps_t[:]).then_inc(sT_ready, 1)
                    act.wait_ge(var_ready, 2 * i + 1)
                    nc.scalar.activation(std[:], mv[:, :, 1], ACT.Sqrt, bias=keep.eps[:]).then_inc(std_ready, 1)
                    act.wait_ge(stored, 48 * (i + 1))
                    act.wait_ge(h_turned, i + 1)
                    nc.scalar.copy(hT[:], ps_t[:, 0:2, :]).then_inc(hT_ready, 1)
                    act.wait_ge(hT_ready, i + 1)
                    act.dma_start(dram.h3T[:, ds(i * 2 * P, 2 * P)].rearrange("f (w p) -> f w p", w=2), hT[:]
                                  ).then_inc(stored, 16)
                    act.wait_ge(dve_left, i + 1)
                    act.dma_start(rows(dram.hx, i), hx[:]).then_inc(stored, 16)
                    nc.scalar.copy(bt[:], ps_p[:, :, 2 * D:4 * D]).then_inc(bt_ready, 1)
                    act.wait_ge(bt_ready, i + 1)
                    act.dma_start(rows(dram.skv, i), bt[:]).then_inc(stored, 16)
                    act.wait_ge(var_ready, 2 * i + 2)
                    nc.scalar.activation(std[:], mv[:, :, 1], ACT.Sqrt, bias=keep.eps[:]).then_inc(std_ready, 1)
                    act.wait_ge(q1_turned, i + 1)
                    nc.scalar.activation(qT[:], ps_t[:, 0:2, :], ACT.Relu, bias=cols[:, 1:2], scale=cols[:, 0:1]
                                         ).then_inc(qT_ready, 1)
                act.wait_ge(stored, 48 * (HT + 1))

            @block.vector
            def _(dve):
                nc.vector.memset(kvq[:, NW * KQ:], 0.0)
                ch = Chain(dve, v, 22)
                dve.wait_ge(w_in, 16 * len(WL))
                dve.sem_inc(used, 1)
                with dve.Fori(0, HT) as i:
                    ch.start(i)
                    a = kvq[:, ds(i * 2 * KQ, 2 * KQ)].rearrange("p (w c) -> p w c", w=2)
                    dve.wait_ge(x_in, 16 * (GS + 2) * (i + 1))
                    ch.link(nc.vector.tensor_tensor(tab[:, 0:2], tab[:, 0:2], tab[:, 2:4], ALU.add))
                    ch.link(nc.vector.tensor_tensor(tab[:, 0], tab[:, 0], tab[:, 1], ALU.add))
                    for u in range(2):
                        ch.link(nc.vector.tensor_scalar(side[:, 0, u, :], tab[:, 0, u, :],
                                                        keep.dis[:, ds(2 * i + u, 1)], None, ALU.mult))
                    ch.link(nc.vector.tensor_tensor(side[:, 1], side[:, 0], h2[:], ALU.mult))
                    dve.sem_inc(side_ready, 1)
                    dve.wait_ge(mixed, i + 1)
                    ch.link(nc.vector.tensor_tensor(xt[:], xt[:], ps_o[:, 0:2 * D].rearrange("p (w d) -> p w d", w=2),
                                                    ALU.add), held=True)
                    layer_norm_statistics(nc, ch, xt, stats, mv, var_ready)
                    hold(dve, std_ready, 2 * i + 1)
                    layer_norm_apply(nc, ch, h, xt, mv, std, rstd)
                    dve.sem_inc(h_ready, 1)
                    dve.wait_ge(stored, 48 * (i + 1))
                    ch.link(nc.vector.tensor_tensor(hx[:], h[:], xt[:], ALU.add))
                    dve.sem_inc(used, 1)
                    dve.wait_ge(projected, i + 1)
                    ch.link(nc.vector.tensor_tensor(a[:, :, 0:2 * D], ps_p[:, :, 0:2 * D], bias[:, 0:2 * D].unsqueeze(1)
                                                    .broadcast_to([P, 2, 2 * D]), ALU.add))
                    ch.link(nc.vector.tensor_tensor(q1[:], ps_p[:, :, 4 * D:5 * D], bias[:, 2 * D:3 * D].unsqueeze(1)
                                                    .broadcast_to([P, 2, D]), ALU.add), held=True)
                    dve.sem_inc(dve_left, 1)
                    layer_norm_statistics(nc, ch, q1, stats, mv, var_ready)
                    hold(dve, std_ready, 2 * i + 2)
                    layer_norm_apply(nc, ch, q1, q1, mv, std, rstd, relu=False)
                    dve.sem_inc(q1_ready, 1)
                    dve.wait_ge(q_done, i + 1)
                    ch.link(nc.vector.tensor_tensor(q1[:], ps_q[:, 0:2 * D].rearrange("p (w d) -> p w d", w=2),
                                                    bias[:, 3 * D:4 * D].unsqueeze(1).broadcast_to([P, 2, D]), ALU.add))
                    ch.link(nc.vector.tensor_scalar(a[:, :, 2 * D:KQ], q1[:], float(DH3) ** -0.5, None, ALU.mult))
                    ch.end()


G3 = 2
LW = NH3 + 1


def edges_3(nc, keep, dram, ins, kvq):
    ctx = ExitStack()
    st = Stage(nc, ctx, "e3")
    QC = 3 * D
    with ctx:
        B = range(2)
        wa, w2 = st.sb("wa", [P, 2 * D + 1]), st.sb("w2", [P, 2, D])
        cols, bias = st.sb("cols", [P, 4]), st.sb("bias", [P, 2 * D])
        dlr = st.sb("dlr", [P, 2, G3 * P], BF16)
        spread = st.sb("spread", [P, 2, G3 * P])
        attr = st.sb("attr", [P, 2, G3, P])
        gidx = st.sb("gidx", [P, 2, G3], I32)
        skv = st.sb("skv", [P, 2, G3, 2 * D])
        xs, xn = st.sb("xs", [P, G3, 2 * D]), st.sb("xn", [P, G3, 2 * D])
        stats, mv = st.sb("stats", [P, 2 * G3, 6]), st.sb("mv", [P, 2 * G3, 2])
        std, rstd = st.sb("std", [P, 2 * G3]), st.sb("rstd", [P, 2 * G3])
        hT = st.sb("hT", [P, 2, G3, P])
        kvo = st.sb("kvo", [P, 2, G3, 2 * D])
        prod = st.sb("prod", [P, G3, D])
        lg = st.sb("lg", [P, 2, G3, LW])
        ps_h = st.ps("ps_h", [P, 2, G3, 512])
        ps_t = st.ps("ps_t", [P, 2, 2, G3, P])
        ps_o = st.ps("ps_o", [P, 2, G3, 2 * D])
        w_in = st.sem("w_in")
        dlr_in, attr_in = [st.sem(f"dlr_in{b}") for b in B], [st.sem(f"attr_in{b}") for b in B]
        skv_in, idx_ready = [st.gather_sem(f"skv_in{b}") for b in B], st.sem("idx_ready")
        spread_ready, hidden = [st.sem(f"spread_ready{b}") for b in B], [st.sem(f"hidden{b}") for b in B]
        xs_ready, stats_ready = st.sem("xs_ready"), st.sem("stats_ready")
        var_ready, std_ready, rstd_ready = st.sem("var_ready"), st.sem("std_ready"), st.sem("rstd_ready")
        xn_ready, turned, hT_ready = st.sem("xn_ready"), [st.sem(f"turned{b}") for b in B], st.sem("hT_ready")
        product2, kvo_ready = [st.sem(f"product2{b}") for b in B], [st.sem(f"kvo_ready{b}") for b in B]
        prod_ready, lg_ready = [st.sem(f"prod_ready{b}") for b in B], [st.sem(f"lg_ready{b}") for b in B]
        stored = [st.sem(f"stored{b}") for b in B]
        half = NS // G3 // 2
        WL = [(wa[0:KA, :], ins["L3_Wa"]), (w2[:], ins["L3_W2"].rearrange("(c p) d -> p c d", p=P)),
              (cols[:], ins["L3_kvcols"]), (bias[:], ins["L3_kvrow"].partition_broadcast(P))]

        def before(i, b):
            return i + b

        with nc.Block() as block:
            @block.sync
            def _(sp):
                for to, frm in WL:
                    sp.dma_start(to, frm).then_inc(w_in, 16)
                tiles = Numbers(sp, dram.tk[0:1, :], NT - 1, "e3_sp", G3)

                def load(i, b):
                    g = 2 * i + b
                    ts = tiles.load(g)
                    if not at_start(i):
                        sp.wait_ge(spread_ready[b], i)
                        sp.wait_ge(hidden[b], i)
                    sp.dma_start(dlr[:, b, :], dram.dlrow.rearrange("s e -> (s e)")[ds(g * G3 * P, G3 * P)]
                                 .partition_broadcast(P)).then_inc(dlr_in[b], 16)
                    for u in range(G3):
                        sp.dma_start(attr[0:KA, b, u, :], ins["attr"][:, ds(ts[u] * P, P)]).then_inc(attr_in[b], 16)

                def store(i, b):
                    g = 2 * i + b
                    sp.wait_ge(lg_ready[b], i + 1)
                    sp.dma_start(dram.lg[ds(g * G3 * P, G3 * P), :].rearrange("(u p) c -> p u c", p=P), lg[:, b]
                                 ).then_inc(stored[b], 16)
                    sp.dma_start(dram.v[ds(g * G3 * P, G3 * P), :].rearrange("(u p) c -> p u c", p=P),
                                 kvo[:, b, :, D:2 * D]).then_inc(stored[b], 16)

                def group(i, b, nxt):
                    if nxt:
                        load(*nxt)
                    if b == 1:
                        store(i, 0)
                    elif not at_start(i):
                        store(i - 1, 1)
                load(0, 0)
                passes(sp, half, group)
                store(half - 1, 1)
                for b in B:
                    sp.wait_ge(stored[b], 32 * half)

            @block.gpsimd
            def _(pool):
                def group(i, b, nxt):
                    if not (at_start(i) and b == 0):
                        hold(pool, xs_ready, 2 * i + b)
                    nc.gpsimd.tensor_copy(gidx[:, b, :], keep.src[:, ds((2 * i + b) * G3, G3)]).then_inc(idx_ready, 1)
                    hold(pool, idx_ready, 2 * i + b + 1)
                    for u in range(G3):
                        pool.indirect_dma_start(
                            out=skv[:, b, u, :], out_offset=None, in_=dram.skv,
                            in_offset=bass.IndirectOffsetOnAxis(ap=gidx[:, b, u:u + 1], axis=0)).then_inc(skv_in[b], 16)
                passes(pool, half, group)

            @block.tensor
            def _(pe):
                windows = Numbers(pe, keep.window, NW, "e3_pe", G3)
                pe.wait_ge(w_in, 16 * len(WL))

                def first_product(i, b):
                    ks = windows.load(2 * i + b)
                    pe.wait_ge(spread_ready[b], i + 1)
                    pe.wait_ge(attr_in[b], 16 * G3 * (i + 1))
                    if not at_start(i):
                        pe.wait_ge(prod_ready[b], i)
                    for u in range(G3):
                        sp_u = spread[:, b, u * P:(u + 1) * P]
                        pe.matmul(ps_h[:, b, u, QC:QC + D], sp_u, kvq[:, ds(ks[u] * KQ + 2 * D, D)], start=True, stop=True)
                        pe.matmul(ps_h[:, b, u, 0:2 * D + 1], attr[0:KA, b, u, :], wa[0:KA, :], start=True, stop=False,
                                  skip_group_check=True)
                        t = pe.matmul(ps_h[:, b, u, 0:2 * D], sp_u, kvq[:, ds(ks[u] * KQ, 2 * D)], start=False,
                                      stop=True, skip_group_check=True)
                    t.then_inc(hidden[b], 1)

                def group(i, b, nxt):
                    g = 2 * i + b
                    if nxt:
                        first_product(*nxt)
                    pe.wait_ge(xn_ready, g + 1)
                    for c in range(2):
                        for u in range(G3):
                            t = pe.transpose(ps_t[:, b, c, u, :], xn[:, u, c * D:(c + 1) * D], keep.ident[:])
                    t.then_inc(turned[b], 1)
                    pe.wait_ge(hT_ready, g + 1)
                    if not at_start(i):
                        pe.wait_ge(kvo_ready[b], i)
                    for u in range(G3):
                        for c in range(2):
                            t = pe.matmul(ps_o[:, b, u, c * D:(c + 1) * D], hT[:, c, u, :], w2[:, c, :], start=True,
                                          stop=True)
                    t.then_inc(product2[b], 1)

                first_product(0, 0)
                passes(pe, half, group)

            @block.scalar
            def _(act):
                act.wait_ge(w_in, 16 * len(WL))

                def group(i, b, nxt):
                    g = 2 * i + b
                    act.wait_ge(var_ready, g + 1)
                    nc.scalar.activation(std[:], mv[:, :, 1], ACT.Sqrt, bias=keep.eps[:]).then_inc(std_ready, 1)
                    act.wait_ge(turned[b], i + 1)
                    if not (at_start(i) and b == 0):
                        act.wait_ge(product2[1 - b], before(i, b))
                    for c in range(2):
                        t = nc.scalar.activation(hT[:, c], ps_t[:, b, c], ACT.Relu, bias=cols[:, 2 * c + 1:2 * c + 2],
                                                 scale=cols[:, 2 * c:2 * c + 1])
                    t.then_inc(hT_ready, 1)
                passes(act, half, group)

            @block.vector
            def _(dve):
                dve.wait_ge(w_in, 16 * len(WL))

                def make_spread(i, b):
                    dve.wait_ge(dlr_in[b], 16 * (i + 1))
                    if not at_start(i):
                        dve.wait_ge(hidden[b], i)
                    nc.vector.tensor_scalar(spread[:, b, :], dlr[:, b, :], keep.iota_col[:, 0:1], None,
                                            ALU.is_equal).then_inc(spread_ready[b], 1)

                def finish(i, b):
                    dve.wait_ge(product2[b], i + 1)
                    if not at_start(i):
                        dve.wait_ge(stored[b], 32 * i)
                    nc.vector.tensor_tensor(kvo[:, b], ps_o[:, b], bias[:].unsqueeze(1).broadcast_to([P, G3, 2 * D]),
                                            ALU.add).then_inc(kvo_ready[b], 1)
                    dve.wait_ge(kvo_ready[b], i + 1)
                    if not (at_start(i) and b == 0):
                        dve.wait_ge(lg_ready[1 - b], before(i, b))
                    nc.vector.tensor_copy(lg[:, b, :, NH3:LW], ps_h[:, b, :, 2 * D:2 * D + 1])
                    nc.vector.tensor_tensor(prod[:], kvo[:, b, :, 0:D], ps_h[:, b, :, QC:QC + D],
                                            ALU.mult).then_inc(prod_ready[b], 1)
                    dve.wait_ge(prod_ready[b], i + 1)
                    nc.vector.tensor_reduce(lg[:, b, :, 0:NH3], prod[:].rearrange("p u (h e) -> p u h e", e=DH3),
                                            AX, ALU.add).then_inc(lg_ready[b], 1)

                def group(i, b, nxt):
                    g = 2 * i + b
                    if nxt:
                        make_spread(*nxt)
                    dve.wait_ge(hidden[b], i + 1)
                    dve.wait_ge(skv_in[b], 16 * G3 * (i + 1))
                    if not (at_start(i) and b == 0):
                        dve.wait_ge(xn_ready, g)
                    nc.vector.tensor_tensor(xs[:], skv[:, b], ps_h[:, b, :, 0:2 * D], ALU.add).then_inc(xs_ready, 1)
                    hold(dve, xs_ready, g + 1)
                    for j in range(2 * G3):
                        t = nc.vector.bn_stats(stats[:, j, :], xs[:, j // 2, (j % 2) * D:(j % 2 + 1) * D])
                    t.then_inc(stats_ready, 1)
                    hold(dve, stats_ready, g + 1)
                    for j in range(2 * G3):
                        t = nc.vector.bn_aggr(mv[:, j, :], stats[:, j, :])
                    t.then_inc(var_ready, 1)
                    if b == 1:
                        finish(i, 0)
                    elif not at_start(i):
                        finish(i - 1, 1)
                    dve.wait_ge(std_ready, g + 1)
                    nc.vector.reciprocal(rstd[:], std[:]).then_inc(rstd_ready, 1)
                    dve.wait_ge(rstd_ready, g + 1)
                    if not (at_start(i) and b == 0):
                        dve.wait_ge(turned[1 - b], before(i, b))
                    for j in range(2 * G3):
                        t = nc.vector.tensor_scalar(xn[:, j // 2, (j % 2) * D:(j % 2 + 1) * D],
                                                    xs[:, j // 2, (j % 2) * D:(j % 2 + 1) * D],
                                                    mv[:, j, 0:1], rstd[:, j:j + 1], ALU.subtract, ALU.mult)
                    t.then_inc(xn_ready, 1)

                make_spread(0, 0)
                passes(dve, half, group)
                finish(half - 1, 1)


def softmax_3(nc, keep, dram, ins):
    ctx = ExitStack()
    st = Stage(nc, ctx, "sm")
    HH = NH3 // 2
    with ctx:
        L = st.sb("L", [P, NS, LW])
        M = st.sb("M", [P, NS * HH])
        wall = st.sb("wall", [P, NS + 1])
        edge, edgeT = st.sb("edge", [P, 2, HH]), st.sb("edgeT", [HH, 2, P])
        run, carry = st.sb("run", [HH, P + 1]), st.sb("carry", [P, HH])
        gate = st.sb("gate", [P, 1])
        ps_e, ps_c = st.ps("ps_e", [P, 512]), st.ps("ps_c", [P, 512])
        loaded, v = st.sem("loaded"), st.sem("v")
        cur_used, prev_in = st.sem("cur_used"), st.sem("prev_in")
        edges_ready, edges_turned, run_ready, carry_turned = (st.sem("edges_ready"), st.sem("edges_turned"),
                                                              st.sem("run_ready"), st.sem("carry_turned"))
        shifted, exped, gated, stored = st.sem("shifted"), st.sem("exped"), st.sem("gated"), st.sem("stored")
        l_in = st.sem("l_in")

        def halo(flat, off):
            return bass.AP(tensor=flat.tensor, offset=flat.offset + off, ap=[[NS, P], [1, NS + 1]])

        dstf = dram.dstflat
        dlf = dram.dlflat.rearrange("s e -> (s e)")
        cur = M[:, 0:NS + 1]
        prv = M[:, 2 * NS:3 * NS + 1]
        out_of = M[:, 4 * NS:5 * NS + 1]
        with nc.Block() as block:
            @block.sync
            def _(sp):
                sp.dma_start(out_of, halo(dlf, 0)).then_inc(loaded, 16)
                sp.dma_start(cur, halo(dstf, 1)).then_inc(loaded, 16)
                sp.dma_start(prv, halo(dstf, 0)).then_inc(loaded, 16)
                sp.dma_start(gate[:], ins["L3_gnn_ew_b"].partition_broadcast(P)).then_inc(loaded, 16)
                sp.dma_start(L[:], dram.lg.rearrange("(p e) c -> p e c", p=P)).then_inc(l_in, 16)
                sp.wait_ge(exped, 1)
                sp.wait_ge(gated, 1)
                sp.dma_start(dram.lg.rearrange("(p e) c -> p e c", p=P), L[:]).then_inc(stored, 16)
                sp.wait_ge(stored, 16)

            @block.scalar
            def _(act):
                act.wait_ge(loaded, 64)
                act.wait_ge(l_in, 16)
                nc.scalar.activation(L[:, :, NH3], L[:, :, NH3], ACT.Sigmoid, bias=gate[:]).then_inc(gated, 1)
                act.wait_ge(shifted, 2)
                nc.scalar.activation(L[:, :, 0:NH3], L[:, :, 0:NH3], ACT.Exp).then_inc(exped, 1)

            @block.tensor
            def _(pe):
                for n in range(4):
                    pe.wait_ge(edges_ready, n + 1)
                    for j in range(2):
                        t = pe.transpose(ps_e[0:HH, j * P:(j + 1) * P], edge[:, j, :], keep.ident[:])
                    t.then_inc(edges_turned, 1)
                    pe.wait_ge(run_ready, n + 1)
                    back = run[:, 0:P] if n % 2 == 0 else run[:, 1:P + 1]
                    pe.transpose(ps_c[:, 0:HH], back, keep.ident[0:HH, 0:HH]).then_inc(carry_turned, 1)

            @block.vector
            def _(dve):
                n = [0]

                def link(ins_):
                    n[0] += 1
                    ins_.then_inc(v, 1)
                    dve.wait_ge(v, n[0])

                dve.wait_ge(loaded, 64)
                link(nc.vector.tensor_scalar(wall[:], out_of, 0.0, None, ALU.is_ge))
                link(nc.vector.tensor_scalar(out_of, out_of, float(P - 1), None, ALU.is_le))
                link(nc.vector.tensor_tensor(out_of, out_of, wall[:], ALU.mult))
                link(nc.vector.tensor_tensor(wall[:], cur, prv, ALU.not_equal))
                link(nc.vector.tensor_tensor(wall[:], wall[:], out_of, ALU.mult))
                link(nc.vector.tensor_scalar(wall[:], wall[:], -BIG, None, ALU.mult))
                link(nc.vector.tensor_scalar(out_of, out_of, -1.0, BIG, ALU.add, ALU.mult))
                dve.wait_ge(l_in, 16)
                link(nc.vector.tensor_tensor(L[:, :, 0:NH3], L[:, :, 0:NH3],
                                             out_of[:, 0:NS].unsqueeze(2).broadcast_to([P, NS, NH3]), ALU.add))
                turn = [0]

                def cross(reverse, mh):
                    end = 0 if reverse else NS - 1
                    link(nc.vector.tensor_copy(edge[:, 0, :], mh[:, end, :]))
                    walls = wall[:, 1:NS + 1] if reverse else wall[:, 0:NS]
                    link(nc.vector.tensor_reduce(edge[:, 1, 0:1], walls, AX, ALU.min))
                    nc.vector.tensor_copy(edge[:, 1, 1:HH], edge[:, 1, 0:1].broadcast_to([P, HH - 1])
                                          ).then_inc(edges_ready, 1)
                    turn[0] += 1
                    dve.wait_ge(edges_turned, turn[0])
                    link(nc.vector.tensor_copy(edgeT[:], ps_e[0:HH, 0:2 * P].rearrange("p (j e) -> p j e", j=2)))
                    link(nc.vector.memset(run[:], -BIG))
                    if reverse:
                        t = nc.vector.tensor_tensor_scan(run[:, 0:P][:, ::-1], edgeT[:, 1, ::-1], edgeT[:, 0, ::-1],
                                                         -BIG, ALU.add, ALU.max)
                    else:
                        t = nc.vector.tensor_tensor_scan(run[:, 1:P + 1], edgeT[:, 1, :], edgeT[:, 0, :], -BIG,
                                                         ALU.add, ALU.max)
                    t.then_inc(run_ready, 1)
                    dve.wait_ge(carry_turned, turn[0])
                    link(nc.vector.tensor_copy(carry[:], ps_c[:, 0:HH]))

                for half in range(2):
                    mh = M[:].rearrange("p (e h) -> p e h", h=HH)
                    lh = L[:, :, half * HH:(half + 1) * HH]

                    def forward(initial):
                        for h in range(HH):
                            link(nc.vector.tensor_tensor_scan(mh[:, :, h], wall[:, 0:NS], lh[:, :, h], initial(h),
                                                              ALU.add, ALU.max))

                    def backward(initial):
                        for h in range(HH):
                            link(nc.vector.tensor_tensor_scan(mh[:, ::-1, h], wall[:, 1:NS + 1][:, ::-1],
                                                              mh[:, ::-1, h], initial(h), ALU.add, ALU.max))

                    forward(lambda h: -BIG)
                    cross(False, mh)
                    forward(lambda h: carry[:, h:h + 1])
                    backward(lambda h: -BIG)
                    cross(True, mh)
                    backward(lambda h: carry[:, h:h + 1])
                    link(nc.vector.tensor_tensor(lh, lh, mh, ALU.subtract))
                    dve.sem_inc(shifted, 1)


def edges_3_sums(nc, keep, dram, nodes):
    ctx = ExitStack()
    st = Stage(nc, ctx, "s3")
    with ctx:
        B = range(2)
        collect = st.sb("collect", [P, 2, GS, P])
        vin, lin = st.sb("vin", [P, 2, GS, D]), st.sb("lin", [P, 2, GS, LW])
        wgt = st.sb("wgt", [P, GS, NH3])
        vals = st.sb("vals", [P, 2, GS, AC3])
        ps_a = st.ps("ps_a", [P, 2, GS, 256])
        v_in = [st.sem(f"v_in{b}") for b in B]
        wgt_ready, vals_ready = st.sem("wgt_ready"), [st.sem(f"vals_ready{b}") for b in B]
        summed, added = [st.sem(f"summed{b}") for b in B], st.sem("added")
        half = NS // GS // 2
        with nc.Block() as block:
            @block.sync
            def _(sp):
                def group(i, b, nxt):
                    if not at_start(i):
                        sp.wait_ge(vals_ready[b], i)
                    sl = ds((2 * i + b) * GS * P, GS * P)
                    sp.dma_start(vin[:, b], dram.v[sl, :].rearrange("(u p) c -> p u c", p=P)).then_inc(v_in[b], 16)
                    sp.dma_start(lin[:, b], dram.lg[sl, :].rearrange("(u p) c -> p u c", p=P)).then_inc(v_in[b], 16)
                passes(sp, half, group)

            @block.tensor
            def _(pe):
                def group(i, b, nxt):
                    pe.wait_ge(vals_ready[b], i + 1)
                    if not at_start(i):
                        pe.wait_ge(added, (2 * i + b - 1) * GS + 1)
                    for u in range(GS):
                        t = pe.matmul(ps_a[:, b, u, 0:AC3], collect[:, b, u, :], vals[:, b, u, :], start=True, stop=True)
                    t.then_inc(summed[b], 1)
                passes(pe, half, group)

            @block.vector
            def _(dve):
                windows = Numbers(dve, keep.window, NW, "s3_dve")

                def add_sums(i, b):
                    ks = windows.load(2 * i + b)
                    dve.wait_ge(summed[b], i + 1)
                    for u in range(GS):
                        a = nodes[:, ds(ks[u] * AC3, AC3)]
                        dve.wait_ge(added, (2 * i + b) * GS + u + 1)
                        nc.vector.tensor_tensor(a, a, ps_a[:, b, u, 0:AC3], ALU.add).then_inc(added, 1)

                def group(i, b, nxt):
                    g = 2 * i + b
                    dve.wait_ge(v_in[b], 32 * (i + 1))
                    if not (at_start(i) and b == 0):
                        dve.wait_ge(vals_ready[1 - b], i + b)
                    nc.vector.tensor_tensor(wgt[:], lin[:, b, :, 0:NH3], lin[:, b, :, NH3:LW]
                                            .broadcast_to([P, GS, NH3]), ALU.mult).then_inc(wgt_ready, 1)
                    if not at_start(i):
                        dve.wait_ge(summed[b], i)
                    nc.vector.tensor_tensor(
                        collect[:, b], keep.iota_row[:].unsqueeze(1).broadcast_to([P, GS, P]),
                        keep.dl[:, ds(g * GS, GS)].unsqueeze(2).broadcast_to([P, GS, P]), ALU.is_equal)
                    nc.vector.tensor_copy(vals[:, b, :, D:AC3], lin[:, b, :, 0:NH3])
                    dve.wait_ge(wgt_ready, g + 1)
                    nc.vector.tensor_tensor(
                        vals[:, b, :, 0:D].rearrange("p u (h e) -> p u h e", e=DH3),
                        vin[:, b].rearrange("p u (h e) -> p u h e", e=DH3),
                        wgt[:].unsqueeze(3).broadcast_to([P, GS, NH3, DH3]), ALU.mult).then_inc(vals_ready[b], 1)
                    if b == 1:
                        add_sums(i, 0)
                    elif not at_start(i):
                        add_sums(i - 1, 1)

                nc.vector.memset(nodes[:], 0.0).then_inc(added, 1)
                passes(dve, half, group)
                add_sums(half - 1, 1)


def mix_3(nc, keep, dram, ins, nodes, out):
    ctx = ExitStack()
    st = Stage(nc, ctx, "m3")
    HT = NW // 2
    with ctx:
        w1, w2 = st.sb("w1", [P, 2, D]), st.sb("w2", [P, D])
        bias, cols = st.sb("bias", [P, 2 * D]), st.sb("cols", [P, 2])
        den, rec = st.sb("den", [P, 2, NH3]), st.sb("rec", [P, 2, NH3])
        at, aT, hT = st.sb("at", [P, 2, D]), st.sb("aT", [P, 2, P]), st.sb("hT", [P, 2, 2, P])
        hx, y, yT = st.sb("hx", [P, 2, 2, D]), st.sb("y", [P, 2, D]), st.sb("yT", [P, 2, P])
        stats, mv = st.sb("stats", [P, 2, 6]), st.sb("mv", [P, 2, 2])
        std, rstd = st.sb("std", [P, 2]), st.sb("rstd", [P, 2])
        ps_t, ps_o, ps_u = st.ps("ps_t", [P, 4, P]), st.ps("ps_o", [P, 512]), st.ps("ps_u", [P, 512])
        w_in, in_, used, at_ready, at_turned = st.sem("w_in"), st.sem("in"), st.sem("used"), st.sem("at_ready"), st.sem("at_turned")
        aT_ready, hidden, var_ready, std_ready = st.sem("aT_ready"), st.sem("hidden"), st.sem("var_ready"), st.sem("std_ready")
        y_ready, y_turned, yT_ready, done, v = st.sem("y_ready"), st.sem("y_turned"), st.sem("yT_ready"), st.sem("done"), st.sem("v")
        out_ready, stored = st.sem("out_ready"), st.sem("stored")
        WL = [(w1[:], ins["L3_gnn_no_w1"].rearrange("(c p) d -> p c d", p=P)), (w2[:], ins["L3_gnn_no_w2"]),
              (bias[:], ins["L3_norow"].partition_broadcast(P)), (cols[:], ins["L3_nocols"])]
        with nc.Block() as block:
            @block.sync
            def _(sp):
                for to, frm in WL:
                    sp.dma_start(to, frm).then_inc(w_in, 16)
                with sp.Fori(0, HT) as i:
                    sp.wait_ge(used, i + 1)
                    sp.dma_start(hT[:, 0], dram.h3T[:, ds(i * 2 * P, 2 * P)].rearrange("f (w p) -> f w p", w=2)
                                 ).then_inc(in_, 16)
                    sp.dma_start(hx[:, 0], rows(dram.hx, i)).then_inc(in_, 16)

            @block.tensor
            def _(pe):
                pe.wait_ge(w_in, 16 * len(WL))
                with pe.Fori(0, HT) as i:
                    pe.wait_ge(at_ready, i + 1)
                    for u in range(2):
                        t = pe.transpose(ps_t[:, u, :], at[:, u, :], keep.ident[:])
                    t.then_inc(at_turned, 1)
                    pe.wait_ge(aT_ready, i + 1)
                    pe.wait_ge(in_, 32 * (i + 1))
                    for u in range(2):
                        pe.matmul(ps_o[:, u * D:(u + 1) * D], aT[:, u, :], w1[:, 0, :], start=True, stop=False)
                        t = pe.matmul(ps_o[:, u * D:(u + 1) * D], hT[:, 0, u, :], w1[:, 1, :], start=False, stop=True)
                    t.then_inc(hidden, 1)
                    pe.wait_ge(y_ready, i + 1)
                    for u in range(2):
                        t = pe.transpose(ps_t[:, 2 + u, :], y[:, u, :], keep.ident[:])
                    t.then_inc(y_turned, 1)
                    pe.wait_ge(yT_ready, i + 1)
                    for u in range(2):
                        t = pe.matmul(ps_u[:, u * D:(u + 1) * D], yT[:, u, :], w2[:], start=True, stop=True)
                    t.then_inc(done, 1)

            @block.scalar
            def _(act):
                act.wait_ge(w_in, 16 * len(WL))
                act.sem_inc(stored, 16)
                with act.Fori(0, HT) as i:
                    act.wait_ge(at_turned, i + 1)
                    nc.scalar.copy(aT[:], ps_t[:, 0:2]).then_inc(aT_ready, 1)
                    act.wait_ge(var_ready, i + 1)
                    nc.scalar.activation(std[:], mv[:, :, 1], ACT.Sqrt, bias=keep.eps[:]).then_inc(std_ready, 1)
                    act.wait_ge(y_turned, i + 1)
                    nc.scalar.activation(yT[:], ps_t[:, 2:4], ACT.Relu, bias=cols[:, 1:2], scale=cols[:, 0:1]
                                         ).then_inc(yT_ready, 1)
                    act.wait_ge(out_ready, i + 1)
                    act.dma_start(rows(out, i), hx[:, 1]).then_inc(stored, 16)
                act.wait_ge(stored, 16 * (HT + 1))

            @block.vector
            def _(dve):
                ch = Chain(dve, v, 2 + 1 + 2 + 3 + 2)
                dve.wait_ge(w_in, 16 * len(WL))
                dve.sem_inc(used, 1)
                with dve.Fori(0, HT) as i:
                    ch.start(i)
                    w = nodes[:, ds(i * 2 * AC3, 2 * AC3)].rearrange("p (w c) -> p w c", w=2)
                    ch.link(nc.vector.tensor_scalar(den[:], w[:, :, D:AC3], 1e-30, None, ALU.max))
                    ch.link(nc.vector.reciprocal(rec[:], den[:]))
                    nc.vector.tensor_tensor(at[:].rearrange("p w (h e) -> p w h e", e=DH3),
                                            w[:, :, 0:D].rearrange("p w (h e) -> p w h e", e=DH3),
                                            rec[:].unsqueeze(3).broadcast_to([P, 2, NH3, DH3]),
                                            ALU.mult).then_inc(at_ready, 1)
                    dve.wait_ge(hidden, i + 1)
                    ch.link(nc.vector.tensor_tensor(y[:], ps_o[:, 0:2 * D].rearrange("p (w d) -> p w d", w=2),
                                                    bias[:, 0:D].unsqueeze(1).broadcast_to([P, 2, D]), ALU.add), held=True)
                    layer_norm_statistics(nc, ch, y, stats, mv, var_ready)
                    hold(dve, std_ready, i + 1)
                    layer_norm_apply(nc, ch, y, y, mv, std, rstd, relu=False)
                    dve.sem_inc(y_ready, 1)
                    dve.wait_ge(done, i + 1)
                    dve.wait_ge(stored, 16 * (i + 1))
                    ch.link(nc.vector.tensor_tensor(hx[:, 1], hx[:, 0], bias[:, D:2 * D].unsqueeze(1)
                                                    .broadcast_to([P, 2, D]), ALU.add))
                    ch.link(nc.vector.tensor_tensor(hx[:, 1], hx[:, 1], ps_u[:, 0:2 * D]
                                                    .rearrange("p (w d) -> p w d", w=2), ALU.add))
                    dve.sem_inc(out_ready, 1)
                    dve.sem_inc(used, 1)
                    ch.end()


class Dram:
    pass


def build(nc, ins, out):
    with ExitStack() as ctx:
        dram = Dram()

        def scratch(name, shape, dt=F32):
            return nc.dram_tensor(f"scratch_{name}", shape, dt, kind="Internal").ap()

        dram.plan, dram.tk = scratch("plan", [2, NT]), scratch("tk", [2, NSP], I32)
        dram.dlrow, dram.srcrow = scratch("dlrow", [NSP, P], BF16), scratch("srcrow", [NSP, P])
        dram.dlflat, dram.dstflat = scratch("dlflat", [NSP, P]), scratch("dstflat", [NSP * P + P])
        dram.hT, dram.kv = scratch("hT", [P, NP]), scratch("kv", [NP, 2 * D])
        dram.x1, dram.hw = scratch("x1", [NP, D]), scratch("hw", [NP * RT, D])
        dram.x2, dram.h2 = scratch("x2", [NP, D]), scratch("h2", [NP, D])
        dram.side = [scratch(f"side{u}", [NP + P, D]) for u in range(GS)]
        dram.h3T, dram.hx, dram.skv = scratch("h3T", [P, NP]), scratch("hx", [NP, D]), scratch("skv", [NP, 2 * D])
        dram.lg, dram.v = scratch("lg", [NS * P, LW]), scratch("v", [NS * P, D])

        keep = Stage(nc, ctx, "keep")
        keep.dl, keep.src = keep.sb("dl", [P, NSP]), keep.sb("src", [P, NSP], I32)
        keep.window, keep.dis = keep.sb("window", [P, NSP], I32), keep.sb("dis", [P, NW + 1])
        constants(nc, keep)
        with ExitStack() as c:
            cols = Stage(nc, c, "cols")
            keep.et, keep.ew = cols.sb("et", [P, NSP]), cols.sb("ew", [P, NSP])
            keep.srcf, keep.srct = cols.sb("srcf", [P, NSP]), cols.sb("srct", [P, NSP], I32)
            clear_tables(nc, dram)
            plan_slots(nc, keep, dram, ins["src"], ins["dst"], ins["edge_type_16"], ins["edge_weight"])
            nodes = cols.sb("nodes", [P, (NW + 1) * AC0])
            with ExitStack() as c0:
                q = Stage(nc, c0, "l0").sb("q", [P, (NW + 1) * D])
                project_qkv(nc, keep, dram, ins["x"], ins["L0_gnn_Wqkv"], q)
                edges_0(nc, keep, dram, q, nodes)
            mix_0(nc, keep, dram, ins, nodes)
            edges_1(nc, keep, dram, nodes)
            with ExitStack() as c2:
                hp = Stage(nc, c2, "l2").sb("hp", [P, (NW + 1) * D])
                mix_1(nc, keep, dram, nodes, hp)
                edges_2(nc, keep, dram, hp)
        with ExitStack() as c:
            kvq = Stage(nc, c, "l3").sb("kvq", [P, (NW + 1) * KQ])
            mix_2(nc, keep, dram, ins, kvq)
            edges_3(nc, keep, dram, ins, kvq)
        softmax_3(nc, keep, dram, ins)
        with ExitStack() as c:
            nodes = Stage(nc, c, "l3s").sb("nodes", [P, (NW + 1) * AC3])
            edges_3_sums(nc, keep, dram, nodes)
            mix_3(nc, keep, dram, ins, nodes, out)


def kernel(**inputs):
    import numpy as np
    import concourse.bacc as _bacc
    from concourse.bass_utils import run_bass_kernel_spmd as _run

    a = {k: np.asarray(v) for k, v in inputs.items()}
    lay = {}
    lay["x"] = np.pad(a["x"], ((0, NP - N), (0, 0)))
    lay["src"] = np.pad(a["src"], (0, EP - E))
    lay["dst"] = np.pad(a["dst"], (0, EP - E), constant_values=NP - 1)
    lay["edge_type_16"] = np.pad(a["edge_type_16"], (0, EP - E))
    lay["edge_weight"] = np.pad(a["edge_weight"], (0, EP - E))
    lay["L0_gnn_Wqkv"] = np.concatenate([a["L0_gnn_Wq"].T, a["L0_gnn_Wk"].T, a["L0_gnn_Wv"].T], axis=1)
    lay["L0_gnn_Wo"] = a["L0_gnn_Wo"].T
    lay["L0_gnn_W1"] = a["L0_gnn_W1"].T
    lay["L0_gnn_W2"] = a["L0_gnn_W2"].T
    lay["L0_cols"] = np.stack([a["L0_gnn_bo"], a["L0_gnn_b1"][:D], a["L0_gnn_b1"][D:], a["L0_gnn_bn1_w"], a["L0_gnn_bn1_b"],
                               a["L0_gnn_b2"], a["L0_gnn_bn2_w"], a["L0_gnn_bn2_b"]], axis=1)
    lay["L1_W"] = np.concatenate([a["L1_gnn_W_edge"], a["L1_gnn_W_node"]]).transpose(1, 0, 2).reshape(D, -1)
    lay["L1_b"] = np.concatenate([a["L1_gnn_b_edge"], a["L1_gnn_b_node"]])
    lay["node_type_8"] = np.pad(a["node_type_8"], (0, NP - N)).reshape(NW, P).T
    lay["L2_W"] = np.concatenate([a["L2_gnn_W0"].T, a["L2_gnn_W1"].T])
    hk, hv = a["L3_gnn_hk_w1"], a["L3_gnn_hv_w1"]
    dd, ss = slice(KA, KA + D), slice(KA + D, KA + 2 * D)
    lay["L3_Wp"] = np.concatenate([hk[dd], hv[dd], hk[ss], hv[ss], a["L3_gnn_hq_w1"]], axis=1)
    lay["L3_gnn_hq_w2"] = a["L3_gnn_hq_w2"]
    lay["L3_brow"] = np.concatenate([a["L3_gnn_hk_b1"], a["L3_gnn_hv_b1"], a["L3_gnn_hq_b1"], a["L3_gnn_hq_b2"]])
    lay["L3_qcols"] = np.stack([a["L3_gnn_hq_g"], a["L3_gnn_hq_beta"]], axis=1)
    lay["attr"] = np.pad(np.concatenate([a["edge_attr_4"], a["edge_attr_64"]], axis=1), ((0, EP - E), (0, 0))).T
    gate = np.pad(a["L3_gnn_ew_w"], ((AF, 0), (0, 0)))
    lay["L3_Wa"] = np.concatenate([hk[:KA], hv[:KA], gate], axis=1)
    lay["L3_W2"] = np.concatenate([a["L3_gnn_hk_w2"], a["L3_gnn_hv_w2"]])
    lay["L3_kvcols"] = np.stack([a["L3_gnn_hk_g"], a["L3_gnn_hk_beta"], a["L3_gnn_hv_g"], a["L3_gnn_hv_beta"]], axis=1)
    lay["L3_kvrow"] = np.concatenate([a["L3_gnn_hk_b2"], a["L3_gnn_hv_b2"]])
    lay["L3_gnn_ew_b"] = a["L3_gnn_ew_b"]
    lay["L3_gnn_no_w1"], lay["L3_gnn_no_w2"] = a["L3_gnn_no_w1"], a["L3_gnn_no_w2"]
    lay["L3_norow"] = np.concatenate([a["L3_gnn_no_b1"], a["L3_gnn_no_b2"]])
    lay["L3_nocols"] = np.stack([a["L3_gnn_no_g"], a["L3_gnn_no_beta"]], axis=1)
    nc = _bacc.Bacc("TRN2", target_bir_lowering=False, num_devices=1)
    arrays, ins = {}, {}
    for name, arr in lay.items():
        arr = np.ascontiguousarray(arr)
        arrays[f"in_{name}"] = arr
        ins[name] = nc.dram_tensor(f"in_{name}", arr.shape, mybir.dt.from_np(arr.dtype), kind="ExternalInput").ap()
    out = nc.dram_tensor("out_0", (NP, D), F32, kind="ExternalOutput").ap()
    build(nc, ins, out)
    r = _run(nc, [arrays], core_ids=[0])
    return r.results[0]["out_0"][:N]
```

```python
from contextlib import ExitStack

import concourse.bass as bass
from concourse import mybir

P = 128
D = 128
N = 12500
E = 212500
NW = -(-N // P)
NP = NW * P
NT = P * -(-E // (P * P))
EP = NT * P
TC = NT // P
GS = 4
NS = -(-(-(-E // P) + NW - 1) // (2 * GS)) * 2 * GS
NC = -(-NS // P)
NSP = NC * P
NH0, DH0 = 8, 16
RT, VT = 16, 8
NH3, DH3 = 16, 8
AF, RF = 4, 64
KA = AF + RF
AC0 = D + NH0 + RT
AC3 = D + NH3
BIG = 1.0e30
EPS = 1e-5

ALU = mybir.AluOpType
ACT = mybir.ActivationFunctionType
F32 = mybir.dt.float32
BF16 = mybir.dt.bfloat16
I32 = mybir.dt.int32
AX = mybir.AxisListType.X
ds = bass.ds


def hold(eng, sem, value):
    eng.wait_ge(sem, value)
    eng.nop(nofuse=True)


class Stage:

    def __init__(self, nc, ctx, prefix):
        self.nc, self.ctx, self.prefix = nc, ctx, prefix
        self.held, self.sems = ExitStack(), []
        ctx.push(self.give_back)

    def sb(self, name, shape, dt=F32):
        return self.ctx.enter_context(self.nc.sbuf_tensor(f"{self.prefix}_{name}", shape, dt))

    def ps(self, name, shape):
        return self.ctx.enter_context(self.nc.psum_tensor(f"{self.prefix}_{name}", shape, F32))

    def gather_sem(self, name):
        return self.nc.alloc_semaphore(f"{self.prefix}_{name}")

    def sem(self, name):
        self.sems.append(self.held.enter_context(self.nc.semaphore(f"{self.prefix}_{name}")))
        return self.sems[-1]

    def give_back(self, failed, *_):
        if self.sems and not failed:
            with self.nc.Block() as block:
                @block.sync
                def _(sp):
                    for s in self.sems:
                        sp.sem_clear(s)
        self.held.close()


def constants(nc, keep):
    keep.iota_row = keep.sb("iota_row", [P, P])
    keep.iota_col = keep.sb("iota_col", [P, 1])
    keep.ident = keep.sb("ident", [P, P])
    keep.before = keep.sb("before", [P, P])
    keep.eps = keep.sb("eps", [P, 1])
    ones_ready, placed = keep.sem("ones_ready"), keep.sem("placed")
    with nc.Block() as block:
        @block.gpsimd
        def _(pool):
            nc.gpsimd.memset(keep.eps[:], EPS)
            nc.gpsimd.memset(keep.before[:], 1.0)
            nc.gpsimd.memset(keep.ident[:], 0.0).then_inc(ones_ready, 1)
            nc.gpsimd.iota(keep.iota_row[:], [[1, P]], base=0, channel_multiplier=0,
                           allow_small_or_imprecise_dtypes=True)
            nc.gpsimd.iota(keep.iota_col[:], [[1, 1]], base=0, channel_multiplier=1,
                           allow_small_or_imprecise_dtypes=True)
            pool.wait_ge(ones_ready, 1)
            nc.gpsimd.affine_select(out=keep.ident[:], in_=keep.ident[:], compare_op=ALU.not_equal, fill=1.0,
                                    base=0, pattern=[[-1, P]], channel_multiplier=1)
            nc.gpsimd.affine_select(out=keep.before[:], in_=keep.before[:], compare_op=ALU.is_ge, fill=0.0,
                                    base=-1, pattern=[[1, P]], channel_multiplier=-1).then_inc(placed, 1)
            pool.wait_ge(placed, 1)


def plan_slots(nc, keep, dram, src, dst, etype, eweight):
    ctx = ExitStack()
    st = Stage(nc, ctx, "plan")
    with ctx:
        drow = st.sb("drow", [P, TC * P], I32)
        ab = st.sb("ab", [P, 2, TC])
        abi = st.sb("abi", [P, 2, TC], I32)
        cnt = st.sb("cnt", [P, TC])
        incl = st.sb("incl", [P, TC])
        zero = st.sb("zero", [P, NT])
        offs = st.sb("offs", [P, 1])
        bv = st.sb("bv", [P, 2, TC])
        row = st.sb("row", [P, 2, NT])
        step = st.sb("step", [P, NT])
        mask = st.sb("mask", [P, NT])
        prod = st.sb("prod", [P, NT])
        sid = st.sb("sid", [P, NC])
        tsum = st.sb("tsum", [P, NC])
        ksum = st.sb("ksum", [P, NC])
        tk = st.sb("tk", [P, 2, NC])
        tki = st.sb("tki", [P, 2, NC], I32)
        raw = st.sb("raw", [P, 4, P], I32)
        flt = st.sb("flt", [P, 5, P])
        dlb = st.sb("dlb", [P, P], BF16)
        none = st.sb("none", [P, 1])
        ps_o = st.ps("ps_o", [P, 512])
        ps_t = st.ps("ps_t", [P, 4, P])
        loaded, iota_done, v, pe_done = st.sem("loaded"), st.sem("iota"), st.sem("v"), st.sem("offs_summed")
        stored, rows_back, tk_stored, tk_back = st.sem("stored"), st.sem("rows_back"), st.sem("tk_stored"), st.sem("tk_back")
        tk_ready, got, rows_ready, rows_out = st.sem("tk_ready"), st.gather_sem("got"), st.sem("rows_ready"), st.sem("rows_out")
        turned, kept, bv_ready, d_ready = st.sem("turned"), st.sem("kept"), st.sem("bv_ready"), st.sem("d_ready")
        cnt_ready = st.sem("cnt_ready")
        ni = [0]
        with nc.Block() as block:
            @block.sync
            def _(sp):
                sp.dma_start(drow[:], dst.rearrange("(p f) -> p f", p=P)).then_inc(loaded, 16)
                sp.wait_ge(bv_ready, 1)
                for j in range(2):
                    sp.dma_start(dram.plan[j].rearrange("(p c) -> p c", p=P), bv[:, j, :]).then_inc(stored, 16)
                sp.wait_ge(stored, 32)
                for j in range(2):
                    sp.dma_start(row[:, j, :], dram.plan[j].partition_broadcast(P)).then_inc(rows_back, 16)
                sp.wait_ge(tk_ready, 1)
                for j in range(2):
                    sp.dma_start(dram.tk[j].rearrange("(c p) -> p c", p=P), tki[:, j, :],
                                 allow_slow_non_contiguous=True).then_inc(tk_stored, 16)
                sp.wait_ge(tk_stored, 32)
                sp.dma_start(keep.window[0:1, :], dram.tk[1:2, :]).then_inc(tk_back, 16)
                sp.wait_ge(tk_back, 16)
                for c in range(NC):
                    sp.wait_ge(rows_ready, c + 1)
                    sp.dma_start(dram.dlrow[c * P:(c + 1) * P, :], dlb[:]).then_inc(rows_out, 16)
                    sp.dma_start(dram.srcrow[c * P:(c + 1) * P, :], flt[:, 1, :]).then_inc(rows_out, 16)
                    sp.dma_start(dram.dlflat[c * P:(c + 1) * P, :], flt[:, 0, :]).then_inc(rows_out, 16)
                    sp.dma_start(dram.dstflat[c * P * P + 1:(c + 1) * P * P + 1].rearrange("(s e) -> s e", e=P),
                                 flt[:, 4, :]).then_inc(rows_out, 16)
                    sp.wait_ge(rows_out, 64 * (c + 1))
                sp.dma_start(dram.dstflat[0:1].unsqueeze(0), none[0:1, :]).then_inc(rows_out, 16)
                sp.wait_ge(rows_out, 64 * NC + 16)

            @block.gpsimd
            def _(pool):
                nc.gpsimd.iota(sid[:], [[P, NC]], base=0, channel_multiplier=1,
                               allow_small_or_imprecise_dtypes=True).then_inc(iota_done, 1)
                pool.wait_ge(tk_ready, 1)
                for c in range(NC):
                    if c:
                        pool.wait_ge(rows_ready, c)
                    for j, table in enumerate((dst, src, etype, eweight)):
                        pool.indirect_dma_start(
                            out=raw[:, j, :].bitcast(table.dtype), out_offset=None,
                            in_=table.rearrange("(t e) -> t e", e=P),
                            in_offset=bass.IndirectOffsetOnAxis(ap=tki[:, 0, c:c + 1], axis=0)).then_inc(got, 16)

            @block.tensor
            def _(pe):
                pe.wait_ge(cnt_ready, 1)
                pe.matmul(ps_o[:, 0:1], keep.before[:], incl[:, TC - 1:TC], start=True, stop=True).then_inc(pe_done, 1)
                for c in range(NC):
                    pe.wait_ge(rows_ready, c + 1)
                    if c:
                        pe.wait_ge(kept, c)
                    for j in range(4):
                        t = pe.transpose(ps_t[:, j, :], flt[:, j, :], keep.ident[:])
                    t.then_inc(turned, 1)

            @block.vector
            def _(dve):
                n = [0]

                def link(ins):
                    n[0] += 1
                    ins.then_inc(v, 1)
                    dve.wait_ge(v, n[0])

                link(nc.vector.memset(none[:], -1.0))
                link(nc.vector.memset(zero[:], 0.0))
                dve.wait_ge(loaded, 16)
                dv = drow[:].rearrange("p (c e) -> p c e", e=P)
                link(nc.vector.tensor_scalar(abi[:, 0, :], dv[:, :, 0], 7, None, ALU.arith_shift_right))
                link(nc.vector.tensor_scalar(abi[:, 1, :], dv[:, :, P - 1], 7, None, ALU.arith_shift_right))
                link(nc.vector.tensor_copy(ab[:], abi[:]))
                link(nc.vector.scalar_tensor_tensor(out=cnt[:], in0=ab[:, 1, :], scalar=1.0, in1=ab[:, 0, :],
                                                    op0=ALU.add, op1=ALU.subtract))
                nc.vector.tensor_tensor_scan(incl[:], cnt[:], zero[:, 0:TC], 0.0, ALU.add, ALU.add).then_inc(cnt_ready, 1)
                dve.wait_ge(pe_done, 1)
                link(nc.vector.tensor_copy(offs[:], ps_o[:, 0:1]))
                link(nc.vector.scalar_tensor_tensor(out=bv[:, 0, :], in0=incl[:], scalar=offs[:, 0:1], in1=cnt[:],
                                                    op0=ALU.add, op1=ALU.subtract))
                nc.vector.tensor_tensor(bv[:, 1, :], ab[:, 0, :], bv[:, 0, :], ALU.subtract).then_inc(bv_ready, 1)
                dve.wait_ge(rows_back, 32)
                link(nc.vector.tensor_copy(step[:, 0:1], row[:, 1, 0:1]))
                link(nc.vector.tensor_tensor(step[:, 1:NT], row[:, 1, 1:NT], row[:, 1, 0:NT - 1], ALU.subtract))
                dve.wait_ge(iota_done, 1)
                for c in range(NC):
                    link(nc.vector.tensor_scalar(mask[:], row[:, 0, :], sid[:, c:c + 1], None, ALU.is_le))
                    link(nc.vector.tensor_reduce(tsum[:, c:c + 1], mask[:], AX, ALU.add))
                    link(nc.vector.tensor_tensor(prod[:], mask[:], step[:], ALU.mult))
                    link(nc.vector.tensor_reduce(ksum[:, c:c + 1], prod[:], AX, ALU.add))
                link(nc.vector.tensor_scalar(tk[:, 0, :], tsum[:], -1.0, None, ALU.add))
                link(nc.vector.tensor_tensor(tk[:, 1, :], ksum[:], sid[:], ALU.add))
                link(nc.vector.tensor_scalar(tk[:, 1, :], tk[:, 1, :], float(NW), None, ALU.min))
                nc.vector.tensor_copy(tki[:], tk[:]).then_inc(tk_ready, 1)
                link(nc.vector.tensor_scalar(ksum[:], tk[:, 1, :], float(-P), None, ALU.mult))
                for c in range(NC):
                    dve.wait_ge(got, 64 * (c + 1))
                    if c:
                        dve.wait_ge(rows_out, 64 * c)
                        dve.wait_ge(turned, c)
                    link(nc.vector.tensor_copy(flt[:, 4, :], raw[:, 0, :]))
                    link(nc.vector.tensor_copy(flt[:, 1:3, :], raw[:, 1:3, :]))
                    link(nc.vector.tensor_copy(flt[:, 3, :], raw[:, 3, :].bitcast(F32)))
                    link(nc.vector.tensor_scalar(flt[:, 0, :], flt[:, 4, :], ksum[:, c:c + 1], None, ALU.add))
                    nc.vector.tensor_copy(dlb[:], flt[:, 0, :]).then_inc(rows_ready, 1)
                    dve.wait_ge(turned, c + 1)
                    sl = slice(c * P, (c + 1) * P)
                    link(nc.vector.tensor_copy(keep.dl[:, sl], ps_t[:, 0, :]))
                    link(nc.vector.tensor_copy(keep.src[:, sl], ps_t[:, 1, :]))
                    link(nc.vector.tensor_copy(keep.srcf[:, sl], ps_t[:, 1, :]))
                    link(nc.vector.tensor_copy(keep.et[:, sl], ps_t[:, 2, :]))
                    link(nc.vector.tensor_copy(keep.ew[:, sl], ps_t[:, 3, :]))
                    link(nc.vector.tensor_scalar(mask[:, 0:P], ps_t[:, 1, :], float(RT), None, ALU.mult))
                    nc.vector.tensor_tensor(keep.srct[:, sl], mask[:, 0:P], ps_t[:, 2, :], ALU.add).then_inc(kept, 1)
                dve.wait_ge(kept, NC)


class Chain:

    def __init__(self, eng, sem, per):
        self.eng, self.sem, self.per, self.base, self.n = eng, sem, per, 0, 0

    def start(self, i):
        self.base, self.n = i * self.per, 0

    def end(self):
        assert self.n == self.per, (self.n, self.per)

    def link(self, ins, held=False):
        self.n += 1
        ins.then_inc(self.sem, 1)
        if held:
            hold(self.eng, self.sem, self.base + self.n)
        else:
            self.eng.wait_ge(self.sem, self.base + self.n)


def layer_norm_statistics(nc, chain, x, stats, mv, var_ready):
    for w in range(2):
        chain.link(nc.vector.bn_stats(stats[:, w, :], x[:, w, :]), held=True)
    nc.vector.bn_aggr(mv[:, 0, :], stats[:, 0, :])
    nc.vector.bn_aggr(mv[:, 1, :], stats[:, 1, :]).then_inc(var_ready, 1)


def layer_norm_apply(nc, chain, out, x, mv, std, rstd, relu=True):
    chain.link(nc.vector.reciprocal(rstd[:], std[:]))
    for w in range(2):
        chain.link(nc.vector.tensor_scalar(out[:, w, :], x[:, w, :], mv[:, w, 0:1], rstd[:, w:w + 1],
                                           ALU.subtract, ALU.mult))
    if relu:
        chain.link(nc.vector.tensor_scalar(out[:], out[:], 0.0, None, ALU.max))


def rows(table, i):
    return table[ds(i * 2 * P, 2 * P), :].rearrange("(w p) d -> p w d", p=P)


def project_qkv(nc, keep, dram, x, wqkv, q):
    ctx = ExitStack()
    st = Stage(nc, ctx, "qkv")
    with ctx:
        w = st.sb("w", [P, 3 * D])
        xt = st.sb("xt", [P, 2, D])
        h = st.sb("h", [P, 2, D])
        hT = st.sb("hT", [P, 2, P])
        kv = st.sb("kv", [P, 2, 2 * D])
        stats, mv = st.sb("stats", [P, 2, 6]), st.sb("mv", [P, 2, 2])
        std, rstd = st.sb("std", [P, 2]), st.sb("rstd", [P, 2])
        ps_t = st.ps("ps_t", [P, 2, P])
        ps_o = st.ps("ps_o", [P, 2, 512])
        w_in, x_in, x_used, v = st.sem("w_in"), st.sem("x_in"), st.sem("x_used"), st.sem("v")
        var_ready, std_ready, h_ready = st.sem("var_ready"), st.sem("std_ready"), st.sem("h_ready")
        h_turned, hT_ready, projected = st.sem("h_turned"), st.sem("hT_ready"), st.sem("projected")
        q_kept, kv_ready, stored = st.sem("q_kept"), st.sem("kv_ready"), st.sem("stored")
        with nc.Block() as block:
            @block.sync
            def _(sp):
                sp.dma_start(w[:], wqkv).then_inc(w_in, 16)
                sp.sem_inc(x_used, 1)
                with sp.Fori(0, NW // 2) as i:
                    sp.wait_ge(x_used, i + 1)
                    sp.dma_start(xt[:], rows(x, i)).then_inc(x_in, 16)

            @block.vector
            def _(dve):
                ch = Chain(dve, v, 6)
                nc.vector.memset(q[:, NW * D:], 0.0)
                with dve.Fori(0, NW // 2) as i:
                    ch.start(i)
                    hold(dve, x_in, 16 * (i + 1))
                    layer_norm_statistics(nc, ch, xt, stats, mv, var_ready)
                    hold(dve, std_ready, i + 1)
                    layer_norm_apply(nc, ch, h, xt, mv, std, rstd)
                    dve.sem_inc(h_ready, 1)
                    dve.sem_inc(x_used, 1)
                    hold(dve, projected, i + 1)
                    nc.vector.tensor_copy(q[:, ds(i * 2 * D, 2 * D)].rearrange("p (w d) -> p w d", w=2),
                                          ps_o[:, :, 0:D]).then_inc(q_kept, 1)

                    ch.end()
            @block.scalar
            def _(act):
                act.sem_inc(stored, 32)
                with act.Fori(0, NW // 2) as i:
                    act.wait_ge(var_ready, i + 1)
                    nc.scalar.activation(std[:], mv[:, :, 1], ACT.Sqrt, bias=keep.eps[:]).then_inc(std_ready, 1)
                    act.wait_ge(stored, 32 * (i + 1))
                    act.wait_ge(h_turned, i + 1)
                    nc.scalar.copy(hT[:], ps_t[:]).then_inc(hT_ready, 1)
                    act.wait_ge(hT_ready, i + 1)
                    act.dma_start(dram.hT[:, ds(i * 2 * P, 2 * P)].rearrange("f (w p) -> f w p", w=2),
                                  hT[:]).then_inc(stored, 16)
                    act.wait_ge(q_kept, i + 2)
                    nc.scalar.copy(kv[:], ps_o[:, :, D:3 * D]).then_inc(kv_ready, 1)
                    act.wait_ge(kv_ready, i + 1)
                    act.dma_start(rows(dram.kv, i), kv[:]).then_inc(stored, 16)
                act.wait_ge(stored, 32 * (NW // 2 + 1))

            @block.tensor
            def _(pe):
                pe.wait_ge(w_in, 16)
                pe.sem_inc(q_kept, 1)
                with pe.Fori(0, NW // 2) as i:
                    pe.wait_ge(h_ready, i + 1)
                    for u in range(2):
                        t = pe.transpose(ps_t[:, u, :], h[:, u, :], keep.ident[:])
                    t.then_inc(h_turned, 1)
                    pe.wait_ge(hT_ready, i + 1)
                    pe.wait_ge(q_kept, i + 1)
                    for u in range(2):
                        t = pe.matmul(ps_o[:, u, 0:3 * D], hT[:, u, :], w[:], start=True, stop=True)
                    t.then_inc(projected, 1)


def at_start(j):
    return isinstance(j, int) and j == 0


def passes(eng, half, group):
    for b, nxt in ((0, (0, 1)), (1, (1, 0))):
        group(0, b, nxt)
    with eng.Fori(1, half - 1) as i:
        for b, nxt in ((0, (i, 1)), (1, (i + 1, 0))):
            group(i, b, nxt)
    for b, nxt in ((0, (half - 1, 1)), (1, None)):
        group(half - 1, b, nxt)


class Numbers:

    def __init__(self, eng, table, top, prefix, slots=GS):
        self.eng, self.table, self.top, self.slots = eng, table, top, slots
        self.regs = [eng.alloc_register(f"{prefix}_{u}") for u in range(slots)]

    def load(self, g):
        self.eng.load(self.regs, self.table[0:1, ds(g * self.slots, self.slots)])
        return [self.eng.snap(r, min_val=0, max_val=self.top) for r in self.regs]


def edges_0(nc, keep, dram, q, acc):
    ctx = ExitStack()
    st = Stage(nc, ctx, "e0")
    with ctx:
        B = range(2)
        dlr = st.sb("dlr", [P, 2, GS * P], BF16)
        spread = st.sb("spread", [P, 2, GS * P])
        collect = st.sb("collect", [P, 2, GS, P])
        gidx = st.sb("gidx", [P, 2, GS], I32)
        kv = st.sb("kv", [P, 2, GS, 2 * D])
        prod = st.sb("prod", [P, GS, D])
        score = st.sb("score", [P, 2, GS * NH0])
        vals = st.sb("vals", [P, 2, GS, AC0])
        ps_q = st.ps("ps_q", [P, 2, GS, D])
        ps_a = st.ps("ps_a", [P, 2, GS, 256])
        dlr_in, kv_in = [st.sem(f"dlr_in{b}") for b in B], [st.gather_sem(f"kv_in{b}") for b in B]
        idx_ready = st.sem("idx_ready")
        spread_ready, collect_ready = [st.sem(f"spread_ready{b}") for b in B], [st.sem(f"collect_ready{b}") for b in B]
        q_spread, prod_ready = [st.sem(f"q_spread{b}") for b in B], [st.sem(f"prod_ready{b}") for b in B]
        dots, score_ready = [st.sem(f"dots{b}") for b in B], [st.sem(f"score_ready{b}") for b in B]
        weights_ready, vals_ready = [st.sem(f"weights_ready{b}") for b in B], [st.sem(f"vals_ready{b}") for b in B]
        summed, added = [st.sem(f"summed{b}") for b in B], st.sem("added")
        half = NS // GS // 2
        with nc.Block() as block:
            @block.sync
            def _(sp):
                def group(i, b, nxt):
                    if not at_start(i):
                        sp.wait_ge(spread_ready[b], i)
                    sp.dma_start(dlr[:, b, :], local_rows(dram, 2 * i + b)).then_inc(dlr_in[b], 16)
                passes(sp, half, group)

            @block.gpsimd
            def _(pool):
                def group(i, b, nxt):
                    if not at_start(i):
                        hold(pool, vals_ready[b], i)
                    nc.gpsimd.tensor_copy(gidx[:, b, :], keep.src[:, ds((2 * i + b) * GS, GS)]).then_inc(idx_ready, 1)
                    hold(pool, idx_ready, 2 * i + b + 1)
                    for u in range(GS):
                        pool.indirect_dma_start(
                            out=kv[:, b, u, :], out_offset=None, in_=dram.kv,
                            in_offset=bass.IndirectOffsetOnAxis(ap=gidx[:, b, u:u + 1], axis=0)).then_inc(kv_in[b], 16)
                passes(pool, half, group)

            @block.tensor
            def _(pe):
                windows = Numbers(pe, keep.window, NW, "e0_pe")

                def spread_q(i, b):
                    ks = windows.load(2 * i + b)
                    pe.wait_ge(spread_ready[b], i + 1)
                    if not at_start(i):
                        pe.wait_ge(prod_ready[b], i)
                    for u in range(GS):
                        t = pe.matmul(ps_q[:, b, u, :], spread[:, b, u * P:(u + 1) * P], q[:, ds(ks[u] * D, D)],
                                      start=True, stop=True)
                    t.then_inc(q_spread[b], 1)

                def group(i, b, nxt):
                    if nxt:
                        spread_q(*nxt)
                    pe.wait_ge(collect_ready[b], i + 1)
                    pe.wait_ge(vals_ready[b], i + 1)
                    if not at_start(i):
                        pe.wait_ge(added, (2 * i + b - 1) * GS + 1)
                    for u in range(GS):
                        t = pe.matmul(ps_a[:, b, u, 0:AC0], collect[:, b, u, :], vals[:, b, u, :], start=True, stop=True)
                    t.then_inc(summed[b], 1)

                spread_q(0, 0)
                passes(pe, half, group)

            @block.scalar
            def _(act):
                def group(i, b, nxt):
                    act.wait_ge(score_ready[b], i + 1)
                    nc.scalar.activation(vals[:, b, :, D:D + NH0],
                                         score[:, b, :].rearrange("p (u h) -> p u h", u=GS),
                                         ACT.Exp, scale=float(DH0) ** -0.5).then_inc(weights_ready[b], 1)
                passes(act, half, group)

            @block.vector
            def _(dve):
                windows = Numbers(dve, keep.window, NW, "e0_dve")

                def make_spread(i, b):
                    dve.wait_ge(dlr_in[b], 16 * (i + 1))
                    if not at_start(i):
                        dve.wait_ge(q_spread[b], i)
                    nc.vector.tensor_scalar(spread[:, b, :], dlr[:, b, :], keep.iota_col[:, 0:1], None,
                                            ALU.is_equal).then_inc(spread_ready[b], 1)

                def make_collect(i, b):
                    g = 2 * i + b
                    if not at_start(i):
                        dve.wait_ge(summed[b], i)
                    nc.vector.tensor_tensor(
                        collect[:, b], keep.iota_row[:].unsqueeze(1).broadcast_to([P, GS, P]),
                        keep.dl[:, ds(g * GS, GS)].unsqueeze(2).broadcast_to([P, GS, P]), ALU.is_equal)
                    nc.vector.tensor_tensor(
                        vals[:, b, :, D + NH0:AC0], keep.iota_row[:, 0:RT].unsqueeze(1).broadcast_to([P, GS, RT]),
                        keep.et[:, ds(g * GS, GS)].unsqueeze(2).broadcast_to([P, GS, RT]),
                        ALU.is_equal).then_inc(collect_ready[b], 1)

                def add_sums(i, b):
                    ks = windows.load(2 * i + b)
                    dve.wait_ge(summed[b], i + 1)
                    for u in range(GS):
                        a = acc[:, ds(ks[u] * AC0, AC0)]
                        dve.wait_ge(added, (2 * i + b) * GS + u + 1)
                        nc.vector.tensor_tensor(a, a, ps_a[:, b, u, 0:AC0], ALU.add).then_inc(added, 1)

                def group(i, b, nxt):
                    if nxt:
                        make_spread(*nxt)
                    dve.wait_ge(q_spread[b], i + 1)
                    dve.wait_ge(kv_in[b], 16 * GS * (i + 1))
                    if not (at_start(i) and b == 0):
                        dve.wait_ge(dots[1 - b], i + b)
                    nc.vector.tensor_tensor(prod[:], kv[:, b, :, 0:D], ps_q[:, b], ALU.mult).then_inc(prod_ready[b], 1)
                    dve.wait_ge(prod_ready[b], i + 1)
                    nc.vector.tensor_reduce(score[:, b, :], prod[:].rearrange("p u (h e) -> p (u h) e", e=DH0),
                                            AX, ALU.add).then_inc(dots[b], 1)
                    dve.wait_ge(dots[b], i + 1)
                    lim = 5.0 * float(DH0) ** 0.5
                    nc.vector.tensor_scalar(score[:, b, :], score[:, b, :], -lim, lim, ALU.max,
                                            ALU.min).then_inc(score_ready[b], 1)
                    if b == 1:
                        add_sums(i, 0)
                    elif not at_start(i):
                        add_sums(i - 1, 1)
                    if nxt:
                        make_collect(*nxt)
                    dve.wait_ge(weights_ready[b], i + 1)
                    nc.vector.tensor_tensor(
                        vals[:, b, :, 0:D].rearrange("p u (h e) -> p u h e", e=DH0),
                        kv[:, b, :, D:2 * D].rearrange("p u (h e) -> p u h e", e=DH0),
                        vals[:, b, :, D:D + NH0].unsqueeze(3).broadcast_to([P, GS, NH0, DH0]),
                        ALU.mult).then_inc(vals_ready[b], 1)

                nc.vector.memset(acc[:], 0.0).then_inc(added, 1)
                make_spread(0, 0)
                make_collect(0, 0)
                passes(dve, half, group)
                add_sums(half - 1, 1)


def local_rows(dram, g):
    return dram.dlrow.rearrange("s e -> (s e)")[ds(g * GS * P, GS * P)].partition_broadcast(P)


def norm_coefficients(nc, link, scale, shift, stats, mv, var_ready, std, std_ready, gain, offset, nodes, turn, dve):
    full = N // P // 4
    for c in range(full):
        link(nc.vector.bn_stats(stats[:, c, :], nodes[:, 4 * c:4 * c + 4, 0:D]), held=True)
    rest = [(w, min(P, N - w * P)) for w in range(4 * full, NW)]
    for j, (w, n) in enumerate(rest):
        link(nc.vector.bn_stats(stats[:, full + j, :], nodes[:, w, 0:n]), held=True)
    nc.vector.bn_aggr(mv[:], stats[:, 0:full + len(rest), :]).then_inc(var_ready, 1)
    dve.wait_ge(std_ready, turn)
    link(nc.vector.reciprocal(scale[:], std[:]))
    link(nc.vector.tensor_tensor(scale[:], scale[:], gain, ALU.mult))
    link(nc.vector.tensor_tensor(shift[:], mv[:, 0:1], scale[:], ALU.mult))
    link(nc.vector.tensor_tensor(shift[:], offset, shift[:], ALU.subtract))


def mix_0(nc, keep, dram, ins, nodes):
    ctx = ExitStack()
    st = Stage(nc, ctx, "m0")
    nd = nodes[:].rearrange("p (w c) -> p w c", c=AC0)
    HT = NW // 2
    HC = RT // 4
    with ctx:
        wo, w1 = st.sb("wo", [P, D]), st.sb("w1", [P, 2 * D])
        w2, cols = st.sb("w2", [P, 2, D]), st.sb("cols", [P, 8])
        wt, bt = st.sb("wt", [P, (RT + VT) * D]), st.sb("bt", [RT + VT, D])
        ntype, ntf = st.sb("ntype", [P, NW], I32), st.sb("ntf", [P, NW])
        den, rec = st.sb("den", [P, 2, NH0]), st.sb("rec", [P, 2, NH0])
        at, aT, hT = st.sb("at", [P, 2, D]), st.sb("aT", [P, 2, P]), st.sb("hT", [P, 2, P])
        xc, hid = st.sb("xc", [P, 2, P]), st.sb("hid", [P, 2, 2 * P])
        stats, mv = st.sb("stats", [P, 32, 6]), st.sb("mv", [P, 2])
        std, scale, shift = st.sb("std", [P, 1]), st.sb("scale", [P, 1]), st.sb("shift", [P, 1])
        deg, sqd, has = st.sb("deg", [P, NW + 1]), st.sb("sqd", [P, NW + 1]), st.sb("has", [P, NW + 1])
        xt, h = st.sb("xt", [P, 2, D]), st.sb("h", [P, 2, D])
        st2, mv2 = st.sb("st2", [P, 2, 6]), st.sb("mv2", [P, 2, 2])
        sd2, rs2 = st.sb("sd2", [P, 2]), st.sb("rs2", [P, 2])
        ind, indT = st.sb("ind", [P, 2, RT + VT]), st.sb("indT", [RT + VT, 2, P])
        hw = st.sb("hw", [P, 2, RT * D])
        ps_t = st.ps("ps_t", [P, 2, 2, P])
        ps_w = st.ps("ps_w", [P, RT + VT, D])
        ps_b = st.ps("ps_b", [P, 512])
        w_in, v, var_ready, std_ready = st.sem("w_in"), st.sem("v"), st.sem("var_ready"), st.sem("std_ready")
        hT_in, hT_used, at_ready, at_turned = st.sem("hT_in"), st.sem("hT_used"), st.sem("at_ready"), st.sem("at_turned")
        aT_ready, mixed, y_ready = st.sem("aT_ready"), st.sem("mixed"), st.sem("y_ready")
        xc_ready, up, hid_ready, down, y2_ready = (st.sem("xc_ready"), st.sem("up"), st.sem("hid_ready"),
                                                   st.sem("down"), st.sem("y2_ready"))
        x_in, z_ready, z_turned, x1_ready = st.sem("x_in"), st.sem("z_ready"), st.sem("z_turned"), st.sem("x1_ready")
        x1_out, var2_ready, std2_ready, h_ready = st.sem("x1_out"), st.sem("var2_ready"), st.sem("std2_ready"), st.sem("h_ready")
        h_turned, hT2_ready, typed, picked, hw_ready = (st.sem("h_turned"), st.sem("hT2_ready"), st.sem("typed"),
                                                        st.sem("picked"), st.sem("hw_ready"))
        hw_out, v1, v2, v3 = [st.sem(f"hw_out{u}") for u in range(2)], st.sem("v1"), st.sem("v2"), st.sem("v3")
        degs, roots, made_row, v4 = st.sem("degs"), st.sem("roots"), st.sem("made_row"), st.sem("v4")
        WL = [(wo[:], ins["L0_gnn_Wo"]), (w1[:], ins["L0_gnn_W1"]),
              (w2[:], ins["L0_gnn_W2"].rearrange("(c p) d -> p c d", p=P)), (cols[:], ins["L0_cols"]),
              (wt[:], ins["L1_W"]), (bt[:], ins["L1_b"]), (ntype[:], ins["node_type_8"])]
        NWL = 16 * len(WL)
        with nc.Block() as block:
            @block.sync
            def _(sp):
                for to, frm in WL:
                    sp.dma_start(to, frm).then_inc(w_in, 16)
                sp.sem_inc(hT_used, 1)
                with sp.Fori(0, HT) as i:
                    sp.wait_ge(hT_used, i + 1)
                    sp.dma_start(hT[:], dram.hT[:, ds(i * 2 * P, 2 * P)].rearrange("f (w p) -> f w p", w=2)
                                 ).then_inc(hT_in, 16)

                def load_x(i):
                    if not at_start(i):
                        sp.wait_ge(x1_out, 16 * i)
                        sp.wait_ge(h_ready, i)
                    sp.dma_start(xt[:], rows(ins["x"], i)).then_inc(x_in, 16)

                def store_rows(i, u):
                    sp.wait_ge(hw_ready, HC * (2 * i + u + 2))
                    sp.dma_start(dram.hw.rearrange("(n t) d -> n (t d)", t=RT)[ds((2 * i + u) * P, P), :],
                                 hw[:, u, :]).then_inc(hw_out[u], 16)

                load_x(0)
                load_x(1)
                with sp.Fori(0, HT - 2) as i:
                    store_rows(i, 0)
                    load_x(i + 2)
                    store_rows(i, 1)
                for i in range(HT - 2, HT):
                    store_rows(i, 0)
                    store_rows(i, 1)
                for u in range(2):
                    sp.wait_ge(hw_out[u], 16 * (HT + 1))

            @block.tensor
            def _(pe):
                pe.wait_ge(w_in, NWL)
                with pe.Fori(0, HT) as i:
                    pe.wait_ge(at_ready, i + 1)
                    for u in range(2):
                        t = pe.transpose(ps_t[:, 0, u, :], at[:, u, :], keep.ident[:])
                    t.then_inc(at_turned, 1)
                    pe.wait_ge(aT_ready, i + 1)
                    pe.matmul(ps_b[:, 0:2 * P], wo[:], aT[:].rearrange("p u e -> p (u e)"), start=True,
                              stop=True).then_inc(mixed, 1)
                with pe.Fori(0, HT) as i:
                    pe.wait_ge(xc_ready, i + 1)
                    for c in range(2):
                        t = pe.matmul(ps_w[:, 4 * c:4 * c + 2, :].rearrange("p a b -> p (a b)"),
                                      w1[:, c * D:(c + 1) * D], xc[:].rearrange("p u e -> p (u e)"),
                                      start=True, stop=True)
                    t.then_inc(up, 1)
                    pe.wait_ge(hid_ready, i + 1)
                    for c in range(2):
                        t = pe.matmul(ps_b[:, 0:2 * P], w2[:, c, :], hid[:, c, :], start=(c == 0), stop=(c == 1))
                    t.then_inc(down, 1)

                def turn_z(i):
                    pe.wait_ge(z_ready, i + 1)
                    for u in range(2):
                        t = pe.transpose(ps_t[:, 0, u, :], xc[:, u, :], keep.ident[:])
                    t.then_inc(z_turned, 1)

                def turn_h(i):
                    pe.wait_ge(h_ready, i + 1)
                    for u in range(2):
                        pe.transpose(ps_t[:, 1, u, :], h[:, u, :], keep.ident[:])
                        t = pe.transpose(ps_b[0:RT + VT, u * P:(u + 1) * P], ind[:, u, :], keep.ident[:])
                    t.then_inc(h_turned, 1)

                def products(i, u):
                    pe.wait_ge(picked, 2 * i + u + 1)
                    for c in range(VT // 4):
                        pe.matmul(ps_w[:, RT + 4 * c:RT + 4 * c + 4, :].rearrange("p a b -> p (a b)"), hT[:, u, :],
                                  wt[:, (HC + c) * 512:(HC + c + 1) * 512], start=True, stop=True)
                    pe.matmul(ps_b[:, 256:256 + D], indT[:, u, :], bt[:], start=True, stop=True).then_inc(typed, 1)
                    for c in range(HC):
                        pe.wait_ge(hw_ready, HC * (2 * i + u) + c + 1)
                        pe.matmul(ps_w[:, 4 * c:4 * c + 4, :].rearrange("p a b -> p (a b)"), hT[:, u, :],
                                  wt[:, c * 512:(c + 1) * 512], start=True, stop=True).then_inc(made_row, 1)

                turn_z(0)
                turn_h(0)
                with pe.Fori(0, HT - 1) as i:
                    pe.wait_ge(hT2_ready, i + 1)
                    turn_z(i + 1)
                    products(i, 0)
                    products(i, 1)
                    turn_h(i + 1)
                pe.wait_ge(hT2_ready, HT)
                products(HT - 1, 0)
                products(HT - 1, 1)

            @block.scalar
            def _(act):
                act.wait_ge(w_in, NWL)
                with act.Fori(0, HT) as i:
                    act.wait_ge(at_turned, i + 1)
                    nc.scalar.copy(aT[:], ps_t[:, 0]).then_inc(aT_ready, 1)
                act.wait_ge(degs, 1)
                nc.scalar.activation(sqd[:], deg[:], ACT.Sqrt).then_inc(roots, 1)
                act.wait_ge(var_ready, 1)
                nc.scalar.activation(std[:], mv[:, 1:2], ACT.Sqrt, bias=keep.eps[:]).then_inc(std_ready, 1)
                with act.Fori(0, HT) as i:
                    act.wait_ge(up, i + 1)
                    for c in range(2):
                        a = nc.scalar.activation(hid[:, c, :], ps_w[:, 4 * c:4 * c + 2, :].rearrange("p a b -> p (a b)"),
                                                 ACT.Relu, bias=cols[:, 1 + c:2 + c])
                    a.then_inc(hid_ready, 1)
                act.wait_ge(var_ready, 2)
                nc.scalar.activation(std[:], mv[:, 1:2], ACT.Sqrt, bias=keep.eps[:]).then_inc(std_ready, 1)
                act.sem_inc(hw_ready, HC)
                act.sem_inc(hw_out[0], 16)
                act.sem_inc(hw_out[1], 16)

                def store_x1(i):
                    act.wait_ge(x1_ready, i + 1)
                    act.dma_start(rows(dram.x1, i), xt[:]).then_inc(x1_out, 16)
                    act.wait_ge(var2_ready, i + 1)
                    nc.scalar.activation(sd2[:], mv2[:, :, 1], ACT.Sqrt, bias=keep.eps[:]).then_inc(std2_ready, 1)

                def copy_turned(i):
                    act.wait_ge(h_turned, i + 1)
                    nc.scalar.copy(indT[:], ps_b[0:RT + VT, 0:2 * P].rearrange("p (u e) -> p u e", u=2))
                    nc.scalar.copy(hT[:], ps_t[:, 1]).then_inc(hT2_ready, 1)

                def copy_rows(i):
                    for u in range(2):
                        for c in range(HC):
                            act.wait_ge(made_row, HC * (2 * i + u) + c + 1)
                            if c == 0:
                                hold(act, hw_out[u], 16 * (i + 1))
                            nc.scalar.copy(hw[:, u, c * 512:(c + 1) * 512],
                                           ps_w[:, 4 * c:4 * c + 4, :].rearrange("p a b -> p (a b)")).then_inc(hw_ready, 1)

                store_x1(0)
                copy_turned(0)
                with act.Fori(0, HT - 1) as i:
                    store_x1(i + 1)
                    copy_rows(i)
                    copy_turned(i + 1)
                copy_rows(HT - 1)
                act.wait_ge(x1_out, 16 * HT)

            @block.vector
            def _(dve):
                ch = Chain(dve, v1, 3)
                dve.wait_ge(w_in, NWL)
                with dve.Fori(0, HT) as i:
                    ch.start(i)
                    w = nodes[:, ds(i * 2 * AC0, 2 * AC0)].rearrange("p (w c) -> p w c", w=2)
                    ch.link(nc.vector.tensor_scalar(den[:], w[:, :, D:D + NH0], 1e-6, None, ALU.add))
                    ch.link(nc.vector.reciprocal(rec[:], den[:]))
                    nc.vector.tensor_tensor(at[:].rearrange("p w (h e) -> p w h e", e=DH0),
                                            w[:, :, 0:D].rearrange("p w (h e) -> p w h e", e=DH0),
                                            rec[:].unsqueeze(3).broadcast_to([P, 2, NH0, DH0]),
                                            ALU.mult).then_inc(at_ready, 1)
                    dve.wait_ge(hT_in, 16 * (i + 1))
                    dve.wait_ge(mixed, i + 1)
                    ch.link(nc.vector.scalar_tensor_tensor(
                        out=w[:, :, 0:D], in0=ps_b[:, 0:2 * P].rearrange("p (w d) -> p w d", w=2),
                        scalar=cols[:, 0:1], in1=hT[:], op0=ALU.add, op1=ALU.add))
                    dve.sem_inc(hT_used, 1)
                    ch.end()
                n = [0]

                def link(ins_, held=False):
                    n[0] += 1
                    ins_.then_inc(v, 1)
                    (hold(dve, v, n[0]) if held else dve.wait_ge(v, n[0]))

                cnt = nd[:, :, D + NH0:AC0]
                link(nc.vector.tensor_reduce(deg[:], cnt, AX, ALU.add))
                link(nc.vector.tensor_scalar(has[:], deg[:], 1.0, None, ALU.min))
                nc.vector.tensor_scalar(deg[:], deg[:], 1.0, None, ALU.max).then_inc(degs, 1)
                dve.wait_ge(roots, 1)
                link(nc.vector.reciprocal(sqd[:], sqd[:]))
                link(nc.vector.tensor_tensor(keep.dis[:], sqd[:], has[:], ALU.mult))
                link(nc.vector.tensor_copy(ntf[:], ntype[:]))
                norm_coefficients(nc, link, scale, shift, stats, mv, var_ready, std, std_ready, cols[:, 3:4],
                                  cols[:, 4:5], nd, 1, dve)
                ch = Chain(dve, v2, 1)
                with dve.Fori(0, HT) as i:
                    ch.start(i)
                    w = nodes[:, ds(i * 2 * AC0, 2 * AC0)].rearrange("p (w c) -> p w c", w=2)
                    nc.vector.tensor_scalar(xc[:], w[:, :, 0:D], scale[:, 0:1], shift[:, 0:1], ALU.mult,
                                            ALU.add).then_inc(xc_ready, 1)
                    dve.wait_ge(down, i + 1)
                    ch.link(nc.vector.scalar_tensor_tensor(
                        out=w[:, :, 0:D], in0=ps_b[:, 0:2 * P].rearrange("p (w d) -> p w d", w=2),
                        scalar=cols[:, 5:6], in1=xc[:], op0=ALU.add, op1=ALU.add))
                    ch.end()
                norm_coefficients(nc, link, scale, shift, stats, mv, var_ready, std, std_ready, cols[:, 6:7],
                                  cols[:, 7:8], nd, 2, dve)
                dve.sem_inc(picked, 1)
                norm, pick = Chain(dve, v3, 9), Chain(dve, v4, 2 * (VT + 1))

                def windows_of(i):
                    return nodes[:, ds(i * 2 * AC0, 2 * AC0)].rearrange("p (w c) -> p w c", w=2)

                def norm_ahead(i):
                    norm.start(i)
                    nc.vector.tensor_scalar(xc[:], windows_of(i)[:, :, 0:D], scale[:, 0:1], shift[:, 0:1], ALU.mult,
                                            ALU.add).then_inc(z_ready, 1)
                    dve.wait_ge(x_in, 16 * (i + 1))
                    dve.wait_ge(z_turned, i + 1)
                    norm.link(nc.vector.tensor_tensor(xt[:], xt[:], ps_t[:, 0], ALU.add), held=True)
                    dve.sem_inc(x1_ready, 1)
                    layer_norm_statistics(nc, norm, xt, st2, mv2, var2_ready)
                    hold(dve, std2_ready, i + 1)
                    layer_norm_apply(nc, norm, h, xt, mv2, sd2, rs2)

                def indicate(i):
                    norm.link(nc.vector.tensor_scalar(ind[:, :, 0:RT], windows_of(i)[:, :, D + NH0:AC0], 1.0, None,
                                                      ALU.min))
                    norm.link(nc.vector.tensor_tensor(
                        ind[:, :, RT:RT + VT], keep.iota_row[:, 0:VT].unsqueeze(1).broadcast_to([P, 2, VT]),
                        ntf[:, ds(i * 2, 2)].unsqueeze(2).broadcast_to([P, 2, VT]), ALU.is_equal))
                    dve.sem_inc(h_ready, 1)
                    norm.end()

                def pick_types(i):
                    pick.start(i)
                    w = windows_of(i)
                    for u in range(2):
                        hold(dve, typed, 2 * i + u + 1)
                        pick.link(nc.vector.tensor_copy(w[:, u, 0:D], ps_b[:, 256:256 + D]), held=True)
                        for t in range(VT):
                            pick.link(nc.vector.scalar_tensor_tensor(
                                out=w[:, u, 0:D], in0=ps_w[:, RT + t, :], scalar=ind[:, u, RT + t:RT + t + 1],
                                in1=w[:, u, 0:D], op0=ALU.mult, op1=ALU.add))
                        dve.sem_inc(picked, 1)
                    pick.end()

                norm_ahead(0)
                indicate(0)
                with dve.Fori(0, HT - 1) as i:
                    norm_ahead(i + 1)
                    pick_types(i)
                    indicate(i + 1)
                pick_types(HT - 1)
                link(nc.vector.tensor_scalar(cnt, cnt, 1.0, None, ALU.max))
                link(nc.vector.reciprocal(cnt, cnt))


def edges_1(nc, keep, dram, nodes):
    ctx = ExitStack()
    st = Stage(nc, ctx, "e1")
    with ctx:
        B = range(2)
        dlr = st.sb("dlr", [P, 2, GS * P], BF16)
        spread = st.sb("spread", [P, 2, GS * P])
        collect = st.sb("collect", [P, 2, GS, P])
        gidx = st.sb("gidx", [P, 2, GS], I32)
        msg = st.sb("msg", [P, 2, GS, D])
        hot, share = st.sb("hot", [P, GS, RT]), st.sb("share", [P, GS])
        ps_r = st.ps("ps_r", [P, 2, 512])
        ps_a = st.ps("ps_a", [P, 2, GS, D])
        dlr_in, msg_in = [st.sem(f"dlr_in{b}") for b in B], [st.gather_sem(f"msg_in{b}") for b in B]
        idx_ready = st.sem("idx_ready")
        spread_ready, counts_spread = [st.sem(f"spread_ready{b}") for b in B], [st.sem(f"counts_spread{b}") for b in B]
        hot_ready, share_ready = st.sem("hot_ready"), st.sem("share_ready")
        counts_read, collect_ready = [st.sem(f"counts_read{b}") for b in B], [st.sem(f"collect_ready{b}") for b in B]
        summed, added = [st.sem(f"summed{b}") for b in B], st.sem("added")
        half = NS // GS // 2
        with nc.Block() as block:
            @block.sync
            def _(sp):
                def group(i, b, nxt):
                    if not at_start(i):
                        sp.wait_ge(spread_ready[b], i)
                    sp.dma_start(dlr[:, b, :], local_rows(dram, 2 * i + b)).then_inc(dlr_in[b], 16)
                passes(sp, half, group)

            @block.gpsimd
            def _(pool):
                def group(i, b, nxt):
                    if not at_start(i):
                        hold(pool, summed[b], i)
                    nc.gpsimd.tensor_copy(gidx[:, b, :], keep.srct[:, ds((2 * i + b) * GS, GS)]).then_inc(idx_ready, 1)
                    hold(pool, idx_ready, 2 * i + b + 1)
                    for u in range(GS):
                        pool.indirect_dma_start(
                            out=msg[:, b, u, :], out_offset=None, in_=dram.hw,
                            in_offset=bass.IndirectOffsetOnAxis(ap=gidx[:, b, u:u + 1], axis=0)).then_inc(msg_in[b], 16)
                passes(pool, half, group)

            @block.tensor
            def _(pe):
                windows = Numbers(pe, keep.window, NW, "e1_pe")

                def spread_counts(i, b):
                    ks = windows.load(2 * i + b)
                    pe.wait_ge(spread_ready[b], i + 1)
                    if not at_start(i):
                        pe.wait_ge(counts_read[b], i)
                    for u in range(GS):
                        t = pe.matmul(ps_r[:, b, u * RT:(u + 1) * RT], spread[:, b, u * P:(u + 1) * P],
                                      nodes[:, ds(ks[u] * AC0 + D + NH0, RT)], start=True, stop=True)
                    t.then_inc(counts_spread[b], 1)

                def group(i, b, nxt):
                    if nxt:
                        spread_counts(*nxt)
                    pe.wait_ge(collect_ready[b], i + 1)
                    pe.wait_ge(msg_in[b], 16 * GS * (i + 1))
                    if not at_start(i):
                        pe.wait_ge(added, (2 * i + b - 1) * GS)
                    for u in range(GS):
                        t = pe.matmul(ps_a[:, b, u, :], collect[:, b, u, :], msg[:, b, u, :], start=True, stop=True)
                    t.then_inc(summed[b], 1)

                spread_counts(0, 0)
                passes(pe, half, group)

            @block.vector
            def _(dve):
                windows = Numbers(dve, keep.window, NW, "e1_dve")

                def make_spread(i, b):
                    dve.wait_ge(dlr_in[b], 16 * (i + 1))
                    if not at_start(i):
                        dve.wait_ge(counts_spread[b], i)
                    nc.vector.tensor_scalar(spread[:, b, :], dlr[:, b, :], keep.iota_col[:, 0:1], None,
                                            ALU.is_equal).then_inc(spread_ready[b], 1)

                def add_sums(i, b):
                    ks = windows.load(2 * i + b)
                    dve.wait_ge(summed[b], i + 1)
                    for u in range(GS):
                        a = nodes[:, ds(ks[u] * AC0, D)]
                        s = (2 * i + b) * GS + u
                        if not (isinstance(s, int) and s == 0):
                            dve.wait_ge(added, s)
                        nc.vector.tensor_tensor(a, a, ps_a[:, b, u, :], ALU.add).then_inc(added, 1)

                def group(i, b, nxt):
                    g = 2 * i + b
                    if nxt:
                        make_spread(*nxt)
                    nc.vector.tensor_tensor(
                        hot[:], keep.iota_row[:, 0:RT].unsqueeze(1).broadcast_to([P, GS, RT]),
                        keep.et[:, ds(g * GS, GS)].unsqueeze(2).broadcast_to([P, GS, RT]),
                        ALU.is_equal).then_inc(hot_ready, 1)
                    dve.wait_ge(hot_ready, g + 1)
                    dve.wait_ge(counts_spread[b], i + 1)
                    nc.vector.tensor_tensor(hot[:], hot[:], ps_r[:, b, 0:GS * RT].rearrange("p (u t) -> p u t", u=GS),
                                            ALU.mult).then_inc(counts_read[b], 1)
                    dve.wait_ge(counts_read[b], i + 1)
                    nc.vector.tensor_reduce(share[:], hot[:], AX, ALU.add).then_inc(share_ready, 1)
                    dve.wait_ge(share_ready, g + 1)
                    if not at_start(i):
                        dve.wait_ge(summed[b], i)
                    for u in range(GS):
                        t = nc.vector.tensor_scalar(collect[:, b, u, :], keep.iota_row[:], keep.dl[:, ds(g * GS + u, 1)],
                                                    share[:, u:u + 1], ALU.is_equal, ALU.mult)
                    t.then_inc(collect_ready[b], 1)
                    if b == 1:
                        add_sums(i, 0)
                    elif not at_start(i):
                        add_sums(i - 1, 1)

                make_spread(0, 0)
                passes(dve, half, group)
                add_sums(half - 1, 1)


def clear_tables(nc, cols, dram):
    ctx = ExitStack()
    st = Stage(nc, ctx, "clear")
    dram.cleared = cols.sem("cleared")
    W = (NW + 1) * D // 9
    with ctx:
        zero = cols.sb("zero", [P, W])
        made = st.sem("made")
        with nc.Block() as block:
            @block.gpsimd
            def _(pool):
                nc.gpsimd.memset(zero[:], 0.0).then_inc(made, 1)

            @block.sync
            def _(sp):
                sp.wait_ge(made, 1)
                for table in dram.side:
                    flat = table.rearrange("(p w) d -> p (w d)", p=P)
                    with sp.Fori(0, 9) as i:
                        sp.dma_start(flat[:, ds(i * W, W)], zero[:]).then_inc(dram.cleared, 16)


def mix_1(nc, keep, dram, nodes, hp):
    ctx = ExitStack()
    st = Stage(nc, ctx, "m1")
    HT = NW // 2
    with ctx:
        xt, h = st.sb("xt", [P, 2, 2, D]), st.sb("h", [P, 2, D])
        stats, mv = st.sb("stats", [P, 2, 6]), st.sb("mv", [P, 2, 2])
        std, rstd = st.sb("std", [P, 2]), st.sb("rstd", [P, 2])
        x_in, x2_ready, x_out = st.sem("x_in"), st.sem("x2_ready"), st.sem("x_out")
        var_ready, std_ready, v, done = st.sem("var_ready"), st.sem("std_ready"), st.sem("v"), st.sem("done")
        h_ready = st.sem("h_ready")
        with nc.Block() as block:
            @block.sync
            def _(sp):
                with sp.Fori(0, HT) as i:
                    sp.wait_ge(done, i + 1)
                    sp.dma_start(xt[:, 0], rows(dram.x1, i)).then_inc(x_in, 16)

            @block.scalar
            def _(act):
                act.sem_inc(x_out, 32)
                with act.Fori(0, HT) as i:
                    act.wait_ge(x2_ready, i + 1)
                    act.dma_start(rows(dram.x2, i), xt[:, 1]).then_inc(x_out, 16)
                    act.wait_ge(var_ready, i + 1)
                    nc.scalar.activation(std[:], mv[:, :, 1], ACT.Sqrt, bias=keep.eps[:]).then_inc(std_ready, 1)
                    act.wait_ge(h_ready, i + 1)
                    act.dma_start(rows(dram.h2, i), h[:]).then_inc(x_out, 16)
                act.wait_ge(x_out, 32 * (HT + 1))

            @block.vector
            def _(dve):
                nc.vector.memset(hp[:, NW * D:], 0.0)
                ch = Chain(dve, v, 8)
                dve.sem_inc(done, 1)
                with dve.Fori(0, HT) as i:
                    ch.start(i)
                    w = nodes[:, ds(i * 2 * AC0, 2 * AC0)].rearrange("p (w c) -> p w c", w=2)
                    dve.wait_ge(x_in, 16 * (i + 1))
                    dve.wait_ge(x_out, 32 * (i + 1))
                    ch.link(nc.vector.scalar_tensor_tensor(out=xt[:, 1], in0=w[:, :, 0:D], scalar=0.0, in1=xt[:, 0],
                                                           op0=ALU.max, op1=ALU.add), held=True)
                    dve.sem_inc(x2_ready, 1)
                    dve.sem_inc(done, 1)
                    layer_norm_statistics(nc, ch, xt[:, 1], stats, mv, var_ready)
                    hold(dve, std_ready, i + 1)
                    layer_norm_apply(nc, ch, h, xt[:, 1], mv, std, rstd)
                    dve.sem_inc(h_ready, 1)
                    for u in range(2):
                        t = nc.vector.tensor_scalar(hp[:, ds((2 * i + u) * D, D)], h[:, u, :],
                                                    keep.dis[:, ds(2 * i + u, 1)], None, ALU.mult)
                    ch.link(t)


                    ch.end()
def edges_2(nc, keep, dram, hp):
    ctx = ExitStack()
    st = Stage(nc, ctx, "e2")
    with ctx:
        B = range(2)
        srow = st.sb("srow", [P, 2, GS, P])
        same, collect = st.sb("same", [P, 2, GS, P]), st.sb("collect", [P, 2, GS, P])
        lower, earlier = st.sb("lower", [P, P]), st.sb("earlier", [P, GS, P])
        cnt, spare, dest = st.sb("cnt", [P, GS]), st.sb("spare", [P, GS]), st.sb("dest", [P, GS])
        ncol = st.sb("ncol", [P, 1])
        index = st.sb("index", [P, 2, GS], I32)
        joint, sums = st.sb("joint", [P, 2, GS, P]), st.sb("sums", [P, 2, GS, D])
        ps_j, ps_s = st.ps("ps_j", [P, 2, GS, P]), st.ps("ps_s", [P, 2, GS, D])
        srow_in, same_ready = [st.sem(f"srow_in{b}") for b in B], [st.sem(f"same_ready{b}") for b in B]
        joined, joint_ready = [st.sem(f"joined{b}") for b in B], [st.sem(f"joint_ready{b}") for b in B]
        summed, sums_ready = [st.sem(f"summed{b}") for b in B], [st.sem(f"sums_ready{b}") for b in B]
        index_ready, v = [st.sem(f"index_ready{b}") for b in B], st.sem("v")
        added = [st.gather_sem(f"added{u}") for u in range(GS)]
        lower_made = st.sem("lower_made")
        half = NS // GS // 2
        with nc.Block() as block:
            @block.sync
            def _(sp):
                def group(i, b, nxt):
                    if not at_start(i):
                        sp.wait_ge(same_ready[b], i)
                    sp.dma_start(srow[:, b].rearrange("p u e -> p (u e)"),
                                 dram.srcrow.rearrange("s e -> (s e)")[ds((2 * i + b) * GS * P, GS * P)]
                                 .partition_broadcast(P)).then_inc(srow_in[b], 16)
                passes(sp, half, group)

            @block.gpsimd
            def _(pool):
                nc.gpsimd.memset(lower[:], 1.0).then_inc(lower_made, 1)
                pool.wait_ge(lower_made, 1)
                nc.gpsimd.affine_select(out=lower[:], in_=lower[:], compare_op=ALU.is_ge, fill=0.0, base=-1,
                                        pattern=[[-1, P]], channel_multiplier=1).then_inc(lower_made, 1)

                pool.wait_ge(dram.cleared, 16 * 9 * GS)

                def group(i, b, nxt):
                    hold(pool, index_ready[b], i + 1)
                    hold(pool, sums_ready[b], i + 1)
                    for u in range(GS):
                        if not (at_start(i) and b == 0):
                            hold(pool, added[u], 16 * (2 * i + b))
                        pool.indirect_dma_start(
                            out=dram.side[u], out_offset=bass.IndirectOffsetOnAxis(ap=index[:, b, u:u + 1], axis=0),
                            in_=sums[:, b, u, :], in_offset=None, compute_op=ALU.add).then_inc(added[u], 16)
                passes(pool, half, group)
                for u in range(GS):
                    pool.wait_ge(added[u], 16 * (NS // GS))

            @block.tensor
            def _(pe):
                windows = Numbers(pe, keep.window, NW, "e2_pe")

                def join(i, b):
                    pe.wait_ge(same_ready[b], i + 1)
                    if not at_start(i):
                        pe.wait_ge(joint_ready[b], i)
                    for u in range(GS):
                        t = pe.matmul(ps_j[:, b, u, :], collect[:, b, u, :], same[:, b, u, :], start=True, stop=True)
                    t.then_inc(joined[b], 1)

                def group(i, b, nxt):
                    if nxt:
                        join(*nxt)
                    ks = windows.load(2 * i + b)
                    pe.wait_ge(joint_ready[b], i + 1)
                    if not at_start(i):
                        pe.wait_ge(sums_ready[b], i)
                    for u in range(GS):
                        t = pe.matmul(ps_s[:, b, u, :], joint[:, b, u, :], hp[:, ds(ks[u] * D, D)], start=True, stop=True)
                    t.then_inc(summed[b], 1)

                join(0, 0)
                passes(pe, half, group)

            @block.scalar
            def _(act):
                def copy_joint(i, b):
                    act.wait_ge(joined[b], i + 1)
                    if not at_start(i):
                        act.wait_ge(summed[b], i)
                    nc.scalar.copy(joint[:, b], ps_j[:, b]).then_inc(joint_ready[b], 1)

                def group(i, b, nxt):
                    if nxt:
                        copy_joint(*nxt)
                    if not at_start(i):
                        for u in range(GS):
                            act.wait_ge(added[u], 16 * (2 * i + b - 1))
                    act.wait_ge(summed[b], i + 1)
                    nc.scalar.copy(sums[:, b], ps_s[:, b]).then_inc(sums_ready[b], 1)

                copy_joint(0, 0)
                passes(act, half, group)

            @block.vector
            def _(dve):
                ch = Chain(dve, v, 6)

                def group(i, b, nxt):
                    g = 2 * i + b
                    ch.start(g)
                    cols = ds(g * GS, GS)
                    dve.wait_ge(srow_in[b], 16 * (i + 1))
                    if not at_start(i):
                        dve.wait_ge(joined[b], i)
                    for u in range(GS):
                        nc.vector.tensor_scalar(collect[:, b, u, :], keep.iota_row[:], keep.dl[:, ds(g * GS + u, 1)],
                                                keep.ew[:, ds(g * GS + u, 1)], ALU.is_equal, ALU.mult)
                    nc.vector.tensor_tensor(same[:, b], srow[:, b], keep.srcf[:, cols].unsqueeze(2)
                                            .broadcast_to([P, GS, P]), ALU.is_equal).then_inc(same_ready[b], 1)
                    dve.wait_ge(same_ready[b], i + 1)
                    ch.link(nc.vector.tensor_tensor(earlier[:], same[:, b], lower[:].unsqueeze(1)
                                                    .broadcast_to([P, GS, P]), ALU.mult))
                    ch.link(nc.vector.tensor_reduce(cnt[:], earlier[:], AX, ALU.add))
                    ch.link(nc.vector.scalar_tensor_tensor(out=spare[:], in0=keep.srcf[:, cols], scalar=-1.0,
                                                           in1=ncol[:, 0:1].broadcast_to([P, GS]), op0=ALU.mult,
                                                           op1=ALU.add))
                    ch.link(nc.vector.scalar_tensor_tensor(out=spare[:], in0=cnt[:], scalar=1.0, in1=spare[:],
                                                           op0=ALU.min, op1=ALU.mult))
                    ch.link(nc.vector.tensor_tensor(dest[:], spare[:], keep.srcf[:, cols], ALU.add))
                    if not at_start(i):
                        for u in range(GS):
                            hold(dve, added[u], 16 * (g - 1))
                    ch.link(nc.vector.tensor_copy(index[:, b, :], dest[:]))
                    dve.sem_inc(index_ready[b], 1)

                    ch.end()
                nc.vector.tensor_scalar(ncol[:], keep.iota_col[:], float(NP), None, ALU.add)
                dve.wait_ge(lower_made, 2)
                passes(dve, half, group)


KQ = 3 * D


def mix_2(nc, keep, dram, ins, kvq):
    ctx = ExitStack()
    st = Stage(nc, ctx, "m2")
    HT = NW // 2
    with ctx:
        w01, wp, wq2 = st.sb("w01", [P, 2, D]), st.sb("wp", [P, 5 * D]), st.sb("wq2", [P, D])
        bias, cols = st.sb("bias", [P, 4 * D]), st.sb("cols", [P, 2])
        tab, side = st.sb("tab", [P, GS, 2, D]), st.sb("side", [P, 2, 2, D])
        sT, hT = st.sb("sT", [P, 4, P]), st.sb("hT", [P, 2, P])
        xt, h, hx = st.sb("xt", [P, 2, D]), st.sb("h", [P, 2, D]), st.sb("hx", [P, 2, D])
        h2 = st.sb("h2", [P, 2, D])
        q1, qT = st.sb("q1", [P, 2, D]), st.sb("qT", [P, 2, P])
        bt = st.sb("bt", [P, 2, 2 * D])
        stats, mv = st.sb("stats", [P, 2, 6]), st.sb("mv", [P, 2, 2])
        std, rstd = st.sb("std", [P, 2]), st.sb("rstd", [P, 2])
        ps_t, ps_o = st.ps("ps_t", [P, 4, P]), st.ps("ps_o", [P, 512])
        ps_p = st.ps("ps_p", [P, 2, 1024])
        ps_q = st.ps("ps_q", [P, 512])
        w_in, x_in, used = st.sem("w_in"), st.sem("x_in"), st.sem("used")
        side_ready, side_turned, sT_ready, mixed = st.sem("side_ready"), st.sem("side_turned"), st.sem("sT_ready"), st.sem("mixed")
        var_ready, std_ready, h_ready, h_turned = st.sem("var_ready"), st.sem("std_ready"), st.sem("h_ready"), st.sem("h_turned")
        hT_ready, projected, q1_ready, q1_turned = st.sem("hT_ready"), st.sem("projected"), st.sem("q1_ready"), st.sem("q1_turned")
        qT_ready, q_done, bt_ready, stored, v = st.sem("qT_ready"), st.sem("q_done"), st.sem("bt_ready"), st.sem("stored"), st.sem("v")
        dve_left = st.sem("dve_left")
        WL = [(w01[:], ins["L2_W"].rearrange("(c p) d -> p c d", p=P)), (wp[:], ins["L3_Wp"]), (wq2[:], ins["L3_gnn_hq_w2"]),
              (bias[:], ins["L3_brow"].partition_broadcast(P)), (cols[:], ins["L3_qcols"])]
        with nc.Block() as block:
            @block.sync
            def _(sp):
                for to, frm in WL:
                    sp.dma_start(to, frm).then_inc(w_in, 16)
                with sp.Fori(0, HT) as i:
                    sp.wait_ge(used, i + 1)
                    for u in range(GS):
                        sp.dma_start(tab[:, u], rows(dram.side[u], i)).then_inc(x_in, 16)
                    sp.dma_start(xt[:], rows(dram.x2, i)).then_inc(x_in, 16)
                    sp.dma_start(h2[:], rows(dram.h2, i)).then_inc(x_in, 16)

            @block.tensor
            def _(pe):
                pe.wait_ge(w_in, 16 * len(WL))
                with pe.Fori(0, HT) as i:
                    pe.wait_ge(side_ready, i + 1)
                    for j in range(4):
                        t = pe.transpose(ps_t[:, j, :], side[:, j // 2, j % 2, :], keep.ident[:])
                    t.then_inc(side_turned, 1)
                    pe.wait_ge(sT_ready, i + 1)
                    for u in range(2):
                        pe.matmul(ps_o[:, u * D:(u + 1) * D], sT[:, u, :], w01[:, 0, :], start=True, stop=False)
                        t = pe.matmul(ps_o[:, u * D:(u + 1) * D], sT[:, 2 + u, :], w01[:, 1, :], start=False, stop=True)
                    t.then_inc(mixed, 1)
                    pe.wait_ge(h_ready, i + 1)
                    for u in range(2):
                        t = pe.transpose(ps_t[:, u, :], h[:, u, :], keep.ident[:])
                    t.then_inc(h_turned, 1)
                    pe.wait_ge(hT_ready, i + 1)
                    for u in range(2):
                        pe.matmul(ps_p[:, u, 0:512], hT[:, u, :], wp[:, 0:512], start=True, stop=True)
                        t = pe.matmul(ps_p[:, u, 512:640], hT[:, u, :], wp[:, 512:640], start=True, stop=True)
                    t.then_inc(projected, 1)
                    pe.wait_ge(q1_ready, i + 1)
                    for u in range(2):
                        t = pe.transpose(ps_t[:, u, :], q1[:, u, :], keep.ident[:])
                    t.then_inc(q1_turned, 1)
                    pe.wait_ge(qT_ready, i + 1)
                    for u in range(2):
                        t = pe.matmul(ps_q[:, u * D:(u + 1) * D], qT[:, u, :], wq2[:], start=True, stop=True)
                    t.then_inc(q_done, 1)

            @block.scalar
            def _(act):
                act.wait_ge(w_in, 16 * len(WL))
                act.sem_inc(stored, 48)
                with act.Fori(0, HT) as i:
                    act.wait_ge(side_turned, i + 1)
                    nc.scalar.copy(sT[:], ps_t[:]).then_inc(sT_ready, 1)
                    act.wait_ge(var_ready, 2 * i + 1)
                    nc.scalar.activation(std[:], mv[:, :, 1], ACT.Sqrt, bias=keep.eps[:]).then_inc(std_ready, 1)
                    act.wait_ge(stored, 48 * (i + 1))
                    act.wait_ge(h_turned, i + 1)
                    nc.scalar.copy(hT[:], ps_t[:, 0:2, :]).then_inc(hT_ready, 1)
                    act.wait_ge(hT_ready, i + 1)
                    act.dma_start(dram.h3T[:, ds(i * 2 * P, 2 * P)].rearrange("f (w p) -> f w p", w=2), hT[:]
                                  ).then_inc(stored, 16)
                    act.wait_ge(dve_left, i + 1)
                    act.dma_start(rows(dram.hx, i), hx[:]).then_inc(stored, 16)
                    nc.scalar.copy(bt[:], ps_p[:, :, 2 * D:4 * D]).then_inc(bt_ready, 1)
                    act.wait_ge(bt_ready, i + 1)
                    act.dma_start(rows(dram.skv, i), bt[:]).then_inc(stored, 16)
                    act.wait_ge(var_ready, 2 * i + 2)
                    nc.scalar.activation(std[:], mv[:, :, 1], ACT.Sqrt, bias=keep.eps[:]).then_inc(std_ready, 1)
                    act.wait_ge(q1_turned, i + 1)
                    nc.scalar.activation(qT[:], ps_t[:, 0:2, :], ACT.Relu, bias=cols[:, 1:2], scale=cols[:, 0:1]
                                         ).then_inc(qT_ready, 1)
                act.wait_ge(stored, 48 * (HT + 1))

            @block.vector
            def _(dve):
                nc.vector.memset(kvq[:, NW * KQ:], 0.0)
                ch = Chain(dve, v, 22)
                dve.wait_ge(w_in, 16 * len(WL))
                dve.sem_inc(used, 1)
                with dve.Fori(0, HT) as i:
                    ch.start(i)
                    a = kvq[:, ds(i * 2 * KQ, 2 * KQ)].rearrange("p (w c) -> p w c", w=2)
                    dve.wait_ge(x_in, 16 * (GS + 2) * (i + 1))
                    ch.link(nc.vector.tensor_tensor(tab[:, 0:2], tab[:, 0:2], tab[:, 2:4], ALU.add))
                    ch.link(nc.vector.tensor_tensor(tab[:, 0], tab[:, 0], tab[:, 1], ALU.add))
                    for u in range(2):
                        ch.link(nc.vector.tensor_scalar(side[:, 0, u, :], tab[:, 0, u, :],
                                                        keep.dis[:, ds(2 * i + u, 1)], None, ALU.mult))
                    ch.link(nc.vector.tensor_tensor(side[:, 1], side[:, 0], h2[:], ALU.mult))
                    dve.sem_inc(side_ready, 1)
                    dve.wait_ge(mixed, i + 1)
                    ch.link(nc.vector.tensor_tensor(xt[:], xt[:], ps_o[:, 0:2 * D].rearrange("p (w d) -> p w d", w=2),
                                                    ALU.add), held=True)
                    layer_norm_statistics(nc, ch, xt, stats, mv, var_ready)
                    hold(dve, std_ready, 2 * i + 1)
                    layer_norm_apply(nc, ch, h, xt, mv, std, rstd)
                    dve.sem_inc(h_ready, 1)
                    dve.wait_ge(stored, 48 * (i + 1))
                    ch.link(nc.vector.tensor_tensor(hx[:], h[:], xt[:], ALU.add))
                    dve.sem_inc(used, 1)
                    dve.wait_ge(projected, i + 1)
                    ch.link(nc.vector.tensor_tensor(a[:, :, 0:2 * D], ps_p[:, :, 0:2 * D], bias[:, 0:2 * D].unsqueeze(1)
                                                    .broadcast_to([P, 2, 2 * D]), ALU.add))
                    ch.link(nc.vector.tensor_tensor(q1[:], ps_p[:, :, 4 * D:5 * D], bias[:, 2 * D:3 * D].unsqueeze(1)
                                                    .broadcast_to([P, 2, D]), ALU.add), held=True)
                    dve.sem_inc(dve_left, 1)
                    layer_norm_statistics(nc, ch, q1, stats, mv, var_ready)
                    hold(dve, std_ready, 2 * i + 2)
                    layer_norm_apply(nc, ch, q1, q1, mv, std, rstd, relu=False)
                    dve.sem_inc(q1_ready, 1)
                    dve.wait_ge(q_done, i + 1)
                    ch.link(nc.vector.tensor_tensor(q1[:], ps_q[:, 0:2 * D].rearrange("p (w d) -> p w d", w=2),
                                                    bias[:, 3 * D:4 * D].unsqueeze(1).broadcast_to([P, 2, D]), ALU.add))
                    ch.link(nc.vector.tensor_scalar(a[:, :, 2 * D:KQ], q1[:], float(DH3) ** -0.5, None, ALU.mult))
                    ch.end()


G3 = 2
U3 = 4
LW = NH3 + 1


def done(eng, sem, i, b, lag=0, per=1):
    g = U3 * i + b
    if isinstance(i, int) and g < lag:
        return
    eng.wait_ge(sem, (g - lag + 1) * per)


def ahead(i, b, n, count):
    if b + n < U3:
        return i, b + n
    return None if isinstance(i, int) and i == count - 1 else (i + 1, b + n - U3)


def passes_of_4(eng, count, group):
    for b in range(U3):
        group(0, b)
    with eng.Fori(1, count - 1) as i:
        for b in range(U3):
            group(i, b)
    for b in range(U3):
        group(count - 1, b)


def edges_3(nc, keep, dram, ins, kvq):
    ctx = ExitStack()
    st = Stage(nc, ctx, "e3")
    QC, GC = 2 * D, 3 * D
    with ctx:
        wa, w2 = st.sb("wa", [P, 2 * D + 1]), st.sb("w2", [P, 2, D])
        cols, bias = st.sb("cols", [P, 4]), st.sb("bias", [P, 2 * D])
        dlr = st.sb("dlr", [P, U3, G3 * P], BF16)
        spread = st.sb("spread", [P, U3, G3 * P])
        attr = st.sb("attr", [P, U3, G3, P])
        gidx = st.sb("gidx", [P, U3, G3], I32)
        skv = st.sb("skv", [P, U3, G3, 2 * D])
        xs, xn = st.sb("xs", [P, G3, 2 * D]), st.sb("xn", [P, G3, 2 * D])
        stats, mv = st.sb("stats", [P, 2 * G3, 6]), st.sb("mv", [P, 2 * G3, 2])
        std, rstd = st.sb("std", [P, 2 * G3]), st.sb("rstd", [P, 2 * G3])
        hT = st.sb("hT", [P, 2, 2, G3, P])
        kvo = st.sb("kvo", [P, 2, G3, 2 * D])
        prod = st.sb("prod", [P, G3, D])
        lg = st.sb("lg", [P, 2, G3, LW])
        ps_h = st.ps("ps_h", [P, 2, G3, 2 * D])
        ps_t = st.ps("ps_t", [P, 2, 2, G3, P])
        ps_o = st.ps("ps_o", [P, 2, G3, 512])
        w_in = st.sem("w_in")
        dlr_in, attr_in = [st.sem(f"dlr_in{b}") for b in range(U3)], [st.sem(f"attr_in{b}") for b in range(U3)]
        skv_in, idx_ready = [st.gather_sem(f"skv_in{b}") for b in range(U3)], st.sem("idx_ready")
        spread_ready, hidden, queried = st.sem("spread_ready"), st.sem("hidden"), st.sem("queried")
        xs_ready, stats_ready = st.sem("xs_ready"), st.sem("stats_ready")
        var_ready, std_ready, rstd_ready = st.sem("var_ready"), st.sem("std_ready"), st.sem("rstd_ready")
        xn_ready, turned, hT_ready = st.sem("xn_ready"), st.sem("turned"), st.sem("hT_ready")
        product2, kvo_ready = st.sem("product2"), st.sem("kvo_ready")
        prod_ready, lg_ready = st.sem("prod_ready"), st.sem("lg_ready")
        stored = [st.sem(f"stored{b}") for b in range(2)]
        count = NS // G3 // U3
        WL = [(wa[0:KA, :], ins["L3_Wa"]), (w2[:], ins["L3_W2"].rearrange("(c p) d -> p c d", p=P)),
              (cols[:], ins["L3_kvcols"]), (bias[:], ins["L3_kvrow"].partition_broadcast(P))]

        with nc.Block() as block:
            @block.sync
            def _(sp):
                for to, frm in WL:
                    sp.dma_start(to, frm).then_inc(w_in, 16)
                sp.wait_ge(dram.attr_copied, 16)
                tiles = Numbers(sp, dram.tk[0:1, :], NT - 1, "e3_sp", G3)

                def load(i, b):
                    g = U3 * i + b
                    ts = tiles.load(g)
                    done(sp, queried, i, b, lag=U3)
                    sp.dma_start(dlr[:, b, :], dram.dlrow.rearrange("s e -> (s e)")[ds(g * G3 * P, G3 * P)]
                                 .partition_broadcast(P)).then_inc(dlr_in[b], 16)
                    for u in range(G3):
                        sp.dma_start(attr[0:KA, b, u, :], dram.attr[:, ds(ts[u] * P, P)]).then_inc(attr_in[b], 16)

                def store(i, b):
                    g = U3 * i + b
                    done(sp, lg_ready, i, b)
                    sp.dma_start(dram.lg[ds(g * G3 * P, G3 * P), :].rearrange("(u p) c -> p u c", p=P), lg[:, b % 2]
                                 ).then_inc(stored[b % 2], 16)
                    sp.dma_start(dram.v[ds(g * G3 * P, G3 * P), :].rearrange("(u p) c -> p u c", p=P),
                                 kvo[:, b % 2, :, D:2 * D]).then_inc(stored[b % 2], 16)

                def group(i, b):
                    nxt = ahead(i, b, 3, count)
                    if nxt:
                        load(*nxt)
                    if b > 0:
                        store(i, b - 1)
                    elif not at_start(i):
                        store(i - 1, U3 - 1)
                for b in range(3):
                    load(0, b)
                passes_of_4(sp, count, group)
                store(count - 1, U3 - 1)
                for s in stored:
                    sp.wait_ge(s, 32 * NS // G3 // 2)

            @block.gpsimd
            def _(pool):
                def group(i, b):
                    g = U3 * i + b
                    if not at_start(i):
                        hold(pool, xs_ready, g - U3 + 1)
                    nc.gpsimd.tensor_copy(gidx[:, b, :], keep.src[:, ds(g * G3, G3)]).then_inc(idx_ready, 1)
                    hold(pool, idx_ready, g + 1)
                    for u in range(G3):
                        pool.indirect_dma_start(
                            out=skv[:, b, u, :], out_offset=None, in_=dram.skv,
                            in_offset=bass.IndirectOffsetOnAxis(ap=gidx[:, b, u:u + 1], axis=0)).then_inc(skv_in[b], 16)
                passes_of_4(pool, count, group)

            @block.tensor
            def _(pe):
                windows_h = Numbers(pe, keep.window, NW, "e3_pe_h", G3)
                windows_q = Numbers(pe, keep.window, NW, "e3_pe_q", G3)
                pe.wait_ge(w_in, 16 * len(WL))

                def hidden_sums(i, b):
                    ks = windows_h.load(U3 * i + b)
                    done(pe, spread_ready, i, b)
                    pe.wait_ge(attr_in[b], 16 * G3 * (i + 1))
                    done(pe, xs_ready, i, b, lag=2)
                    for u in range(G3):
                        pe.matmul(ps_h[:, b % 2, u, :], attr[0:KA, b, u, :], wa[0:KA, 0:2 * D], start=True, stop=False)
                        t = pe.matmul(ps_h[:, b % 2, u, :], spread[:, b, u * P:(u + 1) * P],
                                      kvq[:, ds(ks[u] * KQ, 2 * D)], start=False, stop=True)
                    t.then_inc(hidden, 1)

                def queries(i, b):
                    ks = windows_q.load(U3 * i + b)
                    done(pe, prod_ready, i, b, lag=2)
                    for u in range(G3):
                        pe.matmul(ps_o[:, b % 2, u, QC:QC + D], spread[:, b, u * P:(u + 1) * P],
                                  kvq[:, ds(ks[u] * KQ + 2 * D, D)], start=True, stop=True)
                        t = pe.matmul(ps_o[:, b % 2, u, GC:GC + 1], attr[0:KA, b, u, :], wa[0:KA, 2 * D:2 * D + 1],
                                      start=True, stop=True)
                    t.then_inc(queried, 1)

                def group(i, b):
                    done(pe, xn_ready, i, b)
                    done(pe, hT_ready, i, b, lag=2)
                    for c in range(2):
                        for u in range(G3):
                            t = pe.transpose(ps_t[:, b % 2, c, u, :], xn[:, u, c * D:(c + 1) * D], keep.ident[:])
                    t.then_inc(turned, 1)
                    nxt = ahead(i, b, 2, count)
                    if nxt:
                        hidden_sums(*nxt)
                    nxt = ahead(i, b, 1, count)
                    if nxt:
                        queries(*nxt)
                    done(pe, hT_ready, i, b)
                    for u in range(G3):
                        for c in range(2):
                            t = pe.matmul(ps_o[:, b % 2, u, c * D:(c + 1) * D], hT[:, b % 2, c, u, :], w2[:, c, :],
                                          start=True, stop=True)
                    t.then_inc(product2, 1)

                hidden_sums(0, 0)
                hidden_sums(0, 1)
                queries(0, 0)
                passes_of_4(pe, count, group)

            @block.scalar
            def _(act):
                act.wait_ge(w_in, 16 * len(WL))

                def group(i, b):
                    done(act, var_ready, i, b)
                    done(act, rstd_ready, i, b, lag=1)
                    nc.scalar.activation(std[:], mv[:, :, 1], ACT.Sqrt, bias=keep.eps[:]).then_inc(std_ready, 1)
                    done(act, turned, i, b)
                    done(act, product2, i, b, lag=2)
                    for c in range(2):
                        t = nc.scalar.activation(hT[:, b % 2, c], ps_t[:, b % 2, c], ACT.Relu,
                                                 bias=cols[:, 2 * c + 1:2 * c + 2], scale=cols[:, 2 * c:2 * c + 1])
                    t.then_inc(hT_ready, 1)
                passes_of_4(act, count, group)

            @block.vector
            def _(dve):
                dve.wait_ge(w_in, 16 * len(WL))

                def make_spread(i, b):
                    dve.wait_ge(dlr_in[b], 16 * (i + 1))
                    done(dve, queried, i, b, lag=U3)
                    nc.vector.tensor_scalar(spread[:, b, :], dlr[:, b, :], keep.iota_col[:, 0:1], None,
                                            ALU.is_equal).then_inc(spread_ready, 1)

                def finish(i, b):
                    done(dve, product2, i, b)
                    if not (at_start(i) and b < 2):
                        dve.wait_ge(stored[b % 2], 32 * (2 * i + b // 2))
                    nc.vector.tensor_tensor(kvo[:, b % 2], ps_o[:, b % 2, :, 0:2 * D],
                                            bias[:].unsqueeze(1).broadcast_to([P, G3, 2 * D]), ALU.add
                                            ).then_inc(kvo_ready, 1)
                    done(dve, kvo_ready, i, b)
                    done(dve, lg_ready, i, b, lag=1)
                    nc.vector.tensor_copy(lg[:, b % 2, :, NH3:LW], ps_o[:, b % 2, :, GC:GC + 1])
                    nc.vector.tensor_tensor(prod[:], kvo[:, b % 2, :, 0:D], ps_o[:, b % 2, :, QC:QC + D],
                                            ALU.mult).then_inc(prod_ready, 1)
                    done(dve, prod_ready, i, b)
                    nc.vector.tensor_reduce(lg[:, b % 2, :, 0:NH3], prod[:].rearrange("p u (h e) -> p u h e", e=DH3),
                                            AX, ALU.add).then_inc(lg_ready, 1)

                def group(i, b):
                    g = U3 * i + b
                    done(dve, hidden, i, b)
                    dve.wait_ge(skv_in[b], 16 * G3 * (i + 1))
                    done(dve, xn_ready, i, b, lag=1)
                    nc.vector.tensor_tensor(xs[:], skv[:, b], ps_h[:, b % 2], ALU.add).then_inc(xs_ready, 1)
                    hold(dve, xs_ready, g + 1)
                    for j in range(2 * G3):
                        t = nc.vector.bn_stats(stats[:, j, :], xs[:, j // 2, (j % 2) * D:(j % 2 + 1) * D])
                    t.then_inc(stats_ready, 1)
                    hold(dve, stats_ready, g + 1)
                    for j in range(2 * G3):
                        t = nc.vector.bn_aggr(mv[:, j, :], stats[:, j, :])
                    t.then_inc(var_ready, 1)
                    nxt = ahead(i, b, 2, count)
                    if nxt:
                        make_spread(*nxt)
                    done(dve, std_ready, i, b)
                    nc.vector.reciprocal(rstd[:], std[:]).then_inc(rstd_ready, 1)
                    done(dve, rstd_ready, i, b)
                    done(dve, turned, i, b, lag=1)
                    for j in range(2 * G3):
                        t = nc.vector.tensor_scalar(xn[:, j // 2, (j % 2) * D:(j % 2 + 1) * D],
                                                    xs[:, j // 2, (j % 2) * D:(j % 2 + 1) * D],
                                                    mv[:, j, 0:1], rstd[:, j:j + 1], ALU.subtract, ALU.mult)
                    t.then_inc(xn_ready, 1)
                    if b > 0:
                        finish(i, b - 1)
                    elif not at_start(i):
                        finish(i - 1, U3 - 1)

                make_spread(0, 0)
                make_spread(0, 1)
                passes_of_4(dve, count, group)
                finish(count - 1, U3 - 1)


def softmax_3(nc, keep, dram, ins):
    ctx = ExitStack()
    st = Stage(nc, ctx, "sm")
    HH = NH3 // 2
    with ctx:
        L = st.sb("L", [P, NS, LW])
        M = st.sb("M", [P, NS * HH])
        wall = st.sb("wall", [P, NS + 1])
        edge, edgeT = st.sb("edge", [P, 2, HH]), st.sb("edgeT", [HH, 2, P])
        run, carry = st.sb("run", [HH, P + 1]), st.sb("carry", [P, HH])
        gate = st.sb("gate", [P, 1])
        ps_e, ps_c = st.ps("ps_e", [P, 512]), st.ps("ps_c", [P, 512])
        loaded, v = st.sem("loaded"), st.sem("v")
        cur_used, prev_in = st.sem("cur_used"), st.sem("prev_in")
        edges_ready, edges_turned, run_ready, carry_turned = (st.sem("edges_ready"), st.sem("edges_turned"),
                                                              st.sem("run_ready"), st.sem("carry_turned"))
        shifted, exped, gated, stored = st.sem("shifted"), st.sem("exped"), st.sem("gated"), st.sem("stored")
        l_in = st.sem("l_in")

        def halo(flat, off):
            return bass.AP(tensor=flat.tensor, offset=flat.offset + off, ap=[[NS, P], [1, NS + 1]])

        dstf = dram.dstflat
        dlf = dram.dlflat.rearrange("s e -> (s e)")
        cur = M[:, 0:NS + 1]
        prv = M[:, 2 * NS:3 * NS + 1]
        out_of = M[:, 4 * NS:5 * NS + 1]
        with nc.Block() as block:
            @block.sync
            def _(sp):
                sp.dma_start(out_of, halo(dlf, 0)).then_inc(loaded, 16)
                sp.dma_start(cur, halo(dstf, 1)).then_inc(loaded, 16)
                sp.dma_start(prv, halo(dstf, 0)).then_inc(loaded, 16)
                sp.dma_start(gate[:], ins["L3_gnn_ew_b"].partition_broadcast(P)).then_inc(loaded, 16)
                sp.dma_start(L[:], dram.lg.rearrange("(p e) c -> p e c", p=P)).then_inc(l_in, 16)
                sp.wait_ge(exped, 1)
                sp.wait_ge(gated, 1)
                sp.dma_start(dram.lg.rearrange("(p e) c -> p e c", p=P), L[:]).then_inc(stored, 16)
                sp.wait_ge(stored, 16)

            @block.scalar
            def _(act):
                act.wait_ge(loaded, 64)
                act.wait_ge(l_in, 16)
                nc.scalar.activation(L[:, :, NH3], L[:, :, NH3], ACT.Sigmoid, bias=gate[:]).then_inc(gated, 1)
                act.wait_ge(shifted, 2)
                nc.scalar.activation(L[:, :, 0:NH3], L[:, :, 0:NH3], ACT.Exp).then_inc(exped, 1)

            @block.tensor
            def _(pe):
                for n in range(4):
                    pe.wait_ge(edges_ready, n + 1)
                    for j in range(2):
                        t = pe.transpose(ps_e[0:HH, j * P:(j + 1) * P], edge[:, j, :], keep.ident[:])
                    t.then_inc(edges_turned, 1)
                    pe.wait_ge(run_ready, n + 1)
                    back = run[:, 0:P] if n % 2 == 0 else run[:, 1:P + 1]
                    pe.transpose(ps_c[:, 0:HH], back, keep.ident[0:HH, 0:HH]).then_inc(carry_turned, 1)

            @block.vector
            def _(dve):
                n = [0]

                def link(ins_):
                    n[0] += 1
                    ins_.then_inc(v, 1)
                    dve.wait_ge(v, n[0])

                dve.wait_ge(loaded, 64)
                link(nc.vector.tensor_scalar(wall[:], out_of, 0.0, None, ALU.is_ge))
                link(nc.vector.tensor_scalar(out_of, out_of, float(P - 1), None, ALU.is_le))
                link(nc.vector.tensor_tensor(out_of, out_of, wall[:], ALU.mult))
                link(nc.vector.tensor_tensor(wall[:], cur, prv, ALU.not_equal))
                link(nc.vector.tensor_tensor(wall[:], wall[:], out_of, ALU.mult))
                link(nc.vector.tensor_scalar(wall[:], wall[:], -BIG, None, ALU.mult))
                link(nc.vector.tensor_scalar(out_of, out_of, -1.0, BIG, ALU.add, ALU.mult))
                dve.wait_ge(l_in, 16)
                link(nc.vector.tensor_tensor(L[:, :, 0:NH3], L[:, :, 0:NH3],
                                             out_of[:, 0:NS].unsqueeze(2).broadcast_to([P, NS, NH3]), ALU.add))
                turn = [0]

                def cross(reverse, mh):
                    end = 0 if reverse else NS - 1
                    link(nc.vector.tensor_copy(edge[:, 0, :], mh[:, end, :]))
                    walls = wall[:, 1:NS + 1] if reverse else wall[:, 0:NS]
                    link(nc.vector.tensor_reduce(edge[:, 1, 0:1], walls, AX, ALU.min))
                    nc.vector.tensor_copy(edge[:, 1, 1:HH], edge[:, 1, 0:1].broadcast_to([P, HH - 1])
                                          ).then_inc(edges_ready, 1)
                    turn[0] += 1
                    dve.wait_ge(edges_turned, turn[0])
                    link(nc.vector.tensor_copy(edgeT[:], ps_e[0:HH, 0:2 * P].rearrange("p (j e) -> p j e", j=2)))
                    link(nc.vector.memset(run[:], -BIG))
                    if reverse:
                        t = nc.vector.tensor_tensor_scan(run[:, 0:P][:, ::-1], edgeT[:, 1, ::-1], edgeT[:, 0, ::-1],
                                                         -BIG, ALU.add, ALU.max)
                    else:
                        t = nc.vector.tensor_tensor_scan(run[:, 1:P + 1], edgeT[:, 1, :], edgeT[:, 0, :], -BIG,
                                                         ALU.add, ALU.max)
                    t.then_inc(run_ready, 1)
                    dve.wait_ge(carry_turned, turn[0])
                    link(nc.vector.tensor_copy(carry[:], ps_c[:, 0:HH]))

                for half in range(2):
                    mh = M[:].rearrange("p (e h) -> p e h", h=HH)
                    lh = L[:, :, half * HH:(half + 1) * HH]

                    def forward(initial):
                        for h in range(HH):
                            link(nc.vector.tensor_tensor_scan(mh[:, :, h], wall[:, 0:NS], lh[:, :, h], initial(h),
                                                              ALU.add, ALU.max))

                    def backward(initial):
                        for h in range(HH):
                            link(nc.vector.tensor_tensor_scan(mh[:, ::-1, h], wall[:, 1:NS + 1][:, ::-1],
                                                              mh[:, ::-1, h], initial(h), ALU.add, ALU.max))

                    forward(lambda h: -BIG)
                    cross(False, mh)
                    forward(lambda h: carry[:, h:h + 1])
                    backward(lambda h: -BIG)
                    cross(True, mh)
                    backward(lambda h: carry[:, h:h + 1])
                    link(nc.vector.tensor_tensor(lh, lh, mh, ALU.subtract))
                    dve.sem_inc(shifted, 1)


def edges_3_sums(nc, keep, dram, nodes):
    ctx = ExitStack()
    st = Stage(nc, ctx, "s3")
    with ctx:
        B = range(2)
        collect = st.sb("collect", [P, 2, GS, P])
        vin, lin = st.sb("vin", [P, 2, GS, D]), st.sb("lin", [P, 2, GS, LW])
        wgt = st.sb("wgt", [P, GS, NH3])
        vals = st.sb("vals", [P, 2, GS, AC3])
        ps_a = st.ps("ps_a", [P, 2, GS, 256])
        v_in = [st.sem(f"v_in{b}") for b in B]
        wgt_ready, vals_ready = st.sem("wgt_ready"), [st.sem(f"vals_ready{b}") for b in B]
        summed, added = [st.sem(f"summed{b}") for b in B], st.sem("added")
        half = NS // GS // 2
        with nc.Block() as block:
            @block.sync
            def _(sp):
                def group(i, b, nxt):
                    if not at_start(i):
                        sp.wait_ge(vals_ready[b], i)
                    sl = ds((2 * i + b) * GS * P, GS * P)
                    sp.dma_start(vin[:, b], dram.v[sl, :].rearrange("(u p) c -> p u c", p=P)).then_inc(v_in[b], 16)
                    sp.dma_start(lin[:, b], dram.lg[sl, :].rearrange("(u p) c -> p u c", p=P)).then_inc(v_in[b], 16)
                passes(sp, half, group)

            @block.tensor
            def _(pe):
                def group(i, b, nxt):
                    pe.wait_ge(vals_ready[b], i + 1)
                    if not at_start(i):
                        pe.wait_ge(added, (2 * i + b - 1) * GS + 1)
                    for u in range(GS):
                        t = pe.matmul(ps_a[:, b, u, 0:AC3], collect[:, b, u, :], vals[:, b, u, :], start=True, stop=True)
                    t.then_inc(summed[b], 1)
                passes(pe, half, group)

            @block.vector
            def _(dve):
                windows = Numbers(dve, keep.window, NW, "s3_dve")

                def add_sums(i, b):
                    ks = windows.load(2 * i + b)
                    dve.wait_ge(summed[b], i + 1)
                    for u in range(GS):
                        a = nodes[:, ds(ks[u] * AC3, AC3)]
                        dve.wait_ge(added, (2 * i + b) * GS + u + 1)
                        nc.vector.tensor_tensor(a, a, ps_a[:, b, u, 0:AC3], ALU.add).then_inc(added, 1)

                def group(i, b, nxt):
                    g = 2 * i + b
                    dve.wait_ge(v_in[b], 32 * (i + 1))
                    if not (at_start(i) and b == 0):
                        dve.wait_ge(vals_ready[1 - b], i + b)
                    nc.vector.tensor_tensor(wgt[:], lin[:, b, :, 0:NH3], lin[:, b, :, NH3:LW]
                                            .broadcast_to([P, GS, NH3]), ALU.mult).then_inc(wgt_ready, 1)
                    if not at_start(i):
                        dve.wait_ge(summed[b], i)
                    nc.vector.tensor_tensor(
                        collect[:, b], keep.iota_row[:].unsqueeze(1).broadcast_to([P, GS, P]),
                        keep.dl[:, ds(g * GS, GS)].unsqueeze(2).broadcast_to([P, GS, P]), ALU.is_equal)
                    nc.vector.tensor_copy(vals[:, b, :, D:AC3], lin[:, b, :, 0:NH3])
                    dve.wait_ge(wgt_ready, g + 1)
                    nc.vector.tensor_tensor(
                        vals[:, b, :, 0:D].rearrange("p u (h e) -> p u h e", e=DH3),
                        vin[:, b].rearrange("p u (h e) -> p u h e", e=DH3),
                        wgt[:].unsqueeze(3).broadcast_to([P, GS, NH3, DH3]), ALU.mult).then_inc(vals_ready[b], 1)
                    if b == 1:
                        add_sums(i, 0)
                    elif not at_start(i):
                        add_sums(i - 1, 1)

                nc.vector.memset(nodes[:], 0.0).then_inc(added, 1)
                passes(dve, half, group)
                add_sums(half - 1, 1)


def mix_3(nc, keep, dram, ins, nodes, out):
    ctx = ExitStack()
    st = Stage(nc, ctx, "m3")
    HT = NW // 2
    with ctx:
        w1, w2 = st.sb("w1", [P, 2, D]), st.sb("w2", [P, D])
        bias, cols = st.sb("bias", [P, 2 * D]), st.sb("cols", [P, 2])
        den, rec = st.sb("den", [P, 2, NH3]), st.sb("rec", [P, 2, NH3])
        at, aT, hT = st.sb("at", [P, 2, D]), st.sb("aT", [P, 2, P]), st.sb("hT", [P, 2, 2, P])
        hx, y, yT = st.sb("hx", [P, 2, 2, D]), st.sb("y", [P, 2, D]), st.sb("yT", [P, 2, P])
        stats, mv = st.sb("stats", [P, 2, 6]), st.sb("mv", [P, 2, 2])
        std, rstd = st.sb("std", [P, 2]), st.sb("rstd", [P, 2])
        ps_t, ps_o, ps_u = st.ps("ps_t", [P, 4, P]), st.ps("ps_o", [P, 512]), st.ps("ps_u", [P, 512])
        w_in, in_, used, at_ready, at_turned = st.sem("w_in"), st.sem("in"), st.sem("used"), st.sem("at_ready"), st.sem("at_turned")
        aT_ready, hidden, var_ready, std_ready = st.sem("aT_ready"), st.sem("hidden"), st.sem("var_ready"), st.sem("std_ready")
        y_ready, y_turned, yT_ready, done, v = st.sem("y_ready"), st.sem("y_turned"), st.sem("yT_ready"), st.sem("done"), st.sem("v")
        out_ready, stored = st.sem("out_ready"), st.sem("stored")
        WL = [(w1[:], ins["L3_gnn_no_w1"].rearrange("(c p) d -> p c d", p=P)), (w2[:], ins["L3_gnn_no_w2"]),
              (bias[:], ins["L3_norow"].partition_broadcast(P)), (cols[:], ins["L3_nocols"])]
        with nc.Block() as block:
            @block.sync
            def _(sp):
                for to, frm in WL:
                    sp.dma_start(to, frm).then_inc(w_in, 16)
                with sp.Fori(0, HT) as i:
                    sp.wait_ge(used, i + 1)
                    sp.dma_start(hT[:, 0], dram.h3T[:, ds(i * 2 * P, 2 * P)].rearrange("f (w p) -> f w p", w=2)
                                 ).then_inc(in_, 16)
                    sp.dma_start(hx[:, 0], rows(dram.hx, i)).then_inc(in_, 16)

            @block.tensor
            def _(pe):
                pe.wait_ge(w_in, 16 * len(WL))
                with pe.Fori(0, HT) as i:
                    pe.wait_ge(at_ready, i + 1)
                    for u in range(2):
                        t = pe.transpose(ps_t[:, u, :], at[:, u, :], keep.ident[:])
                    t.then_inc(at_turned, 1)
                    pe.wait_ge(aT_ready, i + 1)
                    pe.wait_ge(in_, 32 * (i + 1))
                    for u in range(2):
                        pe.matmul(ps_o[:, u * D:(u + 1) * D], aT[:, u, :], w1[:, 0, :], start=True, stop=False)
                        t = pe.matmul(ps_o[:, u * D:(u + 1) * D], hT[:, 0, u, :], w1[:, 1, :], start=False, stop=True)
                    t.then_inc(hidden, 1)
                    pe.wait_ge(y_ready, i + 1)
                    for u in range(2):
                        t = pe.transpose(ps_t[:, 2 + u, :], y[:, u, :], keep.ident[:])
                    t.then_inc(y_turned, 1)
                    pe.wait_ge(yT_ready, i + 1)
                    for u in range(2):
                        t = pe.matmul(ps_u[:, u * D:(u + 1) * D], yT[:, u, :], w2[:], start=True, stop=True)
                    t.then_inc(done, 1)

            @block.scalar
            def _(act):
                act.wait_ge(w_in, 16 * len(WL))
                act.sem_inc(stored, 16)
                with act.Fori(0, HT) as i:
                    act.wait_ge(at_turned, i + 1)
                    nc.scalar.copy(aT[:], ps_t[:, 0:2]).then_inc(aT_ready, 1)
                    act.wait_ge(var_ready, i + 1)
                    nc.scalar.activation(std[:], mv[:, :, 1], ACT.Sqrt, bias=keep.eps[:]).then_inc(std_ready, 1)
                    act.wait_ge(y_turned, i + 1)
                    nc.scalar.activation(yT[:], ps_t[:, 2:4], ACT.Relu, bias=cols[:, 1:2], scale=cols[:, 0:1]
                                         ).then_inc(yT_ready, 1)
                    act.wait_ge(out_ready, i + 1)
                    act.dma_start(rows(out, i), hx[:, 1]).then_inc(stored, 16)
                act.wait_ge(stored, 16 * (HT + 1))

            @block.vector
            def _(dve):
                ch = Chain(dve, v, 2 + 1 + 2 + 3 + 2)
                dve.wait_ge(w_in, 16 * len(WL))
                dve.sem_inc(used, 1)
                with dve.Fori(0, HT) as i:
                    ch.start(i)
                    w = nodes[:, ds(i * 2 * AC3, 2 * AC3)].rearrange("p (w c) -> p w c", w=2)
                    ch.link(nc.vector.tensor_scalar(den[:], w[:, :, D:AC3], 1e-30, None, ALU.max))
                    ch.link(nc.vector.reciprocal(rec[:], den[:]))
                    nc.vector.tensor_tensor(at[:].rearrange("p w (h e) -> p w h e", e=DH3),
                                            w[:, :, 0:D].rearrange("p w (h e) -> p w h e", e=DH3),
                                            rec[:].unsqueeze(3).broadcast_to([P, 2, NH3, DH3]),
                                            ALU.mult).then_inc(at_ready, 1)
                    dve.wait_ge(hidden, i + 1)
                    ch.link(nc.vector.tensor_tensor(y[:], ps_o[:, 0:2 * D].rearrange("p (w d) -> p w d", w=2),
                                                    bias[:, 0:D].unsqueeze(1).broadcast_to([P, 2, D]), ALU.add), held=True)
                    layer_norm_statistics(nc, ch, y, stats, mv, var_ready)
                    hold(dve, std_ready, i + 1)
                    layer_norm_apply(nc, ch, y, y, mv, std, rstd, relu=False)
                    dve.sem_inc(y_ready, 1)
                    dve.wait_ge(done, i + 1)
                    dve.wait_ge(stored, 16 * (i + 1))
                    ch.link(nc.vector.tensor_tensor(hx[:, 1], hx[:, 0], bias[:, D:2 * D].unsqueeze(1)
                                                    .broadcast_to([P, 2, D]), ALU.add))
                    ch.link(nc.vector.tensor_tensor(hx[:, 1], hx[:, 1], ps_u[:, 0:2 * D]
                                                    .rearrange("p (w d) -> p w d", w=2), ALU.add))
                    dve.sem_inc(out_ready, 1)
                    dve.sem_inc(used, 1)
                    ch.end()


def order_edges(nc, keep, dram, ins):
    flag = keep.unordered
    ctx = ExitStack()
    st = Stage(nc, ctx, "ord")
    HI = NW
    tables = [("src", dram.src), ("dst", dram.dst), ("edge_type_16", dram.et), ("edge_weight", dram.ew)]
    with ctx:
        run_, nxt = st.sb("run", [P, NT], I32), st.sb("next", [P, 1], I32)
        runf, nxtf = st.sb("runf", [P, NT]), st.sb("nxtf", [P, 1])
        bad, worst = st.sb("bad", [P, NT]), st.sb("worst", [P, 1])
        ones = st.sb("ones", [P, P])
        ps_f = st.ps("ps_f", [P, 512])
        loaded, v, worst_ready = st.sem("loaded"), st.sem("v"), st.sem("worst_ready")
        bad_summed = st.sem("bad_summed")
        with nc.Block() as block:
            @block.sync
            def _(sp):
                sp.dma_start(run_[:], ins["dst"].rearrange("(p t) -> p t", p=P)).then_inc(loaded, 16)
                sp.dma_start(nxt[0:P - 1, :], ins["dst"].rearrange("(p t) -> p t", p=P)[1:P, 0:1],
                             allow_slow_non_contiguous=True).then_inc(loaded, 16)

            @block.tensor
            def _(pe):
                pe.wait_ge(worst_ready, 1)
                pe.matmul(ps_f[:, 0:1], ones[:], worst[:], start=True, stop=True).then_inc(bad_summed, 1)

            @block.vector
            def _(dve):
                n = [0]

                def link(ins_):
                    n[0] += 1
                    ins_.then_inc(v, 1)
                    dve.wait_ge(v, n[0])

                link(nc.vector.memset(ones[:], 1.0))
                link(nc.vector.memset(nxtf[:], float(NP)))
                dve.wait_ge(loaded, 32)
                link(nc.vector.tensor_copy(runf[:], run_[:]))
                link(nc.vector.tensor_copy(nxtf[0:P - 1, :], nxt[0:P - 1, :]))
                link(nc.vector.tensor_tensor(bad[:, 0:NT - 1], runf[:, 0:NT - 1], runf[:, 1:NT], ALU.is_gt))
                link(nc.vector.tensor_tensor(bad[:, NT - 1:NT], runf[:, NT - 1:NT], nxtf[:], ALU.is_gt))
                nc.vector.tensor_reduce(worst[:], bad[:], AX, ALU.max).then_inc(worst_ready, 1)
                dve.wait_ge(bad_summed, 1)
                link(nc.vector.tensor_scalar(nxtf[0:1, :], ps_f[0:1, 0:1], 1.0, None, ALU.min))
                link(nc.vector.tensor_copy(flag[:], nxtf[0:1, :]))

    ctx = ExitStack()
    st = Stage(nc, ctx, "sort")
    with ctx:
        key, pos = st.sb("key", [P, 1], I32), st.sb("pos", [P, 1], I32)
        hii = st.sb("hii", [P, 1], I32)
        kf, hif, lof = st.sb("kf", [P, 1]), st.sb("hif", [P, 1]), st.sb("lof", [P, 1])
        lo, hi = st.sb("lo", [P, P]), st.sb("hi", [P, HI])
        loT, hiT = st.sb("loT", [P, P]), st.sb("hiT", [HI, P])
        table, tot, incl, zero = st.sb("table", [P, HI]), st.sb("tot", [P, HI]), st.sb("incl", [P, HI]), st.sb("zero", [P, HI])
        ones, lower = st.sb("ones", [P, P]), st.sb("lower", [P, P])
        sel, eq = st.sb("sel", [P, HI]), st.sb("eq", [P, P])
        bef, rank = st.sb("bef", [P, 1]), st.sb("rank", [P, 1])
        rec = st.sb("rec", [P, 4], I32)
        acol, arow = st.sb("acol", [KA, P]), st.sb("arow", [P, KA])
        ps_c, ps_t, ps_u = st.ps("ps_c", [P, 512]), st.ps("ps_t", [P, 512]), st.ps("ps_u", [P, 512])
        ps_r, ps_lo, ps_hi = st.ps("ps_r", [P, 512]), st.ps("ps_lo", [P, 512]), st.ps("ps_hi", [P, 512])
        key_in, hot1, count1, v1 = st.sem("key_in"), st.sem("hot1"), st.sem("count1"), st.sem("v1")
        pref, v2, v3, base = st.sem("pref"), st.sem("v2"), st.sem("v3"), st.sem("base")
        rec_in, hot2, turned, copied, counted = (st.sem("rec_in"), st.sem("hot2"), st.sem("turned"), st.sem("copied"),
                                                 st.sem("counted"))
        pos_ready, made = st.sem("pos_ready"), st.sem("made")
        back_in, back_turned, back_ready, back_out = (st.sem("back_in"), st.sem("back_turned"), st.sem("back_ready"),
                                                      st.sem("back_out"))
        cols_out = st.sem("cols_out")
        placed = st.gather_sem("placed")
        dram.attr_copied = st.gather_sem("attr_copied")

        def unordered(eng):
            reg = eng.alloc_register("unordered")
            eng.load([reg], flag[:])
            return reg

        with nc.Block() as block:
            @block.sync
            def _(sp):
                f = unordered(sp)
                with sp.If_eq(f, 0):
                    for name, to in tables:
                        sp.dma_start(to.rearrange("(p t) -> p t", p=P), ins[name].rearrange("(p t) -> p t", p=P)
                                     ).then_inc(cols_out, 16)
                    sp.dma_start(dram.attr.rearrange("a (p t) -> (a p) t", p=2 * P),
                                 ins["attr"].rearrange("a (p t) -> (a p) t", p=2 * P)).then_inc(dram.attr_copied, 16)
                    sp.wait_ge(cols_out, 64)
                with sp.If_ne(f, 0):
                    with sp.Fori(0, NT) as i:
                        hold(sp, hot1, i + 1)
                        sp.dma_start(key[:], ins["dst"][ds(i * P, P)].unsqueeze(1)).then_inc(key_in, 16)
                    sp.wait_ge(base, 1)
                    with sp.Fori(0, NT) as i:
                        hold(sp, made, i + 1)
                        sp.dma_start(key[:], ins["dst"][ds(i * P, P)].unsqueeze(1)).then_inc(rec_in, 16)
                        for j, (name, _) in enumerate(tables):
                            sp.dma_start(rec[:, j:j + 1].bitcast(ins[name].dtype), ins[name][ds(i * P, P)].unsqueeze(1)
                                         ).then_inc(rec_in, 16)
                        sp.dma_start(acol[:], ins["attr"][:, ds(i * P, P)]).then_inc(rec_in, 16)
                    sp.wait_ge(made, NT + 1)
                    for j, (name, to) in enumerate(tables):
                        sp.dma_start(to.rearrange("(p t) -> p t", p=P).unsqueeze(2),
                                     dram.rec[:, j:j + 1].rearrange("(p t) c -> p t c", p=P).bitcast(to.dtype),
                                     allow_slow_non_contiguous=True).then_inc(cols_out, 16)
                    with sp.Fori(0, NT) as i:
                        hold(sp, back_out, 16 * (i + 1))
                        sp.dma_start(arow[:], dram.arow[ds(i * P, P), :]).then_inc(back_in, 16)
                        hold(sp, back_ready, i + 1)
                        sp.dma_start(dram.attr[:, ds(i * P, P)], acol[:]).then_inc(back_out, 16)
                    sp.wait_ge(back_out, 16 * (NT + 1))
                    sp.wait_ge(cols_out, 64)
                    sp.sem_inc(dram.attr_copied, 16)

            @block.gpsimd
            def _(pool):
                f = unordered(pool)
                with pool.If_ne(f, 0):
                    nc.gpsimd.memset(lower[:], 1.0).then_inc(v2, 1)
                    pool.wait_ge(v2, 1)
                    nc.gpsimd.affine_select(out=lower[:], in_=lower[:], compare_op=ALU.is_ge, fill=0.0, base=-1,
                                            pattern=[[-1, P]], channel_multiplier=1).then_inc(made, 1)
                    with pool.Fori(0, NT) as i:
                        hold(pool, pos_ready, i + 1)
                        hold(pool, copied, 2 * i + 2)
                        hold(pool, rec_in, 96 * (i + 1))
                        pool.indirect_dma_start(out=dram.rec, out_offset=bass.IndirectOffsetOnAxis(ap=pos[:], axis=0),
                                                in_=rec[:], in_offset=None).then_inc(placed, 16)
                        pool.indirect_dma_start(out=dram.arow, out_offset=bass.IndirectOffsetOnAxis(ap=pos[:], axis=0),
                                                in_=arow[:], in_offset=None).then_inc(placed, 16)
                        pool.wait_ge(placed, 32 * (i + 1))
                        pool.sem_inc(made, 1)

            @block.tensor
            def _(pe):
                f = unordered(pe)
                with pe.If_ne(f, 0):
                    with pe.Fori(0, NT) as i:
                        pe.wait_ge(hot1, i + 2)
                        pe.matmul(ps_c[:, 0:HI], lo[:], hi[:], start=True, stop=True).then_inc(count1, 1)
                    pe.wait_ge(pref, 1)
                    pe.matmul(ps_r[:, 0:HI], keep.before[:], table[:], start=True, stop=True)
                    pe.matmul(ps_t[:, 0:HI], ones[:], table[:], start=True, stop=True).then_inc(pref, 1)
                    with pe.Fori(0, NT) as i:
                        pe.wait_ge(hot2, i + 2)
                        pe.wait_ge(rec_in, 96 * (i + 1))
                        pe.transpose(ps_t[:, 0:P], lo[:], keep.ident[:])
                        pe.transpose(ps_t[0:HI, P:2 * P], hi[:], keep.ident[:])
                        pe.transpose(ps_u[:, 0:KA], acol[:], keep.ident[0:KA, 0:KA]).then_inc(turned, 1)
                        pe.wait_ge(copied, 2 * i + 2)
                        pe.matmul(ps_r[:, 0:HI], loT[:], table[:], start=True, stop=True)
                        pe.matmul(ps_lo[:, 0:P], loT[:], loT[:], start=True, stop=True)
                        pe.matmul(ps_hi[:, 0:P], hiT[:], hiT[:], start=True, stop=True)
                        pe.matmul(ps_c[:, 0:HI], lo[:], hi[:], start=True, stop=True).then_inc(counted, 1)
                    with pe.Fori(0, NT) as i:
                        pe.wait_ge(back_in, 16 * (i + 1))
                        pe.transpose(ps_u[0:KA, 0:P], arow[:], keep.ident[:]).then_inc(back_turned, 1)

            @block.scalar
            def _(act):
                f = unordered(act)
                with act.If_ne(f, 0):
                    with act.Fori(0, NT) as i:
                        act.wait_ge(turned, i + 1)
                        nc.scalar.copy(loT[:], ps_t[:, 0:P])
                        nc.scalar.copy(hiT[:], ps_t[0:HI, P:2 * P]).then_inc(copied, 1)
                        nc.scalar.copy(arow[:], ps_u[:, 0:KA]).then_inc(copied, 1)
                    act.sem_inc(back_out, 16)
                    with act.Fori(0, NT) as i:
                        act.wait_ge(back_turned, i + 1)
                        nc.scalar.copy(acol[:], ps_u[0:KA, 0:P]).then_inc(back_ready, 1)

            @block.vector
            def _(dve):
                f = unordered(dve)
                with dve.If_ne(f, 0):
                    def one_hots(ch):
                        ch.link(nc.vector.tensor_copy(kf[:], key[:]))
                        ch.link(nc.vector.tensor_scalar(hii[:], key[:], 7, None, ALU.arith_shift_right))
                        ch.link(nc.vector.tensor_copy(hif[:], hii[:]))
                        ch.link(nc.vector.scalar_tensor_tensor(out=lof[:], in0=hif[:], scalar=float(-P), in1=kf[:],
                                                               op0=ALU.mult, op1=ALU.add))
                        ch.link(nc.vector.tensor_scalar(lo[:], keep.iota_row[:], lof[:, 0:1], None, ALU.is_equal))
                        ch.link(nc.vector.tensor_scalar(hi[:], keep.iota_row[:, 0:HI], hif[:, 0:1], None, ALU.is_equal))

                    nc.vector.memset(zero[:], 0.0)
                    nc.vector.memset(ones[:], 1.0)
                    nc.vector.memset(table[:], 0.0).then_inc(hot1, 1)
                    ch = Chain(dve, v1, 7)
                    with dve.Fori(0, NT) as i:
                        ch.start(i)
                        hold(dve, key_in, 16 * (i + 1))
                        one_hots(ch)
                        dve.sem_inc(hot1, 1)
                        dve.wait_ge(count1, i + 1)
                        ch.link(nc.vector.tensor_tensor(table[:], table[:], ps_c[:, 0:HI], ALU.add))
                        ch.end()
                    dve.sem_inc(pref, 1)
                    dve.wait_ge(pref, 2)
                    nc.vector.tensor_copy(tot[:], ps_t[:, 0:HI]).then_inc(pref, 1)
                    dve.wait_ge(pref, 3)
                    nc.vector.tensor_tensor_scan(incl[:], tot[:], zero[:], 0.0, ALU.add, ALU.add).then_inc(pref, 1)
                    dve.wait_ge(pref, 4)
                    nc.vector.tensor_tensor(incl[:], incl[:], tot[:], ALU.subtract).then_inc(pref, 1)
                    dve.wait_ge(pref, 5)
                    nc.vector.tensor_tensor(table[:], incl[:], ps_r[:, 0:HI], ALU.add).then_inc(base, 1)
                    dve.wait_ge(base, 1)
                    dve.sem_inc(hot2, 1)
                    ch = Chain(dve, v3, 14)
                    with dve.Fori(0, NT) as i:
                        ch.start(i)
                        hold(dve, rec_in, 96 * (i + 1))
                        one_hots(ch)
                        dve.sem_inc(hot2, 1)
                        dve.wait_ge(counted, i + 1)
                        ch.link(nc.vector.tensor_tensor(sel[:], hi[:], ps_r[:, 0:HI], ALU.mult))
                        ch.link(nc.vector.tensor_reduce(bef[:], sel[:], AX, ALU.add))
                        ch.link(nc.vector.tensor_tensor(eq[:], lower[:], ps_lo[:, 0:P], ALU.mult))
                        ch.link(nc.vector.tensor_tensor(eq[:], eq[:], ps_hi[:, 0:P], ALU.mult))
                        ch.link(nc.vector.tensor_reduce(rank[:], eq[:], AX, ALU.add))
                        ch.link(nc.vector.tensor_tensor(bef[:], bef[:], rank[:], ALU.add))
                        ch.link(nc.vector.tensor_tensor(table[:], table[:], ps_c[:, 0:HI], ALU.add))
                        dve.wait_ge(made, i + 1)
                        ch.link(nc.vector.tensor_copy(pos[:], bef[:]))
                        dve.sem_inc(pos_ready, 1)
                        ch.end()


class Dram:
    pass


def build(nc, ins, out):
    with ExitStack() as ctx:
        dram = Dram()

        def scratch(name, shape, dt=F32):
            return nc.dram_tensor(f"scratch_{name}", shape, dt, kind="Internal").ap()

        dram.rec, dram.arow = scratch("rec", [EP, 4], I32), scratch("arow", [EP, KA])
        dram.src, dram.dst = scratch("src", [EP], I32), scratch("dst", [EP], I32)
        dram.et, dram.ew, dram.attr = scratch("et", [EP], I32), scratch("ew", [EP]), scratch("attr", [KA, EP])
        dram.plan, dram.tk = scratch("plan", [2, NT]), scratch("tk", [2, NSP], I32)
        dram.dlrow, dram.srcrow = scratch("dlrow", [NSP, P], BF16), scratch("srcrow", [NSP, P])
        dram.dlflat, dram.dstflat = scratch("dlflat", [NSP, P]), scratch("dstflat", [NSP * P + P])
        dram.hT, dram.kv = scratch("hT", [P, NP]), scratch("kv", [NP, 2 * D])
        dram.x1, dram.hw = scratch("x1", [NP, D]), scratch("hw", [NP * RT, D])
        dram.x2, dram.h2 = scratch("x2", [NP, D]), scratch("h2", [NP, D])
        dram.side = [scratch(f"side{u}", [NP + P, D]) for u in range(GS)]
        dram.h3T, dram.hx, dram.skv = scratch("h3T", [P, NP]), scratch("hx", [NP, D]), scratch("skv", [NP, 2 * D])
        dram.lg, dram.v = scratch("lg", [NS * P, LW]), scratch("v", [NS * P, D])

        keep = Stage(nc, ctx, "keep")
        keep.dl, keep.src = keep.sb("dl", [P, NSP]), keep.sb("src", [P, NSP], I32)
        keep.window, keep.dis = keep.sb("window", [P, NSP], I32), keep.sb("dis", [P, NW + 1])
        keep.unordered = keep.sb("unordered", [1, 1], I32)
        constants(nc, keep)
        with ExitStack() as c:
            cols = Stage(nc, c, "cols")
            keep.et, keep.ew = cols.sb("et", [P, NSP]), cols.sb("ew", [P, NSP])
            keep.srcf, keep.srct = cols.sb("srcf", [P, NSP]), cols.sb("srct", [P, NSP], I32)
            order_edges(nc, keep, dram, ins)
            clear_tables(nc, cols, dram)
            plan_slots(nc, keep, dram, dram.src, dram.dst, dram.et, dram.ew)
            nodes = cols.sb("nodes", [P, (NW + 1) * AC0])
            with ExitStack() as c0:
                q = Stage(nc, c0, "l0").sb("q", [P, (NW + 1) * D])
                project_qkv(nc, keep, dram, ins["x"], ins["L0_gnn_Wqkv"], q)
                edges_0(nc, keep, dram, q, nodes)
            mix_0(nc, keep, dram, ins, nodes)
            edges_1(nc, keep, dram, nodes)
            with ExitStack() as c2:
                hp = Stage(nc, c2, "l2").sb("hp", [P, (NW + 1) * D])
                mix_1(nc, keep, dram, nodes, hp)
                edges_2(nc, keep, dram, hp)
        with ExitStack() as c:
            kvq = Stage(nc, c, "l3").sb("kvq", [P, (NW + 1) * KQ])
            mix_2(nc, keep, dram, ins, kvq)
            edges_3(nc, keep, dram, ins, kvq)
        softmax_3(nc, keep, dram, ins)
        with ExitStack() as c:
            nodes = Stage(nc, c, "l3s").sb("nodes", [P, (NW + 1) * AC3])
            edges_3_sums(nc, keep, dram, nodes)
            mix_3(nc, keep, dram, ins, nodes, out)


def kernel(**inputs):
    import numpy as np
    import concourse.bacc as _bacc
    from concourse.bass_utils import run_bass_kernel_spmd as _run

    a = {k: np.asarray(v) for k, v in inputs.items()}
    lay = {}
    lay["x"] = np.pad(a["x"], ((0, NP - N), (0, 0)))
    lay["src"] = np.pad(a["src"], (0, EP - E))
    lay["dst"] = np.pad(a["dst"], (0, EP - E), constant_values=NP - 1)
    lay["edge_type_16"] = np.pad(a["edge_type_16"], (0, EP - E))
    lay["edge_weight"] = np.pad(a["edge_weight"], (0, EP - E))
    lay["L0_gnn_Wqkv"] = np.concatenate([a["L0_gnn_Wq"].T, a["L0_gnn_Wk"].T, a["L0_gnn_Wv"].T], axis=1)
    lay["L0_gnn_Wo"] = a["L0_gnn_Wo"].T
    lay["L0_gnn_W1"] = a["L0_gnn_W1"].T
    lay["L0_gnn_W2"] = a["L0_gnn_W2"].T
    lay["L0_cols"] = np.stack([a["L0_gnn_bo"], a["L0_gnn_b1"][:D], a["L0_gnn_b1"][D:], a["L0_gnn_bn1_w"], a["L0_gnn_bn1_b"],
                               a["L0_gnn_b2"], a["L0_gnn_bn2_w"], a["L0_gnn_bn2_b"]], axis=1)
    lay["L1_W"] = np.concatenate([a["L1_gnn_W_edge"], a["L1_gnn_W_node"]]).transpose(1, 0, 2).reshape(D, -1)
    lay["L1_b"] = np.concatenate([a["L1_gnn_b_edge"], a["L1_gnn_b_node"]])
    lay["node_type_8"] = np.pad(a["node_type_8"], (0, NP - N)).reshape(NW, P).T
    lay["L2_W"] = np.concatenate([a["L2_gnn_W0"].T, a["L2_gnn_W1"].T])
    hk, hv = a["L3_gnn_hk_w1"], a["L3_gnn_hv_w1"]
    dd, ss = slice(KA, KA + D), slice(KA + D, KA + 2 * D)
    lay["L3_Wp"] = np.concatenate([hk[dd], hv[dd], hk[ss], hv[ss], a["L3_gnn_hq_w1"]], axis=1)
    lay["L3_gnn_hq_w2"] = a["L3_gnn_hq_w2"]
    lay["L3_brow"] = np.concatenate([a["L3_gnn_hk_b1"], a["L3_gnn_hv_b1"], a["L3_gnn_hq_b1"], a["L3_gnn_hq_b2"]])
    lay["L3_qcols"] = np.stack([a["L3_gnn_hq_g"], a["L3_gnn_hq_beta"]], axis=1)
    lay["attr"] = np.pad(np.concatenate([a["edge_attr_4"], a["edge_attr_64"]], axis=1), ((0, EP - E), (0, 0))).T
    gate = np.pad(a["L3_gnn_ew_w"], ((AF, 0), (0, 0)))
    lay["L3_Wa"] = np.concatenate([hk[:KA], hv[:KA], gate], axis=1)
    lay["L3_W2"] = np.concatenate([a["L3_gnn_hk_w2"], a["L3_gnn_hv_w2"]])
    lay["L3_kvcols"] = np.stack([a["L3_gnn_hk_g"], a["L3_gnn_hk_beta"], a["L3_gnn_hv_g"], a["L3_gnn_hv_beta"]], axis=1)
    lay["L3_kvrow"] = np.concatenate([a["L3_gnn_hk_b2"], a["L3_gnn_hv_b2"]])
    lay["L3_gnn_ew_b"] = a["L3_gnn_ew_b"]
    lay["L3_gnn_no_w1"], lay["L3_gnn_no_w2"] = a["L3_gnn_no_w1"], a["L3_gnn_no_w2"]
    lay["L3_norow"] = np.concatenate([a["L3_gnn_no_b1"], a["L3_gnn_no_b2"]])
    lay["L3_nocols"] = np.stack([a["L3_gnn_no_g"], a["L3_gnn_no_beta"]], axis=1)
    nc = _bacc.Bacc("TRN2", target_bir_lowering=False, num_devices=1)
    arrays, ins = {}, {}
    for name, arr in lay.items():
        arr = np.ascontiguousarray(arr)
        arrays[f"in_{name}"] = arr
        ins[name] = nc.dram_tensor(f"in_{name}", arr.shape, mybir.dt.from_np(arr.dtype), kind="ExternalInput").ap()
    out = nc.dram_tensor("out_0", (NP, D), F32, kind="ExternalOutput").ap()
    build(nc, ins, out)
    r = _run(nc, [arrays], core_ids=[0])
    return r.results[0]["out_0"][:N]
```
